# Optimizing a Trainium2 kernel written in Bass

```python
import numpy as np
import jax
import jax.numpy as jnp

def _softmax(x, axis=-1):
    return jax.nn.softmax(x, axis=axis)

def _gelu(x):
    return jax.nn.gelu(x, approximate=True)

def _silu(x):
    return jax.nn.silu(x)

def _sigmoid(x):
    return jax.nn.sigmoid(x)

def _layernorm(x, axis=-1, eps=1e-05):
    m = jnp.mean(x, axis=axis, keepdims=True)
    v = jnp.var(x, axis=axis, keepdims=True)
    return (x - m) / jnp.sqrt(v + eps)

def _scatter_add(tgt, idx, src, axis=0):
    return tgt.at[idx].add(src)

def _segment_sum(src, seg, n):
    return jax.ops.segment_sum(src, seg, n)
kernel_name = 'mk_decoder_preln_d2_seqx_r8_c253e6'

def setup_inputs(seed: int=0):
    np.random.seed(seed)
    _w = jnp.asarray

    def _rec_inputs():
        import jax
        import jax.numpy as jnp
        _rk = jax.random.key(seed)
        x = 4.136e-05 + 0.9999 * jax.random.normal(jax.random.fold_in(_rk, 1), (8, 256, 128), jnp.float32)
        _lenS = 256 - jax.random.randint(jax.random.fold_in(_rk, 7), (8,), 0, max(1, 256 // 4) + 1, jnp.int32)
        _lenS2 = 256 - jax.random.randint(jax.random.fold_in(_rk, 8), (8,), 0, max(1, 256 // 4) + 1, jnp.int32)
        _ctx_1024P = jax.random.normal(jax.random.fold_in(_rk, 11), (8, 16, 128), jnp.float32)
        _ctx_1024c = jax.random.dirichlet(jax.random.fold_in(_rk, 511), 0.3 * jnp.ones((16,), jnp.float32), (8, 256))
        _ctx_1024t = jnp.einsum('bsk,bkd->bsd', _ctx_1024c, _ctx_1024P)
        _ctx_1024t = _ctx_1024t * jax.lax.rsqrt(jnp.mean(jnp.square(_ctx_1024t)) + 1e-12) * 0.953939
        ctx_1024 = 7.22013e-05 + 1.00017 * (_ctx_1024t + 0.3 * jax.random.normal(jax.random.fold_in(_rk, 611), (8, 256, 128), jnp.float32))
        return (x, ctx_1024)
    x, ctx_1024 = _rec_inputs()

    def _L0_attn_setup():
        import jax, jax.numpy as jnp
        import numpy as np
        DIM = 128
        HEADS = 16
        HIDDEN = 512
        EPS_ATTN = 1e-06
        EPS_LN = 1e-05

        def layer_norm(x, g, b):
            mu = jnp.mean(x, axis=-1, keepdims=True)
            var = jnp.var(x, axis=-1, keepdims=True)
            return (x - mu) * jax.lax.rsqrt(var + EPS_LN) * g + b
        key = jax.random.key(seed)
        ks = jax.random.split(key, 8)
        s = 0.02
        return {'x': jax.random.normal(ks[0], (4, 512, DIM), jnp.float32), 'norm1_g': jnp.ones((DIM,), jnp.float32), 'norm1_b': jnp.zeros((DIM,), jnp.float32), 'qkv_w': jax.random.normal(ks[1], (3 * DIM, DIM), jnp.float32) * s, 'proj_w': jax.random.normal(ks[2], (DIM, DIM), jnp.float32) * s, 'proj_b': jnp.zeros((DIM,), jnp.float32), 'norm2_g': jnp.ones((DIM,), jnp.float32), 'norm2_b': jnp.zeros((DIM,), jnp.float32), 'fc1_w': jax.random.normal(ks[3], (HIDDEN, DIM), jnp.float32) * s, 'fc1_b': jnp.zeros((HIDDEN,), jnp.float32), 'fc2_w': jax.random.normal(ks[4], (DIM, HIDDEN), jnp.float32) * s, 'fc2_b': jnp.zeros((DIM,), jnp.float32)}
    _L0_attn_all = _L0_attn_setup()
    _L0_attn_in = {k: v for k, v in _L0_attn_all.items() if k in ('norm1_g', 'norm1_b', 'qkv_w', 'proj_w', 'proj_b', 'norm2_g', 'norm2_b', 'fc1_w', 'fc1_b', 'fc2_w', 'fc2_b')}
    del _L0_attn_all

    def _L0_xattn_setup():
        import jax, jax.numpy as jnp
        import numpy as np
        B, L_Q, L_KV, D, H = (4, 256, 256, 128, 16)
        key = jax.random.key(seed)
        ks = jax.random.split(key, 11)
        s = 0.02
        return {'kv': jax.random.normal(ks[0], (B, L_KV, D), dtype=jnp.float32), 'q': jax.random.normal(ks[1], (B, L_Q, D), dtype=jnp.float32), 'Wq': jax.random.normal(ks[2], (D, D), dtype=jnp.float32) * s, 'bq': jnp.zeros((D,), dtype=jnp.float32), 'Wk': jax.random.normal(ks[3], (D, D), dtype=jnp.float32) * s, 'bk': jnp.zeros((D,), dtype=jnp.float32), 'Wv': jax.random.normal(ks[4], (D, D), dtype=jnp.float32) * s, 'bv': jnp.zeros((D,), dtype=jnp.float32), 'Wo': jax.random.normal(ks[5], (D, D), dtype=jnp.float32) * s, 'bo': jnp.zeros((D,), dtype=jnp.float32)}
    _L0_xattn_all = _L0_xattn_setup()
    _L0_xattn_in = {k: v for k, v in _L0_xattn_all.items() if k in ('Wq', 'bq', 'Wk', 'bk', 'Wv', 'bv', 'Wo', 'bo')}
    del _L0_xattn_all

    def _L0_ffn_setup():
        import math
        import jax, jax.numpy as jnp
        import numpy as np
        B, S, H, BOT, RD, N, K = (4, 256, 128, 128, 48, 512, 8)
        key = jax.random.key(seed)
        ks = jax.random.split(key, 12)
        hidden_states = jax.random.normal(ks[0], (B, S, H), jnp.float32)
        q_proj_w = jax.random.normal(ks[1], (BOT, H), jnp.float32) * (1.0 / math.sqrt(H))
        router_w = jax.random.normal(ks[2], (RD, BOT), jnp.float32) * (1.0 / math.sqrt(BOT))
        aux_keys = jax.random.normal(ks[3], (N, BOT), jnp.float32) * 0.01
        aux_values = jax.random.normal(ks[4], (N, H), jnp.float32) * 0.02
        reliability_mask = jax.random.uniform(ks[5], (N,), jnp.float32)
        unc_w1 = jax.random.normal(ks[6], (H // 4, H), jnp.float32) * (1.0 / math.sqrt(H))
        unc_b1 = jnp.zeros((H // 4,), jnp.float32)
        unc_w2 = jax.random.normal(ks[7], (1, H // 4), jnp.float32) * 0.02
        unc_b2 = jnp.zeros((1,), jnp.float32)
        gate_w1 = jnp.asarray(0.5, jnp.float32)
        gate_bias = jnp.asarray(-1.0, jnp.float32)
        return {'hidden_states': hidden_states, 'q_proj_w': q_proj_w, 'router_w': router_w, 'aux_keys': aux_keys, 'aux_values': aux_values, 'reliability_mask': reliability_mask, 'unc_w1': unc_w1, 'unc_b1': unc_b1, 'unc_w2': unc_w2, 'unc_b2': unc_b2, 'gate_w1': gate_w1, 'gate_bias': gate_bias}
    _L0_ffn_all = _L0_ffn_setup()
    _L0_ffn_in = {k: v for k, v in _L0_ffn_all.items() if k in ('q_proj_w', 'router_w', 'aux_keys', 'aux_values', 'reliability_mask', 'unc_w1', 'unc_b1', 'unc_w2', 'unc_b2', 'gate_w1', 'gate_bias')}
    del _L0_ffn_all

    def _L1_attn_setup():
        import jax, jax.numpy as jnp
        import numpy as np
        B, S, D, H, MLP = (2, 256, 128, 16, 512)
        DH = D // H
        EPS_LN = 1e-06
        KERNEL_EPS = 0.001

        def layer_norm(x, scale, bias):
            m = jnp.mean(x, axis=-1, keepdims=True)
            v = jnp.mean(jnp.square(x - m), axis=-1, keepdims=True)
            return (x - m) * jax.lax.rsqrt(v + EPS_LN) * scale + bias

        def performer_causal_attention(q, k, v):
            phi_q = jax.nn.relu(q) + KERNEL_EPS
            phi_k = jax.nn.relu(k) + KERNEL_EPS
            kv = jnp.cumsum(jnp.einsum('bshm,bshd->bshmd', phi_k, v), axis=1)
            num = jnp.einsum('bshm,bshmd->bshd', phi_q, kv)
            den = jnp.einsum('bshm,bshm->bsh', phi_q, jnp.cumsum(phi_k, axis=1))
            return num / den[..., None]
        key = jax.random.key(seed)
        ks = jax.random.split(key, 7)

        def w(k, shape, scale):
            return jax.random.normal(k, shape, jnp.float32) * scale
        s_in = 1.0 / np.sqrt(D)
        return {'inputs': jax.random.normal(ks[0], (B, S, D), jnp.float32), 'ln1_scale': jnp.ones((D,), jnp.float32), 'ln1_bias': jnp.zeros((D,), jnp.float32), 'wq': w(ks[1], (D, H, DH), s_in), 'wk': w(ks[2], (D, H, DH), s_in), 'wv': w(ks[3], (D, H, DH), s_in), 'wo': w(ks[4], (H, DH, D), s_in), 'ln2_scale': jnp.ones((D,), jnp.float32), 'ln2_bias': jnp.zeros((D,), jnp.float32), 'w1': w(ks[5], (D, MLP), s_in), 'b1': jnp.zeros((MLP,), jnp.float32), 'w2': w(ks[6], (MLP, D), 1.0 / np.sqrt(MLP)), 'b2': jnp.zeros((D,), jnp.float32)}
    _L1_attn_all = _L1_attn_setup()
    _L1_attn_in = {k: v for k, v in _L1_attn_all.items() if k in ('ln1_scale', 'ln1_bias', 'wq', 'wk', 'wv', 'wo', 'ln2_scale', 'ln2_bias', 'w1', 'b1', 'w2', 'b2')}
    del _L1_attn_all

    def _L1_xattn_setup():
        import jax, jax.numpy as jnp
        import numpy as np
        D_MODEL = 128
        N_HEADS = 16
        D_K = D_MODEL // N_HEADS
        key = jax.random.key(seed)
        ks = jax.random.split(key, 12)
        B, S, D = (2, 256, D_MODEL)
        lim = 1.0 / np.sqrt(D)

        def lin(k):
            kw, kb = jax.random.split(k)
            W = jax.random.uniform(kw, (D, D), jnp.float32, -lim, lim)
            b = jax.random.uniform(kb, (D,), jnp.float32, -lim, lim)
            return (W, b)
        wq, bq = lin(ks[0])
        wk, bk = lin(ks[1])
        wv, bv = lin(ks[2])
        wo, bo = lin(ks[3])
        return {'query': jax.random.normal(ks[4], (B, S, D), jnp.float32), 'key': jax.random.normal(ks[5], (B, S, D), jnp.float32), 'value': jax.random.normal(ks[6], (B, S, D), jnp.float32), 'wq': wq, 'bq': bq, 'wk': wk, 'bk': bk, 'wv': wv, 'bv': bv, 'wo': wo, 'bo': bo, 'time_decay': jnp.float32(0.1)}
    _L1_xattn_all = _L1_xattn_setup()
    _L1_xattn_in = {k: v for k, v in _L1_xattn_all.items() if k in ('wq', 'bq', 'wk', 'bk', 'wv', 'bv', 'wo', 'bo', 'time_decay')}
    del _L1_xattn_all

    def _L1_ffn_setup():
        import jax, jax.numpy as jnp
        import numpy as np
        TOP_K = 8
        key = jax.random.key(seed)
        ks = jax.random.split(key, 6)
        B, S, D, F, E = (2, 128, 128, 64, 64)
        x = jax.random.normal(ks[0], (B, S, D), dtype=jnp.float32)
        centroids = jax.random.normal(ks[1], (E, D), dtype=jnp.float32) * 0.05
        expert_biases = jnp.zeros((E,), dtype=jnp.float32)
        Ws_up = jax.random.normal(ks[2], (D, F), dtype=jnp.float32) / np.sqrt(D)
        Ws_down = jax.random.normal(ks[3], (F, D), dtype=jnp.float32) / np.sqrt(F)
        W_up = jax.random.normal(ks[4], (E, D, F), dtype=jnp.float32) / np.sqrt(D)
        W_down = jax.random.normal(ks[5], (E, F, D), dtype=jnp.float32) / np.sqrt(F)
        return {'x': x, 'centroids': centroids, 'expert_biases': expert_biases, 'Ws_up': Ws_up, 'Ws_down': Ws_down, 'W_up': W_up, 'W_down': W_down}
    _L1_ffn_all = _L1_ffn_setup()
    _L1_ffn_in = {k: v for k, v in _L1_ffn_all.items() if k in ('centroids', 'expert_biases', 'Ws_up', 'Ws_down', 'W_up', 'W_down')}
    del _L1_ffn_all
    return {'x': x, 'ctx_1024': ctx_1024, 'L0_attn_norm1_g': _L0_attn_in['norm1_g'], 'L0_attn_norm1_b': _L0_attn_in['norm1_b'], 'L0_attn_qkv_w': _L0_attn_in['qkv_w'], 'L0_attn_proj_w': _L0_attn_in['proj_w'], 'L0_attn_proj_b': _L0_attn_in['proj_b'], 'L0_attn_norm2_g': _L0_attn_in['norm2_g'], 'L0_attn_norm2_b': _L0_attn_in['norm2_b'], 'L0_attn_fc1_w': _L0_attn_in['fc1_w'], 'L0_attn_fc1_b': _L0_attn_in['fc1_b'], 'L0_attn_fc2_w': _L0_attn_in['fc2_w'], 'L0_attn_fc2_b': _L0_attn_in['fc2_b'], 'L0_xattn_Wq': _L0_xattn_in['Wq'], 'L0_xattn_bq': _L0_xattn_in['bq'], 'L0_xattn_Wk': _L0_xattn_in['Wk'], 'L0_xattn_bk': _L0_xattn_in['bk'], 'L0_xattn_Wv': _L0_xattn_in['Wv'], 'L0_xattn_bv': _L0_xattn_in['bv'], 'L0_xattn_Wo': _L0_xattn_in['Wo'], 'L0_xattn_bo': _L0_xattn_in['bo'], 'L0_ffn_q_proj_w': _L0_ffn_in['q_proj_w'], 'L0_ffn_router_w': _L0_ffn_in['router_w'], 'L0_ffn_aux_keys': _L0_ffn_in['aux_keys'], 'L0_ffn_aux_values': _L0_ffn_in['aux_values'], 'L0_ffn_reliability_mask': _L0_ffn_in['reliability_mask'], 'L0_ffn_unc_w1': _L0_ffn_in['unc_w1'], 'L0_ffn_unc_b1': _L0_ffn_in['unc_b1'], 'L0_ffn_unc_w2': _L0_ffn_in['unc_w2'], 'L0_ffn_unc_b2': _L0_ffn_in['unc_b2'], 'L0_ffn_gate_w1': _L0_ffn_in['gate_w1'], 'L0_ffn_gate_bias': _L0_ffn_in['gate_bias'], 'L1_attn_ln1_scale': _L1_attn_in['ln1_scale'], 'L1_attn_ln1_bias': _L1_attn_in['ln1_bias'], 'L1_attn_wq': _L1_attn_in['wq'], 'L1_attn_wk': _L1_attn_in['wk'], 'L1_attn_wv': _L1_attn_in['wv'], 'L1_attn_wo': _L1_attn_in['wo'], 'L1_attn_ln2_scale': _L1_attn_in['ln2_scale'], 'L1_attn_ln2_bias': _L1_attn_in['ln2_bias'], 'L1_attn_w1': _L1_attn_in['w1'], 'L1_attn_b1': _L1_attn_in['b1'], 'L1_attn_w2': _L1_attn_in['w2'], 'L1_attn_b2': _L1_attn_in['b2'], 'L1_xattn_wq': _L1_xattn_in['wq'], 'L1_xattn_bq': _L1_xattn_in['bq'], 'L1_xattn_wk': _L1_xattn_in['wk'], 'L1_xattn_bk': _L1_xattn_in['bk'], 'L1_xattn_wv': _L1_xattn_in['wv'], 'L1_xattn_bv': _L1_xattn_in['bv'], 'L1_xattn_wo': _L1_xattn_in['wo'], 'L1_xattn_bo': _L1_xattn_in['bo'], 'L1_xattn_time_decay': _L1_xattn_in['time_decay'], 'L1_ffn_centroids': _L1_ffn_in['centroids'], 'L1_ffn_expert_biases': _L1_ffn_in['expert_biases'], 'L1_ffn_Ws_up': _L1_ffn_in['Ws_up'], 'L1_ffn_Ws_down': _L1_ffn_in['Ws_down'], 'L1_ffn_W_up': _L1_ffn_in['W_up'], 'L1_ffn_W_down': _L1_ffn_in['W_down']}

def reference(x, ctx_1024, L0_attn_norm1_g, L0_attn_norm1_b, L0_attn_qkv_w, L0_attn_proj_w, L0_attn_proj_b, L0_attn_norm2_g, L0_attn_norm2_b, L0_attn_fc1_w, L0_attn_fc1_b, L0_attn_fc2_w, L0_attn_fc2_b, L0_xattn_Wq, L0_xattn_bq, L0_xattn_Wk, L0_xattn_bk, L0_xattn_Wv, L0_xattn_bv, L0_xattn_Wo, L0_xattn_bo, L0_ffn_q_proj_w, L0_ffn_router_w, L0_ffn_aux_keys, L0_ffn_aux_values, L0_ffn_reliability_mask, L0_ffn_unc_w1, L0_ffn_unc_b1, L0_ffn_unc_w2, L0_ffn_unc_b2, L0_ffn_gate_w1, L0_ffn_gate_bias, L1_attn_ln1_scale, L1_attn_ln1_bias, L1_attn_wq, L1_attn_wk, L1_attn_wv, L1_attn_wo, L1_attn_ln2_scale, L1_attn_ln2_bias, L1_attn_w1, L1_attn_b1, L1_attn_w2, L1_attn_b2, L1_xattn_wq, L1_xattn_bq, L1_xattn_wk, L1_xattn_bk, L1_xattn_wv, L1_xattn_bv, L1_xattn_wo, L1_xattn_bo, L1_xattn_time_decay, L1_ffn_centroids, L1_ffn_expert_biases, L1_ffn_Ws_up, L1_ffn_Ws_down, L1_ffn_W_up, L1_ffn_W_down):
    import jax
    import jax.numpy as jnp

    def _L0_attn_ref(x, norm1_g, norm1_b, qkv_w, proj_w, proj_b, norm2_g, norm2_b, fc1_w, fc1_b, fc2_w, fc2_b):
        import jax, jax.numpy as jnp
        import numpy as np
        DIM = 128
        HEADS = 16
        HIDDEN = 512
        EPS_ATTN = 1e-06
        EPS_LN = 1e-05

        def layer_norm(x, g, b):
            mu = jnp.mean(x, axis=-1, keepdims=True)
            var = jnp.var(x, axis=-1, keepdims=True)
            return (x - mu) * jax.lax.rsqrt(var + EPS_LN) * g + b
        B, N, C = x.shape
        H = HEADS
        d = C // H
        h = layer_norm(x, norm1_g, norm1_b)
        qkv = jnp.einsum('bnc,oc->bno', h, qkv_w)
        qkv = qkv.reshape(B, N, 3, H, d)
        q = jnp.transpose(qkv[:, :, 0], (0, 2, 1, 3))
        k = jnp.transpose(qkv[:, :, 1], (0, 2, 1, 3))
        v = jnp.transpose(qkv[:, :, 2], (0, 2, 1, 3))
        q = jax.nn.elu(q) + 1.0
        k = jax.nn.elu(k) + 1.0
        kv = jnp.einsum('bhnd,bhne->bhde', k, v)
        ksum = jnp.sum(k, axis=2)
        z = 1.0 / (jnp.einsum('bhnd,bhd->bhn', q, ksum) + EPS_ATTN)
        attn_out = jnp.einsum('bhnd,bhde->bhne', q, kv) * z[..., None]
        attn_out = jnp.transpose(attn_out, (0, 2, 1, 3)).reshape(B, N, C)
        attn_out = jnp.einsum('bnc,oc->bno', attn_out, proj_w) + proj_b
        x = x + attn_out
        h = layer_norm(x, norm2_g, norm2_b)
        h = jax.nn.gelu(jnp.einsum('bnc,hc->bnh', h, fc1_w) + fc1_b, approximate=False)
        h = jnp.einsum('bnh,ch->bnc', h, fc2_w) + fc2_b
        return x + h

    def _L0_xattn_ref(kv, q, Wq, bq, Wk, bk, Wv, bv, Wo, bo):
        import jax, jax.numpy as jnp
        import numpy as np
        B, L_Q, L_KV, D, H = (4, 256, 256, 128, 16)
        Bb, Lkv, Dm = kv.shape
        Lq = q.shape[1]
        hd = Dm // H
        scale = hd ** (-0.5)
        qh = (q @ Wq.T + bq).reshape(Bb, Lq, H, hd).transpose(0, 2, 1, 3)
        kh = (kv @ Wk.T + bk).reshape(Bb, Lkv, H, hd).transpose(0, 2, 1, 3)
        vh = (kv @ Wv.T + bv).reshape(Bb, Lkv, H, hd).transpose(0, 2, 1, 3)
        scores = jnp.einsum('bhqd,bhkd->bhqk', qh, kh) * scale
        mask = jnp.arange(Lkv)[None, :] <= jnp.arange(Lq)[:, None]
        scores = jnp.where(mask[None, None], scores, -jnp.inf)
        attn = jax.nn.softmax(scores, axis=-1)
        out = jnp.einsum('bhqk,bhkd->bhqd', attn, vh)
        out = out.transpose(0, 2, 1, 3).reshape(Bb, Lq, Dm)
        return out @ Wo.T + bo

    def _L0_ffn_ref(hidden_states, q_proj_w, router_w, aux_keys, aux_values, reliability_mask, unc_w1, unc_b1, unc_w2, unc_b2, gate_w1, gate_bias):
        import math
        import jax, jax.numpy as jnp
        import numpy as np
        B, S, H, BOT, RD, N, K = (4, 256, 128, 128, 48, 512, 8)
        query = jnp.einsum('bsh,dh->bsd', hidden_states, q_proj_w)
        rq = jnp.einsum('bsd,rd->bsr', query, router_w)
        rk = jnp.einsum('nd,rd->nr', aux_keys, router_w)
        scores = jnp.einsum('bsr,nr->bsn', rq, rk) / math.sqrt(RD)
        scores = scores + reliability_mask[None, None, :]
        top_scores, top_idx = jax.lax.top_k(scores, K)
        mean = hidden_states.mean(axis=-1, keepdims=True)
        variance = ((hidden_states - mean) ** 2).mean(axis=-1)
        log_var = jnp.log1p(variance)
        normalized_var = log_var / (log_var.mean() + 1e-06)
        h1 = jax.nn.gelu(jnp.einsum('bsh,fh->bsf', hidden_states, unc_w1) + unc_b1, approximate=False)
        learned = (jnp.einsum('bsf,of->bso', h1, unc_w2) + unc_b2)[..., 0]
        uncertainty = jnp.clip(normalized_var * 0.5 + jax.nn.sigmoid(learned) * 2.5, 0.0, 5.0)
        gate = jax.nn.sigmoid(gate_w1 * uncertainty + gate_bias)
        w = jax.nn.softmax(top_scores, axis=-1)
        v = aux_values[top_idx]
        agg = jnp.einsum('bsk,bskh->bsh', w, v)
        out = hidden_states + gate[..., None] * agg
        return out

    def _L1_attn_ref(inputs, ln1_scale, ln1_bias, wq, wk, wv, wo, ln2_scale, ln2_bias, w1, b1, w2, b2):
        import jax, jax.numpy as jnp
        import numpy as np
        B, S, D, H, MLP = (2, 256, 128, 16, 512)
        DH = D // H
        EPS_LN = 1e-06
        KERNEL_EPS = 0.001

        def layer_norm(x, scale, bias):
            m = jnp.mean(x, axis=-1, keepdims=True)
            v = jnp.mean(jnp.square(x - m), axis=-1, keepdims=True)
            return (x - m) * jax.lax.rsqrt(v + EPS_LN) * scale + bias

        def performer_causal_attention(q, k, v):
            phi_q = jax.nn.relu(q) + KERNEL_EPS
            phi_k = jax.nn.relu(k) + KERNEL_EPS
            kv = jnp.cumsum(jnp.einsum('bshm,bshd->bshmd', phi_k, v), axis=1)
            num = jnp.einsum('bshm,bshmd->bshd', phi_q, kv)
            den = jnp.einsum('bshm,bshm->bsh', phi_q, jnp.cumsum(phi_k, axis=1))
            return num / den[..., None]
        x = layer_norm(inputs, ln1_scale, ln1_bias)
        q = jnp.einsum('bsd,dhm->bshm', x, wq)
        k = jnp.einsum('bsd,dhm->bshm', x, wk)
        v = jnp.einsum('bsd,dhm->bshm', x, wv)
        attn = performer_causal_attention(q, k, v)
        attn_out = jnp.einsum('bshm,hmd->bsd', attn, wo)
        x = attn_out + inputs
        y = layer_norm(x, ln2_scale, ln2_bias)
        y = jax.nn.gelu(y @ w1 + b1) @ w2 + b2
        return x + y

    def _L1_xattn_ref(query, key, value, wq, bq, wk, bk, wv, bv, wo, bo, time_decay):
        import jax, jax.numpy as jnp
        import numpy as np
        D_MODEL = 128
        N_HEADS = 16
        D_K = D_MODEL // N_HEADS
        B, S, D = query.shape
        H, Dk = (N_HEADS, D_K)

        def proj(x, W, b):
            y = jnp.einsum('bsd,ed->bse', x, W) + b
            return y.reshape(B, S, H, Dk).transpose(0, 2, 1, 3)
        Q = proj(query, wq, bq)
        K = proj(key, wk, bk)
        V = proj(value, wv, bv)
        scores = jnp.einsum('bhqd,bhkd->bhqk', Q, K) / jnp.sqrt(jnp.float32(Dk))
        pos = jnp.arange(S, dtype=jnp.float32)
        decay = -time_decay * jnp.abs(pos[:, None] - pos[None, :])
        scores = scores + decay[None, None, :, :]
        attn = jax.nn.softmax(scores, axis=-1)
        ctx = jnp.einsum('bhqk,bhkd->bhqd', attn, V)
        ctx = ctx.transpose(0, 2, 1, 3).reshape(B, S, D)
        out = jnp.einsum('bsd,ed->bse', ctx, wo) + bo
        return out

    def _L1_ffn_ref(x, centroids, expert_biases, Ws_up, Ws_down, W_up, W_down):
        import jax, jax.numpy as jnp
        import numpy as np
        TOP_K = 8
        B, S, D = x.shape
        E = centroids.shape[0]
        T = B * S
        xf = x.reshape(T, D)
        shared = jax.nn.silu(xf @ Ws_up) @ Ws_down
        aff = xf @ centroids.T
        biased = aff + expert_biases
        _, idx = jax.lax.top_k(biased, TOP_K)
        sel = jnp.take_along_axis(aff, idx, axis=1)
        w = jax.nn.sigmoid(sel)
        w = w / (jnp.sum(w, axis=-1, keepdims=True) + 1e-08)
        cw = jnp.zeros((T, E), dtype=x.dtype).at[jnp.arange(T)[:, None], idx].add(w)
        h = jax.nn.silu(jnp.einsum('td,edf->etf', xf, W_up))
        y = jnp.einsum('etf,efd->etd', h, W_down)
        routed = jnp.einsum('etd,te->td', y, cw)
        return (shared + routed).reshape(B, S, D)
    x = x + _L0_attn_ref(_layernorm(x, axis=-1), L0_attn_norm1_g, L0_attn_norm1_b, L0_attn_qkv_w, L0_attn_proj_w, L0_attn_proj_b, L0_attn_norm2_g, L0_attn_norm2_b, L0_attn_fc1_w, L0_attn_fc1_b, L0_attn_fc2_w, L0_attn_fc2_b)
    x = x + _L0_xattn_ref(ctx_1024, _layernorm(x, axis=-1), L0_xattn_Wq, L0_xattn_bq, L0_xattn_Wk, L0_xattn_bk, L0_xattn_Wv, L0_xattn_bv, L0_xattn_Wo, L0_xattn_bo)
    x = x + _L0_ffn_ref(_layernorm(x, axis=-1), L0_ffn_q_proj_w, L0_ffn_router_w, L0_ffn_aux_keys, L0_ffn_aux_values, L0_ffn_reliability_mask, L0_ffn_unc_w1, L0_ffn_unc_b1, L0_ffn_unc_w2, L0_ffn_unc_b2, L0_ffn_gate_w1, L0_ffn_gate_bias)
    x = x + _L1_attn_ref(_layernorm(x, axis=-1), L1_attn_ln1_scale, L1_attn_ln1_bias, L1_attn_wq, L1_attn_wk, L1_attn_wv, L1_attn_wo, L1_attn_ln2_scale, L1_attn_ln2_bias, L1_attn_w1, L1_attn_b1, L1_attn_w2, L1_attn_b2)
    x = x + _L1_xattn_ref(_layernorm(x, axis=-1), ctx_1024, ctx_1024, L1_xattn_wq, L1_xattn_bq, L1_xattn_wk, L1_xattn_bk, L1_xattn_wv, L1_xattn_bv, L1_xattn_wo, L1_xattn_bo, L1_xattn_time_decay)
    x = x + _L1_ffn_ref(_layernorm(x, axis=-1), L1_ffn_centroids, L1_ffn_expert_biases, L1_ffn_Ws_up, L1_ffn_Ws_down, L1_ffn_W_up, L1_ffn_W_down)
    return x

_drawn_inputs = setup_inputs


def setup_inputs(seed=0):
    import zlib

    import numpy as np

    out = dict(_drawn_inputs(seed))
    spreads = {'L0_attn_norm1_g': (1.0, 0.6),
     'L0_attn_norm1_b': (0.0, 0.8),
     'L0_attn_proj_b': (0.0, 0.1),
     'L0_attn_norm2_g': (1.0, 0.6),
     'L0_attn_norm2_b': (0.0, 2.0),
     'L0_attn_fc1_b': (0.0, 0.57),
     'L0_attn_fc2_b': (0.0, 0.27),
     'L0_xattn_bq': (0.0, 0.8),
     'L0_xattn_bk': (0.0, 2.0),
     'L0_xattn_bv': (0.0, 0.616),
     'L0_xattn_bo': (0.0, 0.279),
     'L0_ffn_unc_b1': (0.0, 2.0),
     'L1_attn_ln1_scale': (1.0, 0.6),
     'L1_attn_ln1_bias': (0.0, 0.383),
     'L1_attn_ln2_scale': (1.0, 0.6),
     'L1_attn_ln2_bias': (0.0, 0.423),
     'L1_attn_b1': (0.0, 0.399),
     'L1_attn_b2': (0.0, 0.309),
     'L1_ffn_expert_biases': (0.0, 0.963)}
    factors = {'L0_attn_qkv_w': 8.0,
     'L0_attn_proj_w': 8.0,
     'L0_xattn_Wq': 8.0,
     'L0_xattn_Wk': 8.0,
     'L0_xattn_Wv': 3.642,
     'L0_xattn_Wo': 2.842,
     'L0_ffn_q_proj_w': 32.906,
     'L0_ffn_router_w': 33.286,
     'L0_ffn_aux_keys': 33.173,
     'L0_ffn_aux_values': 33.329,
     'L0_ffn_unc_w1': 64.0,
     'L0_ffn_unc_w2': 64.0,
     'L1_xattn_wq': 7.814,
     'L1_xattn_bq': 31.957,
     'L1_xattn_wk': 7.648,
     'L1_xattn_bk': 64.0,
     'L1_xattn_bv': 7.066,
     'L1_xattn_bo': 4.03,
     'L1_attn_wq': 2.69}
    for name, (base, spread) in spreads.items():
        noise = np.random.default_rng([zlib.crc32(name.encode()), seed]).standard_normal(out[name].shape)
        drawn = base * np.exp(spread * noise) if base else spread * noise
        out[name] = jnp.asarray(drawn.astype(out[name].dtype))
    for name, factor in factors.items():
        out[name] = (out[name] * factor).astype(out[name].dtype)
    return out
```

```python
from contextlib import ExitStack

import numpy as np
import concourse.bass as bass
from concourse import mybir

ALU = mybir.AluOpType
ACT = mybir.ActivationFunctionType
AX_X = mybir.AxisListType.X
F32 = mybir.dt.float32
BF16 = mybir.dt.bfloat16
I32 = mybir.dt.int32

P = 128
D = 128
B, S = 8, 256
T = B * S
NT = T // P
H, DH = 16, 8
GT = 4
G = GT * P
NG = NT // GT
HID = 512
HC = HID // P
NMEM, RD = 512, 48
UNC = D // 4
E, F = 64, 64
EP = E // 2
BIG = 1.0e30
LOW = -3.0e38
MINUS_ONES = float(np.array([0xBF80BF80], np.uint32).view(np.float32)[0])
SCRATCH = 31900

_W = [
    ("qkv0", 3 * D), ("proj0", D), ("fc1_0", HID), ("fc2_0", HID),
    ("xq0", D), ("xk0", D), ("xv0", D), ("xo0", D),
    ("qproj", D), ("router", RD), ("keys", NMEM), ("values", HC * D), ("unc1", UNC), ("unc2", 1),
    ("qkv1", 3 * D), ("wo1", D), ("fc1_1", HID), ("fc2_1", HID),
    ("xq1", D), ("xk1", D), ("xv1", D), ("xo1", D),
    ("cent", E), ("sup", F), ("sdown", D),
]
_C = [
    ("g1_0", 1), ("b1_0", 1), ("g2_0", 1), ("b2_0", 1), ("fcb_0", HC),
    ("bq0", 1), ("bk0", 1), ("bq1", 1), ("bk1", 1), ("uncb1", 1),
    ("g1_1", 1), ("b1_1", 1), ("g2_1", 1), ("b2_1", 1), ("fcb_1", HC),
]
_R = [
    ("projb", D), ("fc2b_0", D), ("bv0", D), ("bo0", D), ("fc2b_1", D), ("bv1", D), ("bo1", D),
    ("mask", NMEM), ("eb", E), ("uncb2", 1), ("gw1", 1), ("gbias", 1), ("decay", 1),
]


def _spans(items):
    at, out = 0, {}
    for name, n in items:
        out[name] = (at, at + n)
        at += n
    return out, at


W_AT, NW = _spans(_W)
C_AT, NC_ = _spans(_C)
R_AT, NR = _spans(_R)
W_LOADS = [("qkv0", "xq0"), ("xq0", "qproj"), ("qproj", "qkv1"), ("qkv1", "xq1"), ("xq1", None)]
SCALE = float(np.float32(DH) ** np.float32(-0.5))


def build(nc, x, ctxT, wts, cols, rows, positions, wup, wdown, scratch, out):
    with ExitStack() as ctx:
        def sb(name, shape, dt=F32):
            return ctx.enter_context(nc.sbuf_tensor(name, shape, dt))

        sems, given = {}, []

        def sem(name):
            if name not in sems:
                given.append(name)
                sems[name] = nc.alloc_semaphore(name if given.count(name) == 1 else f"{name}_{given.count(name)}")
            return sems[name]

        def phase(run, *args):
            run(*args)
            own = [n for n in sems if not n.endswith(("_loaded", "_stored", "_stats"))]
            nc.clear_and_free_semaphores([sems.pop(n) for n in own])
            nc.all_engine_barrier()

        X = sb("X", [P, NT * D])
        W = sb("W", [P, NW])
        CO = sb("CO", [P, NC_])
        RO = sb("RO", [P, NR])
        VA = sb("VA", [P, NT * 512])
        XX = VA[:, 0:NT * D]
        ident = sb("ident", [P, P])
        identb = sb("identb", [P, P], BF16)
        ST = sb("ST", [P, NT * 6])
        MV = sb("MV", [P, NT, 2])
        SD = sb("SD", [P, NT])
        RS = sb("RS", [P, NT])
        SD2 = sb("SD2", [P, NT])
        RS2 = sb("RS2", [P, NT])
        AR = sb("AR", [P, SCRATCH])
        PS = ctx.enter_context(nc.psum_tensor("PS", [P, 8, 512], F32))

        at = [0]

        def cut(n, dt=F32):
            words = n if dt == F32 else (n + 1) // 2
            v = AR[:, at[0]:at[0] + words]
            at[0] += words
            assert at[0] <= SCRATCH
            return v if dt == F32 else v.bitcast(dt)

        def w(name, a=0, n=None):
            s, e = W_AT[name]
            return W[:, s + a:(e if n is None else s + a + n)]

        def col(name, k=0):
            return CO[:, C_AT[name][0] + k:C_AT[name][0] + k + 1]

        def row(name, k=0):
            s, e = R_AT[name]
            return RO[:, s:e]

        def tiles(ap, n=GT):
            return ap.rearrange("p (t d) -> p t d", t=n)

        def over(ap, n, axis=1):
            v = ap.unsqueeze(axis)
            shape = list(v.shape)
            shape[axis] = n
            return v.broadcast_to(shape)

        TRI = sb("TRI", [P, P])
        ONES = sb("ONES", [P, P])
        HM = sb("HM", [P, H])
        BM = sb("BM", [P, P])

        CONST = 5

        def set_up():
            with nc.Block() as block:
                @block.sync
                def _(sp):
                    for g in range(NG):
                        sp.dma_start(X[:, g * G:(g + 1) * G].rearrange("p (t d) -> p t d", t=GT),
                                     x[g * G:(g + 1) * G, :].rearrange("(t p) d -> p t d", p=P))\
                            .then_inc(sem(f"x{g}_loaded"), 16)
                    sp.dma_start(CO[:, :], cols).then_inc(sem("cols_loaded"), 16)
                    sp.dma_start(RO[:, :], rows).then_inc(sem("rows_loaded"), 16)
                    for k, (a, b) in enumerate(W_LOADS):
                        lo, hi = W_AT[a][0], (W_AT[b][0] if b else NW)
                        sp.dma_start(W[:, lo:hi], wts[:, lo:hi]).then_inc(sem(f"w{k}_loaded"), 16)

                @block.gpsimd
                def _(pool):
                    c = sem("const_filled")
                    d = sem("const_ready")
                    pool.memset(ident[:, :], 0.0).then_inc(c, 1)
                    pool.memset(identb[:, :], 0.0).then_inc(c, 1)
                    pool.memset(TRI[:, :], 1.0).then_inc(c, 1)
                    pool.memset(ONES[:, :], 1.0).then_inc(d, 1)
                    pool.memset(HM[:, :], 1.0).then_inc(c, 1)
                    pool.wait_ge(c, 4)
                    for m in (ident, identb):
                        pool.affine_select(out=m[:, :], in_=m[:, :], compare_op=ALU.not_equal, fill=1.0, base=0,
                                           pattern=[[-1, P]], channel_multiplier=1).then_inc(d, 1)
                    pool.affine_select(out=TRI[:, :], in_=TRI[:, :], compare_op=ALU.is_ge, fill=0.0, base=0,
                                       pattern=[[1, P]], channel_multiplier=-1).then_inc(d, 1)
                    pool.affine_select(out=HM[:, :], in_=HM[:, :], compare_op=ALU.is_ge, fill=0.0, base=0,
                                       pattern=[[-DH, H]], channel_multiplier=1).then_inc(c, 1)
                    pool.wait_ge(c, 5)
                    pool.affine_select(out=HM[:, :], in_=HM[:, :], compare_op=ALU.is_ge, fill=0.0, base=DH - 1,
                                       pattern=[[DH, H]], channel_multiplier=-1).then_inc(c, 1)
                    pool.wait_ge(c, 6)
                    pool.tensor_copy(BM[:, :].rearrange("p (h e) -> p h e", h=H),
                                     over(HM[:, :], DH, 2)).then_inc(d, 1)

                @block.vector
                def _(dve):
                    for g in range(NG):
                        dve.wait_ge(sem(f"x{g}_loaded"), 16)
                        for t in range(g * GT, (g + 1) * GT):
                            dve.bn_stats(ST[:, 6 * t:6 * t + 6], X[:, t * D:(t + 1) * D]).then_inc(sem("stats0"), 1)


        def norm_stats_dve(dve, tag, stats, eps, eps2=None):
            n_ = lambda s: sem(f"{tag}_{s}")
            dve.wait_ge(sem(stats), NT)
            for t in range(NT):
                i = dve.bn_aggr(MV[:, t, :], ST[:, 6 * t:6 * t + 6])
            i.then_inc(n_("mv"), 1)
            dve.wait_ge(n_("mv"), 1)
            dve.tensor_scalar(SD[:, :], MV[:, :, 1], eps, None, ALU.add).then_inc(n_("ve"), 1)
            dve.wait_ge(n_("sd"), 1)
            dve.reciprocal(RS[:, :], SD[:, :]).then_inc(n_("rs"), 1)
            dve.wait_ge(n_("rs"), 1)
            if eps2 is None:
                return
            dve.tensor_tensor(SD2[:, :], MV[:, :, 1], RS[:, :], ALU.mult).then_inc(n_("v2"), 1)
            dve.wait_ge(n_("v2"), 1)
            dve.tensor_tensor(SD2[:, :], SD2[:, :], RS[:, :], ALU.mult).then_inc(n_("v2"), 1)
            dve.wait_ge(n_("v2"), 2)
            dve.tensor_scalar(SD2[:, :], SD2[:, :], eps2, None, ALU.add).then_inc(n_("v2"), 1)
            dve.wait_ge(n_("sd"), 2)
            dve.reciprocal(SD2[:, :], SD2[:, :]).then_inc(n_("v2"), 1)
            dve.wait_ge(n_("v2"), 4)
            dve.tensor_tensor(RS2[:, :], SD2[:, :], RS[:, :], ALU.mult).then_inc(n_("v2"), 1)
            dve.wait_ge(n_("v2"), 5)

        def norm_stats_act(act, tag, eps2=None):
            n_ = lambda s: sem(f"{tag}_{s}")
            act.wait_ge(n_("ve"), 1)
            act.activation(SD[:, :], SD[:, :], ACT.Sqrt).then_inc(n_("sd"), 1)
            if eps2 is not None:
                act.wait_ge(n_("v2"), 3)
                act.activation(SD2[:, :], SD2[:, :], ACT.Sqrt).then_inc(n_("sd"), 1)

        def normalise(dve, i, u, src, dst, rs, done):
            for t in range(GT):
                k = (2 * i + u) * GT + t
                last = dve.tensor_scalar(dst[:, t * D:(t + 1) * D], src[:, bass.ds(k * D, D)],
                                         MV[:, :, :].rearrange("p t s -> p (t s)")[:, bass.ds(2 * k, 1)],
                                         rs[:, bass.ds(k, 1)], ALU.subtract, ALU.mult)
            last.then_inc(done, 1)

        def normed(dve, g, src, dst, rs, done):
            for t in range(GT):
                k = g * GT + t
                last = dve.tensor_scalar(dst[:, t * D:(t + 1) * D], src[:, k * D:(k + 1) * D],
                                         MV[:, k, 0:1], rs[:, k:k + 1], ALU.subtract, ALU.mult)
            last.then_inc(done, 1)

        def bank(u, k):
            return PS[:, 4 * u + k, :]

        def linear_attention():
            at[0] = 0
            h0 = [cut(G) for _ in range(2)]
            hn = [cut(G) for _ in range(2)]
            hb = [cut(G) for _ in range(2)]
            hT = [cut(G) for _ in range(2)]
            eq = [cut(G) for _ in range(2)]
            rq = [cut(G) for _ in range(2)]
            ek = [cut(G) for _ in range(2)]
            rk = [cut(G) for _ in range(2)]
            fq = [cut(G) for _ in range(2)]
            fk = [cut(G) for _ in range(2)]
            va = [cut(GT * (D + 1)).rearrange("p (t c) -> p t c", t=GT) for _ in range(2)]
            kvm = [cut(2 * (D + H)).rearrange("p (b c) -> p b c", b=2) for _ in range(2)]
            ks = [cut(2) for _ in range(2)]
            den = [cut(GT * H) for _ in range(2)]
            rec = [cut(GT * H) for _ in range(2)]
            att = [cut(G) for _ in range(2)]
            aT = [cut(G) for _ in range(2)]
            v = lambda i, u: 2 * i + u + 1
            kvp = lambda u: PS[:, 4 * u + 2:4 * u + 4, :].rearrange("p b (t c) -> p (b t) c", t=2)
            nd = lambda u, k: PS[:, 4 * u + 1 + k, 0:2 * (D + H)].rearrange("p (t c) -> p t c", t=2)
            kvb = lambda u: bank(u, 0)[:, 0:2 * (D + 1)].rearrange("p (b c) -> p b c", b=2)

            with nc.Block() as block:
                @block.vector
                def _(dve):
                    norm_stats_dve(dve, "a0", "stats0", 1e-5, 1e-5)
                    for u in range(2):
                        dve.memset(va[u][:, :, D:D + 1], 1.0).then_inc(sem("a0_ones"), 1)
                    dve.wait_ge(sem("const_ready"), CONST)
                    for i in range(0, NG // 2):
                        for u in range(2):
                            normalise(dve, i, u, X, hn[u], RS2, sem("a0_hn"))
                        for u in range(2):
                            normalise(dve, i, u, X, h0[u], RS, sem("a0_h0"))
                        for u in range(2):
                            dve.wait_ge(sem("a0_k"), v(i, u))
                            dve.scalar_tensor_tensor(out=fk[u][:, :], in0=ek[u][:, :], scalar=1.0, in1=rk[u][:, :],
                                                     op0=ALU.min, op1=ALU.add).then_inc(sem("a0_fk"), 1)
                        for u in range(2):
                            dve.wait_ge(sem("a0_q"), v(i, u))
                            dve.scalar_tensor_tensor(out=fq[u][:, :], in0=eq[u][:, :], scalar=1.0, in1=rq[u][:, :],
                                                     op0=ALU.min, op1=ALU.add).then_inc(sem("a0_fq"), 1)
                        for u in range(2):
                            dve.wait_ge(sem("a0_kv"), v(i, u))
                            dve.tensor_copy(ks[u][:, :], kvb(u)[:, :, D]).then_inc(sem("a0_ks"), 1)
                            dve.tensor_tensor(kvm[u][:, :, 0:D], kvb(u)[:, :, 0:D], over(BM[:, :], 2), ALU.mult)
                            dve.wait_ge(sem("a0_ks"), v(i, u))
                            for b in range(2):
                                last = dve.tensor_scalar(kvm[u][:, b, D:D + H], HM[:, :], ks[u][:, b:b + 1], None,
                                                         ALU.mult)
                            last.then_inc(sem("a0_kvm"), 1)
                        for u in range(2):
                            dve.wait_ge(sem("a0_nd"), v(i, u))
                            for k in range(2):
                                last = dve.tensor_scalar(tiles(den[u][:, 2 * k * H:2 * (k + 1) * H], 2),
                                                         nd(u, k)[:, :, D:D + H], 1e-6, None, ALU.add)
                            last.then_inc(sem("a0_den"), 1)
                            dve.wait_ge(sem("a0_den"), v(i, u))
                            dve.reciprocal(rec[u][:, :], den[u][:, :]).then_inc(sem("a0_rec"), 1)
                            dve.wait_ge(sem("a0_rec"), v(i, u))
                            for t in range(GT):
                                last = dve.tensor_tensor(
                                    att[u][:, t * D:(t + 1) * D].rearrange("p (h e) -> p h e", h=H),
                                    nd(u, t // 2)[:, t % 2, 0:D].rearrange("p (h e) -> p h e", h=H),
                                    over(rec[u][:, t * H:(t + 1) * H], DH, 2), ALU.mult)
                            last.then_inc(sem("a0_att"), 1)
                        for u in range(2):
                            dve.wait_ge(sem("a0_proj"), v(i, u))
                            dve.wait_ge(sem("a0_hb"), v(i, u))
                            dve.tensor_tensor(XX[:, bass.ds((2 * i + u) * G, G)], bank(u, 3), hb[u][:, :],
                                              ALU.add).then_inc(sem("a0_xx"), 1)
                        for u in range(2):
                            dve.wait_ge(sem("a0_xx"), v(i, u))
                            for t in range(GT):
                                k = (2 * i + u) * GT + t
                                dve.bn_stats(ST[:, bass.ds(6 * k, 6)], XX[:, bass.ds(k * D, D)])\
                                    .then_inc(sem("a0_stats"), 1)

                @block.gpsimd
                def _(pool):
                    pool.wait_ge(sem("rows_loaded"), 16)
                    for i in range(0, NG // 2):
                        for u in range(2):
                            pool.wait_ge(sem("a0_h0"), v(i, u))
                            pool.tensor_tensor(tiles(hb[u]), tiles(h0[u]), over(row("projb"), GT), ALU.add)\
                                .then_inc(sem("a0_hb"), 1)

                @block.scalar
                def _(act):
                    norm_stats_act(act, "a0", 1e-5)
                    act.wait_ge(sem("cols_loaded"), 16)
                    for i in range(0, NG // 2):
                        for u in range(2):
                            act.wait_ge(sem("a0_hnT"), v(i, u))
                            act.activation(hT[u][:, :], bank(u, 0), ACT.Identity, bias=col("b1_0"), scale=col("g1_0"))\
                                .then_inc(sem("a0_hT"), 1)
                        for u in range(2):
                            act.wait_ge(sem("a0_kvp"), v(i, u))
                            act.activation(tiles(ek[u]), kvp(u)[:, :, 0:D], ACT.Exp)
                            act.activation(tiles(rk[u]), kvp(u)[:, :, 0:D], ACT.Relu).then_inc(sem("a0_k"), 1)
                            act.activation(va[u][:, :, 0:D], kvp(u)[:, :, D:2 * D], ACT.Copy)\
                                .then_inc(sem("a0_va"), 1)
                        for u in range(2):
                            act.wait_ge(sem("a0_qp"), v(i, u))
                            act.activation(eq[u][:, :], bank(u, 1), ACT.Exp)
                            act.activation(rq[u][:, :], bank(u, 1), ACT.Relu).then_inc(sem("a0_q"), 1)
                        for u in range(2):
                            act.wait_ge(sem("a0_attT"), v(i, u))
                            act.activation(aT[u][:, :], bank(u, 0), ACT.Copy).then_inc(sem("a0_aT"), 1)

                @block.tensor
                def _(pe):
                    pe.wait_ge(sem("const_ready"), CONST)
                    pe.wait_ge(sem("w0_loaded"), 16)
                    for i in range(0, NG // 2):
                        for u in range(2):
                            pe.wait_ge(sem("a0_hn"), v(i, u))
                            for t in range(GT):
                                last = pe.transpose(bank(u, 0)[:, t * P:(t + 1) * P], hn[u][:, t * D:(t + 1) * D],
                                                    ident[:, :])
                            last.then_inc(sem("a0_hnT"), 1)
                        for u in range(2):
                            pe.wait_ge(sem("a0_hT"), v(i, u))
                            for t in range(GT):
                                last = pe.matmul(kvp(u)[:, t, :], hT[u][:, t * P:(t + 1) * P],
                                                 w("qkv0", D, 2 * D), start=True, stop=True)
                            last.then_inc(sem("a0_kvp"), 1)
                            pe.matmul(bank(u, 1), w("qkv0", 0, D), hT[u][:, :], start=True, stop=True)\
                                .then_inc(sem("a0_qp"), 1)
                        for u in range(2):
                            pe.wait_ge(sem("a0_fk"), v(i, u))
                            pe.wait_ge(sem("a0_va"), v(i, u))
                            for b in range(2):
                                for t in range(2):
                                    last = pe.matmul(kvb(u)[:, b, :], fk[u][:, (2 * b + t) * D:(2 * b + t + 1) * D],
                                                     va[u][:, 2 * b + t, :], start=(t == 0), stop=(t == 1))
                            last.then_inc(sem("a0_kv"), 1)
                        for u in range(2):
                            pe.wait_ge(sem("a0_kvm"), v(i, u))
                            pe.wait_ge(sem("a0_fq"), v(i, u))
                            for t in range(GT):
                                last = pe.matmul(nd(u, t // 2)[:, t % 2, :], fq[u][:, t * P:(t + 1) * P],
                                                 kvm[u][:, t // 2, :], start=True, stop=True)
                            last.then_inc(sem("a0_nd"), 1)
                        for u in range(2):
                            pe.wait_ge(sem("a0_att"), v(i, u))
                            for t in range(GT):
                                last = pe.transpose(bank(u, 0)[:, t * P:(t + 1) * P], att[u][:, t * D:(t + 1) * D],
                                                    ident[:, :])
                            last.then_inc(sem("a0_attT"), 1)
                        for u in range(2):
                            pe.wait_ge(sem("a0_aT"), v(i, u))
                            for t in range(GT):
                                last = pe.matmul(bank(u, 3)[:, t * D:(t + 1) * D], aT[u][:, t * P:(t + 1) * P],
                                                 w("proj0"), start=True, stop=True)
                            last.then_inc(sem("a0_proj"), 1)

        def feed_forward(L, func, eps, stats):
            z = f"f{L}_"
            at[0] = 0
            hn = [cut(G) for _ in range(2)]
            hT = [cut(G) for _ in range(2)]
            res = [cut(G) for _ in range(2)]
            res2 = [cut(G) for _ in range(2)]
            hid = [cut(HC * G) for _ in range(2)]
            v = lambda i, u: 2 * i + u + 1
            order = [1, 2, 3, 0]

            with nc.Block() as block:
                @block.vector
                def _(dve):
                    norm_stats_dve(dve, f"f{L}", stats, eps)
                    for i in range(0, NG // 2):
                        for u in range(2):
                            normalise(dve, i, u, XX, hn[u], RS, sem(z + "hn"))
                        for u in range(2):
                            dve.wait_ge(sem(z + "fc2"), v(i, u))
                            dve.wait_ge(sem(z + "res"), v(i, u))
                            dve.tensor_tensor(X[:, bass.ds((2 * i + u) * G, G)], bank(u, 1), res2[u][:, :],
                                              ALU.add).then_inc(sem(z + "x"), 1)
                        for u in range(2):
                            dve.wait_ge(sem(z + "x"), v(i, u))
                            for t in range(GT):
                                k = (2 * i + u) * GT + t
                                dve.bn_stats(ST[:, bass.ds(6 * k, 6)], X[:, bass.ds(k * D, D)])\
                                    .then_inc(sem(z + "stats"), 1)

                @block.gpsimd
                def _(pool):
                    for i in range(0, NG // 2):
                        for u in range(2):
                            pool.wait_ge(sem(z + "hn"), v(i, u))
                            g = bass.ds((2 * i + u) * G, G)
                            pool.tensor_tensor(res[u][:, :], X[:, g], XX[:, g], ALU.add).then_inc(sem(z + "sum"), 1)
                            pool.wait_ge(sem(z + "sum"), v(i, u))
                            pool.tensor_tensor(tiles(res2[u]), tiles(res[u]), over(row(f"fc2b_{L}"), GT), ALU.add)\
                                .then_inc(sem(z + "res"), 1)

                @block.scalar
                def _(act):
                    norm_stats_act(act, f"f{L}")
                    for i in range(0, NG // 2):
                        for u in range(2):
                            act.wait_ge(sem(z + "hnT"), v(i, u))
                            act.activation(hT[u][:, :], bank(u, 0), ACT.Identity, bias=col(f"b2_{L}"),
                                           scale=col(f"g2_{L}")).then_inc(sem(z + "hT"), 1)
                        for u in range(2):
                            for c in range(HC):
                                act.wait_ge(sem(z + "fc1"), (2 * i + u) * HC + c + 1)
                                act.activation(hid[u][:, c * G:(c + 1) * G], bank(u, order[c]), func,
                                               bias=col(f"fcb_{L}", c)).then_inc(sem(z + "hid"), 1)

                @block.tensor
                def _(pe):
                    if L:
                        pe.wait_ge(sem("w3_loaded"), 16)
                    for i in range(0, NG // 2):
                        for u in range(2):
                            pe.wait_ge(sem(z + "hn"), v(i, u))
                            for t in range(GT):
                                last = pe.transpose(bank(u, 0)[:, t * P:(t + 1) * P], hn[u][:, t * D:(t + 1) * D],
                                                    ident[:, :])
                            last.then_inc(sem(z + "hnT"), 1)
                        for u in range(2):
                            pe.wait_ge(sem(z + "hT"), v(i, u))
                            for c in range(HC):
                                pe.matmul(bank(u, order[c]), w(f"fc1_{L}", c * P, P), hT[u][:, :], start=True,
                                          stop=True).then_inc(sem(z + "fc1"), 1)
                        for u in range(2):
                            pe.wait_ge(sem(z + "hid"), (2 * i + u + 1) * HC)
                            for t in range(GT):
                                for c in range(HC):
                                    last = pe.matmul(bank(u, 1)[:, t * D:(t + 1) * D],
                                                     hid[u][:, c * G + t * P:c * G + (t + 1) * P],
                                                     w(f"fc2_{L}", c * D, D), start=(c == 0), stop=(c == HC - 1))
                            last.then_inc(sem(z + "fc2"), 1)

        MROW = 96
        DROW = 72
        DR = 12
        KTILE = S // P
        VB = [VA[:, NT * D + k * 1024:NT * D + (k + 1) * 1024].rearrange("p (t h c) -> p t h c", t=KTILE, h=H)
              for k in range(2)]

        def cross_memory():
            at[0] = 0
            QS = cut(4 * H * S, BF16)
            KS = cut(4 * H * S, BF16)
            bias = cut(KTILE * S).rearrange("p (t c) -> p t c", t=KTILE)
            dist = cut(P, BF16)
            decI = cut(3 * P, BF16).rearrange("p (a c) -> p a c", a=3)
            return QS, KS, bias, dist, decI

        def spread_values(pool, b, done):
            for jj in range(2):
                dst = VB[b % 2].rearrange("p t (x j c) e -> p (t x) j c e", j=2, c=4)
                src = VA[:, b * S:(b + 1) * S].rearrange("p (x j c e) -> p x j c e", j=2, c=4, e=DH)
                last = pool.tensor_copy(dst[:, :, jj, :, 16 * jj:16 * jj + DH], src[:, :, jj])
            last.then_inc(done, 1)

        LOAD = 16 * 4

        def loaded(L, b):
            return sem(f"parts{L}{b % 2}_loaded")

        def stored(L, g):
            return sem(f"parts{L}{g % 2}_stored")

        def load_stacks(sp, L, b, QS, KS):
            at_ = bass.ds(slot(b), H * S)
            sp.wait_ge(stored(L, b // 2), 64 * (b // 4 + 1))
            for a in range(3):
                sp.dma_start(QS[24 * a:24 * a + 24, at_],
                             over(scratch[L][b, 0, a].rearrange("(e h) t -> e (h t)", h=H), 3, 0))\
                    .then_inc(loaded(L, b), 16)
            sp.dma_start(KS[0:72, at_], over(scratch[L][b, 1].rearrange("a (e h) t -> (a e) (h t)", h=H), 3, 0))\
                .then_inc(loaded(L, b), 16)

        def slot(b):
            return b % 4 * (H * S)

        def cross_prepare(L, stats):
            z = f"x{L}_"
            QS, KS, bias, dist, decI = cross_memory()
            V = VA[:, 0:NT * D]
            gap = cut(P)
            gapi = cut(P).bitcast(I32)
            dec = cut(6)
            decb = cut(2, BF16)
            decrow = cut(2)
            PR = cut(4 * S + 3)
            QD, KD = cut(S, BF16), cut(S, BF16)
            hn = [cut(G) for _ in range(2)]
            hT = [cut(G) for _ in range(2)]
            qk = [cut(2 * G).rearrange("p (k t) -> p k t", k=2) for _ in range(2)]
            rem = [cut(2 * G).rearrange("p (k t) -> p k t", k=2) for _ in range(2)]
            cg = [cut(G) for _ in range(2)]
            bq = cut(1)
            parts = [cut(6 * G, BF16).rearrange("p (k a t) -> p k a t", k=2, a=3) for _ in range(2)]
            v = lambda i, u: 2 * i + u + 1

            def decay_tables(dve):
                s, c = sem(z + "d"), dec
                dve.tensor_scalar(c[:, 0:1], row("decay"), -1.0, None, ALU.mult).then_inc(s, 1)
                dve.wait_ge(sem(z + "iota"), 1)
                dve.tensor_copy(gap, gapi).then_inc(s, 1)
                dve.wait_ge(s, 2)
                dve.tensor_copy(decb[:, 0:1], c[:, 0:1]).then_inc(s, 1)
                dve.scalar_tensor_tensor(out=gap, in0=gap, scalar=-1.0, in1=gap, op0=ALU.mult,
                                         op1=ALU.max).then_inc(s, 1)
                dve.wait_ge(s, 4)
                dve.tensor_copy(c[:, 1:2], decb[:, 0:1]).then_inc(s, 1)
                dve.tensor_copy(dist, gap).then_inc(s, 1)
                dve.wait_ge(sem(z + "bias"), 1)
                for t in range(KTILE):
                    dve.tensor_scalar(bias[:, t, t * P:(t + 1) * P], gap, c[:, 0:1], None, ALU.mult)\
                        .then_inc(s, 1)
                dve.wait_ge(s, 8)
                dve.tensor_tensor(c[:, 4:5], c[:, 0:1], c[:, 1:2], ALU.subtract).then_inc(s, 1)
                dve.wait_ge(s, 9)
                dve.tensor_copy(decb[:, 1:2], c[:, 4:5]).then_inc(s, 1)
                dve.wait_ge(s, 10)
                dve.tensor_copy(c[:, 2:3], decb[:, 1:2]).then_inc(s, 1)
                dve.wait_ge(s, 11)
                dve.tensor_tensor(c[:, 3:4], c[:, 4:5], c[:, 2:3], ALU.subtract).then_inc(s, 1)
                dve.wait_ge(s, 12)
                for a in range(3):
                    dve.tensor_scalar(decI[:, a, :], ident[:, :], c[:, 1 + a:2 + a], None, ALU.mult)\
                        .then_inc(s, 1)
                pick = PR[0:DR, 4 * S:4 * S + 3]
                dve.wait_ge(sem(z + "positions"), 16)
                dve.tensor_scalar(decrow[0:DR, 0:1], pick[:, 0:1], c[0:DR, 1:2], None, ALU.mult).then_inc(s, 1)
                for a in (1, 2):
                    dve.wait_ge(s, 15 + a)
                    dve.scalar_tensor_tensor(out=decrow[0:DR, 0:1], in0=pick[:, a:a + 1],
                                             scalar=c[0:DR, 1 + a:2 + a], in1=decrow[0:DR, 0:1], op0=ALU.mult,
                                             op1=ALU.add).then_inc(s, 1)
                dve.wait_ge(s, 18)
                for k, rows_ in enumerate((QD, KD)):
                    dve.scalar_tensor_tensor(out=rows_[0:DR], in0=PR[0:DR, (2 * k + 1) * S:(2 * k + 2) * S],
                                             scalar=decrow[0:DR, 0:1], in1=PR[0:DR, 2 * k * S:(2 * k + 1) * S],
                                             op0=ALU.mult, op1=ALU.add).then_inc(sem(z + "decay_rows"), 1)

            with nc.Block() as block:
                @block.gpsimd
                def _(pool):
                    clear = sem(z + "cleared")
                    if L == 0:
                        pool.memset(bias, 0.0).then_inc(clear, 1)
                        pool.memset(dist, 0.0).then_inc(clear, 1)
                    else:
                        pool.iota(gapi, pattern=[[-1, P]], base=0, channel_multiplier=1).then_inc(sem(z + "iota"), 1)
                        pool.memset(bias, 0.0).then_inc(sem(z + "bias"), 1)
                    pool.memset(QS.bitcast(F32), 0.0).then_inc(clear, 1)
                    pool.memset(KS[0:MROW].bitcast(F32), 0.0).then_inc(clear, 1)
                    if L == 0:
                        for m in VB:
                            pool.memset(m, 0.0).then_inc(clear, 1)
                    pool.wait_ge(clear, 6 if L == 0 else 2)
                    pool.memset(KS[MROW:P].bitcast(F32), MINUS_ONES).then_inc(clear, 1)
                    if L == 0:
                        pool.wait_ge(clear, 7)
                        for m in VB:
                            for jj in range(2):
                                pool.memset(m.rearrange("p t (x j c) e -> p (t x) j c e", j=2, c=4)
                                            [:, :, jj, :, 16 * jj + DH:16 * jj + 16], 1.0).then_inc(clear, 1)
                        pool.affine_select(out=bias, in_=bias, compare_op=ALU.is_ge, fill=-BIG, base=0,
                                           pattern=[[P, 2], [-1, S]], channel_multiplier=1).then_inc(clear, 1)
                        pool.affine_select(out=dist, in_=dist, compare_op=ALU.is_ge,
                                           fill=-BIG, base=0, pattern=[[1, P]], channel_multiplier=-1)\
                            .then_inc(clear, 1)
                    pool.wait_ge(clear, 13 if L == 0 else 3)
                    for g in range(NG):
                        pool.wait_ge(sem(z + "hn"), g + 1)
                        s_ = slice(g * G, (g + 1) * G)
                        pool.tensor_tensor(tiles(X[:, s_]), tiles(X[:, s_]), over(row(f"bo{L}"), GT), ALU.add)\
                            .then_inc(sem(z + "xb"), 1)
                    for b in range(2):
                        pool.wait_ge(sem(z + "v"), 1)
                        spread_values(pool, b, sem(z + "VB"))

                @block.vector
                def _(dve):
                    norm_stats_dve(dve, f"x{L}", stats, 1e-5)
                    dve.tensor_scalar(bq, col(f"bq{L}"), SCALE, None, ALU.mult).then_inc(sem(z + "bq"), 1)
                    normed(dve, 0, X, hn[0], RS, sem(z + "hn"))
                    normed(dve, 1, X, hn[1], RS, sem(z + "hn"))
                    for g in range(NG):
                        u = g % 2
                        dve.wait_ge(sem(z + "vp"), g + 1)
                        dve.tensor_tensor(tiles(V[:, g * G:(g + 1) * G]), tiles(bank(u, 3)),
                                          over(row(f"bv{L}"), GT), ALU.add).then_inc(sem(z + "v"), 1)
                        dve.wait_ge(sem(z + "p1"), g + 1)
                        dve.tensor_tensor(rem[u], qk[u], parts[u][:, :, 0, :], ALU.subtract)\
                            .then_inc(sem(z + "r1"), 1)
                        if g + 2 < NG:
                            normed(dve, g + 2, X, hn[u], RS, sem(z + "hn"))
                        elif g == NG - 2 and L == 1:
                            decay_tables(dve)
                        dve.wait_ge(sem(z + "p2"), g + 1)
                        dve.tensor_tensor(parts[u][:, :, 2, :], rem[u], parts[u][:, :, 1, :], ALU.subtract)\
                            .then_inc(sem(z + "p3"), 1)

                @block.scalar
                def _(act):
                    norm_stats_act(act, f"x{L}")
                    act.wait_ge(sem(z + "bq"), 1)

                    def transposed(g):
                        act.wait_ge(sem(z + "hnT"), g + 1)
                        act.activation(hT[g % 2], bank(g % 2, 0), ACT.Copy).then_inc(sem(z + "hT"), 1)

                    transposed(0)
                    for g in range(NG):
                        u = g % 2
                        act.wait_ge(sem(z + "qkp"), g + 1)
                        if g >= 2:
                            act.wait_ge(stored(L, g), 64 * (g // 2))
                        for k, (bias_, scale) in enumerate(((bq, SCALE), (col(f"bk{L}"), 1.0))):
                            act.activation(qk[u][:, k, :], bank(u, 1 + k), ACT.Identity, bias=bias_, scale=scale)
                            last = act.activation(parts[u][:, k, 0, :], bank(u, 1 + k), ACT.Identity, bias=bias_,
                                                  scale=scale)
                        last.then_inc(sem(z + "p1"), 1)
                        if g + 1 < NG:
                            transposed(g + 1)
                        act.wait_ge(sem(z + "r1"), g + 1)
                        act.activation(parts[u][:, :, 1, :], rem[u], ACT.Copy).then_inc(sem(z + "p2"), 1)

                @block.tensor
                def _(pe):
                    def query(g):
                        pe.wait_ge(sem(z + "hT"), g + 1)
                        pe.matmul(bank(g % 2, 1), w(f"xq{L}"), hT[g % 2], start=True, stop=True)\
                            .then_inc(sem(z + "qkp"), 1)

                    pe.wait_ge(sem(f"w{1 if L == 0 else 4}_loaded"), 16)
                    for g in range(NG):
                        u = g % 2
                        pe.wait_ge(sem(z + f"ctx{u}"), 16 * (g // 2 + 1))
                        if g >= 2:
                            pe.wait_ge(sem(z + "p1"), g - 1)
                            pe.wait_ge(sem(z + "v"), g - 1)
                        pe.matmul(bank(u, 2), w(f"xk{L}"), cg[u], start=True, stop=True)
                        for t in range(GT):
                            last = pe.matmul(bank(u, 3)[:, t * D:(t + 1) * D], cg[u][:, t * P:(t + 1) * P],
                                             w(f"xv{L}"), start=True, stop=True)
                        last.then_inc(sem(z + "vp"), 1)
                        pe.wait_ge(sem(z + "hn"), g + 1)
                        for t in range(GT):
                            last = pe.transpose(bank(u, 0)[:, t * P:(t + 1) * P], hn[u][:, t * D:(t + 1) * D],
                                                ident[:, :])
                        last.then_inc(sem(z + "hnT"), 1)
                        if g:
                            query(g - 1)
                    query(NG - 1)

                @block.sync
                def _(sp):
                    def context(g):
                        sp.dma_start(cg[g % 2], ctxT[:, g * G:(g + 1) * G]).then_inc(sem(z + f"ctx{g % 2}"), 16)

                    context(0)
                    context(1)
                    if L == 1:
                        sp.dma_start(PR[0:DR], positions).then_inc(sem(z + "positions"), 16)
                    for g in range(NG):
                        if g + 2 < NG:
                            sp.wait_ge(sem(z + "vp"), g + 1)
                            context(g + 2)
                        sp.wait_ge(sem(z + "p3"), g + 1)
                        for b in range(2):
                            for k in range(2):
                                sp.dma_start(scratch[L][2 * g + b, k].rearrange("a r t -> r a t"),
                                             parts[g % 2][:, k, :, b * S:(b + 1) * S])\
                                    .then_inc(stored(L, g), 16)
                        if g == NG - 2 and L == 1:
                            sp.wait_ge(sem(z + "cleared"), 3)
                            sp.wait_ge(sem(z + "decay_rows"), 2)
                            for stack, rows_ in ((QS, QD), (KS, KD)):
                                sp.dma_start(stack[DROW:DROW + DR, :].rearrange("r (n t) -> r n t", t=S),
                                             over(rows_[0:DR], 4 * H)).then_inc(sem(z + "filled"), 16)
                        if g == 1:
                            sp.wait_ge(sem(z + "cleared"), 4 if L == 0 else 2)
                            load_stacks(sp, L, 0, QS, KS)
                            load_stacks(sp, L, 1, QS, KS)
                    if L == 1:
                        sp.wait_ge(sem(z + "filled"), 32)

        def cross_attend(L):
            z = f"y{L}_"
            QS, KS, bias, dist, decI = cross_memory()
            V = VA[:, 0:NT * D]
            PT = cut(4 * 2 * 512).rearrange("p (n s c) -> p n s c", n=4, s=2)
            junk = cut(8 * S, BF16).rearrange("p (n c) -> p n c", n=8)
            M = cut(2 * H).rearrange("p (t h) -> p t h", t=2)
            MR = cut(2 * 8).rearrange("p (t h) -> p t h", t=2)
            MP = cut(2 * 2 * 24, BF16).rearrange("p (f t c) -> p f t c", f=2, t=2)
            mT = cut(2 * S, BF16).rearrange("p (f c) -> p f c", f=2)
            OT = VA[:, NT * D + 2048:NT * D + 2560]
            aT = VA[:, NT * D + 2560:NT * D + 2816]
            att = VA[:, NT * D + 2816:NT * D + 3072].rearrange("p (t c) -> p t c", t=2)
            rec = VA[:, NT * D + 3072:NT * D + 3104].rearrange("p (x h) -> p x h", x=4)
            misc = PS[:, 7, :]
            miscb = PS[:, 7, :].bitcast(BF16)
            O = PS[:, 6, :]
            KEYS = [P, 2 * P] if L == 0 else [S, S]
            NCOL = 3 * P if L == 0 else 2 * S

            def wait(e, s, value):
                if not isinstance(value, int) or value > 0:
                    e.wait_ge(sem(z + s), value)

            def pe_max_scores(pe, b, pos):
                wait(pe, "max", 16 * b + pos - 1)
                for t in range(2):
                    last = pe.matmul(PS[:, pos % 2, t * S:t * S + KEYS[t]],
                                     QS[0:MROW, bass.ds(slot(b) + pos * S + t * P, P)],
                                     KS[0:MROW, bass.ds(slot(b) + pos * S, KEYS[t])], start=True, stop=True)
                last.then_inc(sem(z + "A"), 1)

            def pe_scores(pe, b, n, s):
                if s == 0:
                    wait(pe, "exp", 8 * b + n - 1)
                    if n % 4 == 0:
                        wait(pe, f"mrow{n // 4}", 48 * b + 48)
                pos = 2 * n + s
                bk = PS[:, 2 + 2 * (n % 2) + s, :]
                for t in range(2):
                    q0 = P * t if L == 0 else 0
                    pe.matmul(bk[:, t * S:t * S + S - q0], KS[:, bass.ds(slot(b) + pos * S + t * P, P)],
                              QS[:, bass.ds(slot(b) + pos * S + q0, S - q0)], start=True, stop=True)
                    own = t * S + t * P - q0
                    for lhs in ([identb[:, :]] if L == 0 else [decI[:, a, :] for a in range(3)]):
                        last = pe.matmul(bk[:, own:own + P], lhs, dist, start=False, stop=True,
                                         skip_group_check=True)
                if s == 1:
                    last.then_inc(sem(z + "S"), 1)

            def pe_values(pe, b, j):
                wait(pe, "exp", 8 * b + 2 * j + 2)
                if j == 0:
                    wait(pe, "OT", b)
                    wait(pe, "VB", b - 1)
                for t in range(2):
                    q0 = P * t if L == 0 else 0
                    for c in range(4):
                        first = t == 0 and j == 0
                        last = pe.matmul(
                            O[32 * c:32 * c + 32, (j // 2) * S + q0:(j // 2 + 1) * S],
                            VB[b % 2][:, t, 4 * j + c, :], PT[:, (2 * j + c // 2) % 4, c % 2, t * S:t * S + S - q0],
                            start=first, stop=(t == 1), skip_group_check=True)
                last.then_inc(sem(z + "pv"), 1)

            def pe_mT(pe, b, f):
                wait(pe, "mp", 2 * b + f + 1)
                for t in range(2):
                    last = pe.transpose(miscb[0:24, t * P:(t + 1) * P], MP[:, f, t, :], identb[:, :])
                last.then_inc(sem(z + "mTp"), 1)

            def pe_tail1(pe, b):
                wait(pe, "OT", b + 1)
                for x4 in range(2):
                    for t in range(2):
                        last = pe.transpose(misc[:, (2 * x4 + t) * P:(2 * x4 + t + 1) * P],
                                            OT[:, x4 * S + t * P:x4 * S + (t + 1) * P], ident[:, :])
                last.then_inc(sem(z + "t1"), 1)

            def pe_tail2(pe, b):
                wait(pe, "att", b + 1)
                for t in range(2):
                    last = pe.transpose(misc[:, t * P:(t + 1) * P], att[:, t, :], ident[:, :])
                last.then_inc(sem(z + "t2"), 1)

            def pe_tail3(pe, b):
                wait(pe, "aT", b + 1)
                for t in range(2):
                    last = pe.matmul(misc[:, t * D:(t + 1) * D], aT[:, t * P:(t + 1) * P], w(f"xo{L}"),
                                     start=True, stop=True)
                last.then_inc(sem(z + "o"), 1)

            def pe_iteration(pe, b):
                first, last = b == 0, b == B - 1
                for n in range(8):
                    if n == 1:
                        wait(pe, "x", b - 1)
                        pe_mT(pe, b, 1)
                    if n == 5 and not last:
                        wait(pe, "att", b)
                        wait(pe, "mT", 2 * b + 2)
                        pe_mT(pe, b + 1, 0)
                    if n == 0 and not last:
                        pe.wait_ge(loaded(L, b + 1), LOAD * ((b + 1) // 2 + 1))
                    for s in range(2):
                        pe_scores(pe, b, n, s)
                        if not last:
                            pe_max_scores(pe, b + 1, 2 * n + s)
                    if n == 1 and not first:
                        wait(pe, "mT", 2 * b + 2)
                        pe_tail1(pe, b - 1)
                    if n == 5 and not first:
                        if not last:
                            wait(pe, "mT", 2 * b + 3)
                        pe_tail2(pe, b - 1)
                    if n == 6 and not first:
                        pe_tail3(pe, b - 1)
                    if n in (3, 5, 7):
                        pe_values(pe, b, (n - 3) // 2)
                pe_values(pe, b, 3)

            def dve_max(dve, b, n):
                for pos in (2 * n, 2 * n + 1):
                    wait(dve, "A", 16 * b + pos + 1)
                    wait(dve, "max", 16 * b + pos - 3)
                    for t in range(2):
                        last = dve.tensor_tensor_reduce(junk[:, 2 * (pos % 4) + t, 0:KEYS[t]],
                                                        PS[:, pos % 2, t * S:t * S + KEYS[t]],
                                                        bias[:, t, 0:KEYS[t]], 1.0, LOW, ALU.add, ALU.max,
                                                        M[:, t, pos:pos + 1])
                    last.then_inc(sem(z + "max"), 1)

            def pool_parts(pool, b, f):
                m, mp = M[:, :, 8 * f:8 * f + 8], MP[:, f].rearrange("p t (a h) -> p t a h", a=3)
                wait(pool, "max", 16 * b + 8 * f + 8)
                s, k = sem(z + "split"), 6 * b + 3 * f
                pool.tensor_copy(mp[:, :, 0, :], m).then_inc(s, 1)
                pool.wait_ge(s, k + 1)
                pool.tensor_tensor(MR, m, mp[:, :, 0, :], ALU.subtract).then_inc(s, 1)
                pool.wait_ge(s, k + 2)
                pool.tensor_copy(mp[:, :, 1, :], MR).then_inc(s, 1)
                pool.wait_ge(s, k + 3)
                pool.tensor_tensor(mp[:, :, 2, :], MR, mp[:, :, 1, :], ALU.subtract).then_inc(sem(z + "mp"), 1)

            def dve_normalise(dve, b):
                T1 = misc.rearrange("p (x c e) -> p x c e", x=4, e=16)
                wait(dve, "t1", b + 1)
                dve.reciprocal(rec, T1[:, :, :, DH]).then_inc(sem(z + "rec"), 1)
                wait(dve, "rec", b + 1)
                for x4 in range(2):
                    for t in range(2):
                        o = att[:, t, x4 * 64:(x4 + 1) * 64].rearrange("p (j c e) -> p c j e", j=2, e=DH)
                        i_ = T1[:, 2 * x4 + t, :, 0:DH].rearrange("p (c j) e -> p c j e", j=2)
                        r = over(rec[:, 2 * x4 + t, :].rearrange("p (c j) -> p c j", j=2), DH, 3)
                        last = dve.tensor_tensor(o, i_, r, ALU.mult)
                last.then_inc(sem(z + "att"), 1)

            def dve_residual(dve, b):
                wait(dve, "o", b + 1)
                xs = X[:, b * S:(b + 1) * S]
                dve.tensor_tensor(xs, misc[:, 0:S], xs, ALU.add).then_inc(sem(z + "x"), 1)

            def dve_stats(dve, b):
                wait(dve, "x", b + 1)
                for t in range(2):
                    k = 2 * b + t
                    dve.bn_stats(ST[:, 6 * k:6 * k + 6], X[:, k * D:(k + 1) * D]).then_inc(sem(z + "stats"), 1)

            def dve_iteration(dve, b):
                first, last = b == 0, b == B - 1
                for n in range(8):
                    if not last:
                        dve_max(dve, b + 1, n)
                    if n == 7 and not first:
                        dve_residual(dve, b - 1)
                    if n == 1 and b >= 2:
                        dve_stats(dve, b - 2)
                    if n == 3 and not first:
                        dve_normalise(dve, b - 1)

            def act_exp(act, b, n):
                wait(act, "S", 8 * b + n + 1)
                wait(act, "pv", 4 * b + n // 2 - 1)
                act.activation(PT[:, n % 4, :, 0:NCOL], PS[:, 2 + 2 * (n % 2):4 + 2 * (n % 2), 0:NCOL], ACT.Exp)\
                    .then_inc(sem(z + "exp"), 1)

            def act_mT(act, b, f):
                wait(act, "mTp", 2 * b + f + 1)
                wait(act, f"mrow{f}", 48 * b)
                act.activation(mT[0:24, f, :], miscb[0:24, 0:S], ACT.Copy).then_inc(sem(z + "mT"), 1)

            def act_iteration(act, b):
                first, last = b == 0, b == B - 1
                for n in range(8):
                    act_exp(act, b, n)
                    if n == 0 and not first:
                        wait(act, "pv", 4 * b)
                        act.activation(OT, O, ACT.Copy).then_inc(sem(z + "OT"), 1)
                    if n == 0:
                        act_mT(act, b, 1)
                    if n == 4 and not last:
                        act_mT(act, b + 1, 0)
                    if n == 5 and not first:
                        wait(act, "t2", b)
                        act.activation(aT, misc[:, 0:S], ACT.Copy).then_inc(sem(z + "aT"), 1)

            def sp_mrow(sp, b, f):
                wait(sp, "mT", 2 * b + f + 1)
                for a in range(3):
                    sp.dma_start(QS[MROW + a:MROW + a + 1, bass.ds(slot(b) + f * 8 * S, 8 * S)]
                                 .rearrange("o (h t) -> o h t", h=8),
                                 mT[8 * a:8 * a + 8, f, :]).then_inc(sem(z + f"mrow{f}"), 16)

            def sp_iteration(sp, b):
                sp_mrow(sp, b, 1)
                if b + 3 < B:
                    wait(sp, "pv", 4 * b)
                    sp.wait_ge(loaded(L, b + 3), LOAD * ((b + 1) // 2 + 1))
                    load_stacks(sp, L, b + 3, QS, KS)
                if b + 1 < B:
                    sp_mrow(sp, b + 1, 0)

            with nc.Block() as block:
                @block.gpsimd
                def _(pool):
                    pool_parts(pool, 0, 0)
                    pool_parts(pool, 0, 1)
                    for b in range(B):
                        if 1 <= b < B - 1:
                            wait(pool, "pv", 4 * b)
                            spread_values(pool, b + 1, sem(z + "VB"))
                        if b + 1 < B:
                            pool_parts(pool, b + 1, 0)
                        if b + 1 < B:
                            pool_parts(pool, b + 1, 1)

                @block.sync
                def _(sp):
                    sp.wait_ge(loaded(L, 2), LOAD)
                    load_stacks(sp, L, 2, QS, KS)
                    sp_mrow(sp, 0, 0)
                    for b in range(B):
                        sp_iteration(sp, b)

                @block.tensor
                def _(pe):
                    pe.wait_ge(loaded(L, 0), LOAD)
                    for pos in range(H):
                        pe_max_scores(pe, 0, pos)
                        if pos == 9:
                            pe_mT(pe, 0, 0)
                    wait(pe, "mT", 1)
                    for b in range(B):
                        pe_iteration(pe, b)
                    wait(pe, "x", B - 1)
                    pe_tail1(pe, B - 1)
                    pe_tail2(pe, B - 1)
                    pe_tail3(pe, B - 1)

                @block.vector
                def _(dve):
                    for n in range(8):
                        dve_max(dve, 0, n)
                    for b in range(B):
                        dve_iteration(dve, b)
                    dve_stats(dve, B - 2)
                    dve_normalise(dve, B - 1)
                    dve_residual(dve, B - 1)
                    dve_stats(dve, B - 1)

                @block.scalar
                def _(act):
                    act_mT(act, 0, 0)
                    for b in range(B):
                        act_iteration(act, b)
                    wait(act, "pv", 4 * B)
                    act.activation(OT, O, ACT.Copy).then_inc(sem(z + "OT"), 1)
                    wait(act, "t2", B)
                    act.activation(aT, misc[:, 0:S], ACT.Copy).then_inc(sem(z + "aT"), 1)


        def memory_read(stats):
            at[0] = 0
            hs = cut(NT * D)
            rq = cut(NT * P)
            rk = cut(NMEM)
            hT = [cut(G) for _ in range(2)]
            qu = [cut(G) for _ in range(2)]
            h1 = [cut(G) for _ in range(2)]
            sc = [cut(NMEM) for _ in range(2)]
            ex = [cut(NMEM) for _ in range(2)]
            rep = [cut(NMEM) for _ in range(2)]
            wt = [cut(NMEM) for _ in range(2)]
            wT = [cut(NMEM) for _ in range(2)]
            top = [cut(8) for _ in range(2)]
            ntop = [cut(1) for _ in range(2)]
            den = [cut(1) for _ in range(2)]
            rden = [cut(1) for _ in range(2)]
            coef = [cut(1) for _ in range(2)]
            lrn, var, lv, sig, unc, gate = (cut(NT) for _ in range(6))
            lsum, lall, linv = (cut(1) for _ in range(3))
            n_ = lambda s: sem("m_" + s)
            MASK = 64
            front = lambda g, k: PS[:, 3 * (g % 2) + k, :]
            score = lambda k: PS[:, 3 + k % 2, :]
            turned = lambda k: PS[:, 5 + k % 2, :]
            read = lambda k: PS[:, 7, (k % 4) * D:(k % 4 + 1) * D]

            def wait(e, s, value):
                if value > 0:
                    e.wait_ge(n_(s), value)

            with nc.Block() as block:
                @block.vector
                def _(dve):
                    norm_stats_dve(dve, "m", stats, 1e-5)
                    dve.tensor_tensor(var, MV[:, :, 1], RS[:, :], ALU.mult).then_inc(n_("chain"), 1)
                    for g in range(NG):
                        normed(dve, g, X, hs[:, g * G:(g + 1) * G], RS, n_("hs"))
                        if g == 0:
                            dve.wait_ge(n_("chain"), 1)
                            dve.tensor_tensor(var, var, RS[:, :], ALU.mult).then_inc(n_("var"), 1)
                    dve.wait_ge(n_("lv"), 1)
                    dve.tensor_reduce(lsum, lv, AX_X, ALU.add).then_inc(n_("lsum"), 1)
                    for g in range(NG):
                        dve.wait_ge(n_("learned"), g + 1)
                        dve.tensor_scalar(lrn[:, g * GT:(g + 1) * GT], front(g, 1)[:, 0:GT],
                                          row("uncb2"), None, ALU.add).then_inc(n_("lrn"), 1)
                    dve.wait_ge(n_("lall"), 1)
                    dve.tensor_scalar(lall, PS[:, 6, 0:1], 1.0 / T, 1e-6, ALU.mult, ALU.add)\
                        .then_inc(n_("chain"), 1)
                    dve.wait_ge(n_("chain"), 2)
                    dve.reciprocal(linv, lall).then_inc(n_("chain"), 1)
                    dve.wait_ge(n_("chain"), 3)
                    dve.tensor_scalar(unc, lv, linv, 0.5, ALU.mult, ALU.mult).then_inc(n_("chain"), 1)
                    dve.wait_ge(n_("chain"), 4)
                    dve.wait_ge(n_("sig"), 1)
                    dve.scalar_tensor_tensor(out=unc, in0=sig, scalar=2.5, in1=unc, op0=ALU.mult, op1=ALU.add)\
                        .then_inc(n_("chain"), 1)
                    dve.wait_ge(n_("chain"), 5)
                    dve.tensor_scalar(unc, unc, 0.0, 5.0, ALU.max, ALU.min).then_inc(n_("unc"), 1)
                    dve.wait_ge(n_("gate"), 1)
                    dve.wait_ge(n_("xh"), NG)

                    def gated(k):
                        xs = X[:, k * D:(k + 1) * D]
                        dve.wait_ge(n_("agg"), k + 1)
                        dve.wait_ge(n_("coef"), k + 1)
                        dve.scalar_tensor_tensor(out=xs, in0=read(k), scalar=coef[k % 2], in1=xs,
                                                 op0=ALU.mult, op1=ALU.add).then_inc(n_("x"), 1)

                    def stats_of(k):
                        dve.wait_ge(n_("x"), k + 1)
                        dve.bn_stats(ST[:, 6 * k:6 * k + 6], X[:, k * D:(k + 1) * D]).then_inc(n_("stats"), 1)

                    for k in range(NT):
                        u = k % 2
                        dve.wait_ge(n_("sc"), k + 1)
                        dve.max(top[u], sc[u]).then_inc(n_("top"), 1)
                        if k >= 3:
                            stats_of(k - 3)
                        dve.wait_ge(n_("top"), k + 1)
                        dve.tensor_scalar(ntop[u], top[u][:, 0:1], -1.0, None, ALU.mult).then_inc(n_("ntop"), 1)
                        dve.match_replace(rep[u], top[u], sc[u], LOW).then_inc(n_("rep"), 1)
                        if k >= 2:
                            gated(k - 2)
                        dve.wait_ge(n_("rep"), k + 1)
                        dve.wait_ge(n_("ex"), k + 1)
                        dve.scalar_tensor_tensor(out=wt[u], in0=rep[u], scalar=LOW, in1=ex[u], op0=ALU.is_equal,
                                                 op1=ALU.mult, accum_out=den[u]).then_inc(n_("wt"), 1)
                        dve.wait_ge(n_("wt"), k + 1)
                        dve.reciprocal(rden[u], den[u]).then_inc(n_("rden"), 1)
                        dve.wait_ge(n_("rden"), k + 1)
                        dve.tensor_tensor(coef[u], rden[u], gate[:, k:k + 1], ALU.mult).then_inc(n_("coef"), 1)
                    for k in range(NT - 2, NT):
                        gated(k)
                    for k in range(NT - 3, NT):
                        stats_of(k)

                @block.gpsimd
                def _(pool):
                    pool.memset(rk[0:MASK + 1], 0.0).then_inc(n_("cleared"), 1)
                    pool.memset(rq[0:MASK + 1], 0.0).then_inc(n_("cleared"), 1)
                    pool.wait_ge(n_("cleared"), 2)
                    pool.memset(rq[MASK:MASK + 1], 1.0).then_inc(n_("cleared"), 1)
                    pool.wait_ge(n_("cleared"), 3)
                    for g in range(NG):
                        pool.wait_ge(n_("hs"), g + 1)
                        s_ = slice(g * G, (g + 1) * G)
                        pool.tensor_tensor(X[:, s_], X[:, s_], hs[:, s_], ALU.add).then_inc(n_("xh"), 1)

                @block.scalar
                def _(act):
                    norm_stats_act(act, "m")
                    act.wait_ge(n_("var"), 1)
                    act.activation(lv, var, ACT.Ln, bias=1.0).then_inc(n_("lv"), 1)
                    act.wait_ge(n_("cleared"), 3)
                    act.activation(rk[MASK:MASK + 1], row("mask")[MASK:MASK + 1], ACT.Copy)
                    act.wait_ge(n_("rkp"), 1)
                    act.activation(rk[0:RD], PS[0:RD, 7, :], ACT.Copy).then_inc(n_("rk"), 1)

                    def router_query(g):
                        act.wait_ge(n_("rqp"), g + 1)
                        act.activation(rq[0:RD, g * G:(g + 1) * G], front(g, 0)[0:RD], ACT.Copy,
                                       scale=float(1.0 / np.sqrt(RD))).then_inc(n_("rq"), 1)

                    for g in range(NG):
                        u = g % 2
                        act.wait_ge(n_("hsT"), g + 1)
                        act.activation(hT[u], front(g, 0), ACT.Copy).then_inc(n_("hT"), 1)
                        act.wait_ge(n_("qp"), g + 1)
                        act.activation(qu[u], front(g, 2), ACT.Copy).then_inc(n_("qu"), 1)
                        act.activation(h1[u][0:UNC], front(g, 1)[0:UNC], ACT.Gelu,
                                       bias=col("uncb1")[0:UNC]).then_inc(n_("h1"), 1)
                        if g:
                            router_query(g - 1)
                    router_query(NG - 1)
                    act.wait_ge(n_("lrn"), NG)
                    act.activation(sig, lrn, ACT.Sigmoid).then_inc(n_("sig"), 1)
                    act.wait_ge(n_("unc"), 1)
                    act.activation(gate, unc, ACT.Sigmoid, bias=row("gbias"), scale=row("gw1"))\
                        .then_inc(n_("gate"), 1)

                    def scores_out(k):
                        act.wait_ge(n_("scores"), k + 1)
                        wait(act, "wt", k - 1)
                        act.activation(sc[k % 2], score(k), ACT.Copy).then_inc(n_("sc"), 1)

                    def weights_out(k):
                        act.wait_ge(n_("wTp"), k + 1)
                        act.activation(wT[k % 2], turned(k), ACT.Copy).then_inc(n_("wT"), 1)

                    scores_out(0)
                    for k in range(NT):
                        if k + 1 < NT:
                            scores_out(k + 1)
                        act.wait_ge(n_("ntop"), k + 1)
                        act.activation(ex[k % 2], sc[k % 2], ACT.Exp, bias=ntop[k % 2]).then_inc(n_("ex"), 1)
                        if k:
                            weights_out(k - 1)
                    weights_out(NT - 1)

                @block.tensor
                def _(pe):
                    pe.wait_ge(sem("w2_loaded"), 16)
                    pe.matmul(PS[0:RD, 7, :], w("router"), w("keys"), start=True, stop=True)\
                        .then_inc(n_("rkp"), 1)

                    def back(g):
                        u = g % 2
                        pe.wait_ge(n_("qu"), g + 1)
                        pe.matmul(front(g, 0)[0:RD], w("router"), qu[u], start=True, stop=True)\
                            .then_inc(n_("rqp"), 1)
                        pe.wait_ge(n_("h1"), g + 1)
                        for t in range(GT):
                            last = pe.matmul(front(g, 1)[:, t:t + 1], h1[u][0:UNC, t * P:(t + 1) * P],
                                             w("unc2")[0:UNC], start=True, stop=True)
                        last.then_inc(n_("learned"), 1)

                    for g in range(NG):
                        u = g % 2
                        pe.wait_ge(n_("hs"), g + 1)
                        if g >= 2:
                            pe.wait_ge(n_("rq"), g - 1)
                        for t in range(GT):
                            k = g * GT + t
                            last = pe.transpose(front(g, 0)[:, t * P:(t + 1) * P], hs[:, k * D:(k + 1) * D],
                                                ident[:, :])
                        last.then_inc(n_("hsT"), 1)
                        pe.wait_ge(n_("hT"), g + 1)
                        if g >= 2:
                            pe.wait_ge(n_("lrn"), g - 1)
                        pe.matmul(front(g, 1)[0:UNC, :], w("unc1"), hT[u], start=True, stop=True)
                        pe.matmul(front(g, 2), w("qproj"), hT[u], start=True, stop=True).then_inc(n_("qp"), 1)
                        if g:
                            back(g - 1)
                    back(NG - 1)
                    pe.wait_ge(n_("lsum"), 1)
                    pe.matmul(PS[:, 6, 0:1], ONES[:, :], lsum, start=True, stop=True).then_inc(n_("lall"), 1)

                    def scores(k):
                        pe.wait_ge(n_("rq"), NG)
                        wait(pe, "sc", k - 1)
                        pe.matmul(score(k), rq[0:MASK + 1, k * P:(k + 1) * P], rk[0:MASK + 1],
                                  start=True, stop=True).then_inc(n_("scores"), 1)

                    def read_memory(k):
                        pe.wait_ge(n_("wT"), k + 1)
                        wait(pe, "x", k)
                        for c in range(HC):
                            last = pe.matmul(read(k), wT[k % 2][:, c * P:(c + 1) * P], w("values", c * D, D),
                                             start=(c == 0), stop=(c == HC - 1))
                        last.then_inc(n_("agg"), 1)

                    pe.wait_ge(n_("lrn"), NG)
                    pe.wait_ge(n_("rk"), 1)
                    scores(0)
                    scores(1)
                    pe.wait_ge(n_("chain"), 2)
                    for k in range(NT):
                        if k + 2 < NT:
                            scores(k + 2)
                        pe.wait_ge(n_("wt"), k + 1)
                        for c in range(HC):
                            last = pe.transpose(turned(k)[:, c * P:(c + 1) * P], wt[k % 2][:, c * P:(c + 1) * P],
                                                ident[:, :])
                        last.then_inc(n_("wTp"), 1)
                        if k:
                            read_memory(k - 1)
                    read_memory(NT - 1)

        def causal_attention(stats):
            at[0] = 0
            EH = DH + 1
            FW = H * EH * DH
            HB = [(0, 6), (6, 5), (11, 5)]
            hn = [cut(G) for _ in range(2)]
            hT = [cut(G) for _ in range(2)]
            hb = cut(NT * D)
            qk = cut(NT * 2 * D).rearrange("p (t c) -> p t c", t=NT)
            va = cut(NT * H * EH).rearrange("p (t h e) -> p t h e", t=NT, h=H)
            outer = [cut(FW) for _ in range(4)]
            prod = [cut(FW) for _ in range(2)]
            nd = [cut(H * EH).rearrange("p (h e) -> p h e", h=H) for _ in range(2)]
            rec = [cut(H) for _ in range(2)]
            att = [cut(D) for _ in range(2)]
            aT = [cut(D) for _ in range(2)]
            n_ = lambda s: sem("a1_" + s)
            qkv = lambda k: PS[:, 2 + k % 6, 0:3 * D]
            sums = lambda k, c: PS[:, 3 * (k % 2) + c, :]

            def heads(ap, h0, n):
                return ap[:, h0 * DH:(h0 + n) * DH].rearrange("p (h m) -> p h m", m=DH)

            def wait(e, s, value):
                if value > 0:
                    e.wait_ge(n_(s), value)

            with nc.Block() as block:
                @block.vector
                def _(dve):
                    norm_stats_dve(dve, "a1", stats, 1e-5, 1e-6)
                    normed(dve, 0, X, hn[0], RS2, n_("hn"))
                    normed(dve, 1, X, hn[1], RS2, n_("hn"))
                    dve.memset(va[:, :, :, DH:EH], 1.0).then_inc(n_("ones"), 1)
                    for g in range(NG):
                        for k in range(g * GT, (g + 1) * GT):
                            dve.wait_ge(n_("qkv"), k + 1)
                            dve.tensor_scalar(qk[:, k, :], qkv(k)[:, 0:2 * D], 0.0, 1e-3, ALU.max, ALU.add)\
                                .then_inc(n_("phi"), 1)
                        if g + 2 < NG:
                            normed(dve, g + 2, X, hn[g % 2], RS2, n_("hn"))
                    for g in range(NG):
                        normed(dve, g, X, hb[:, g * G:(g + 1) * G], RS, n_("hb"))

                    def residual(k):
                        dve.wait_ge(n_("proj"), k + 1)
                        dve.wait_ge(n_("hb"), k // GT + 1)
                        dve.tensor_tensor(XX[:, k * D:(k + 1) * D], PS[:, 7, 0:D], hb[:, k * D:(k + 1) * D],
                                          ALU.add).then_inc(n_("xx"), 1)

                    def stats_of(k):
                        dve.wait_ge(n_("xx"), k + 1)
                        dve.bn_stats(ST[:, 6 * k:6 * k + 6], XX[:, k * D:(k + 1) * D]).then_inc(n_("stats"), 1)

                    for k in range(NT):
                        u = k % 2
                        dve.wait_ge(n_("cum"), k + 1)
                        for c, (h0, n) in enumerate(HB):
                            last = dve.tensor_tensor(
                                prod[u][:, h0 * EH * DH:(h0 + n) * EH * DH]
                                .rearrange("p (h e m) -> p h e m", e=EH, m=DH),
                                sums(k, c)[:, 0:n * EH * DH].rearrange("p (h e m) -> p h e m", e=EH, m=DH),
                                over(heads(qk[:, k, 0:D], h0, n), EH, 2), ALU.mult)
                        last.then_inc(n_("prod"), 1)
                        if k >= 2:
                            residual(k - 2)
                        dve.wait_ge(n_("prod"), k + 1)
                        dve.tensor_reduce(nd[u].rearrange("p h e -> p (h e)"),
                                          prod[u].rearrange("p (c m) -> p c m", m=DH), AX_X, ALU.add)\
                            .then_inc(n_("nd"), 1)
                        if k >= 2:
                            stats_of(k - 2)
                        dve.wait_ge(n_("nd"), k + 1)
                        dve.reciprocal(rec[u], nd[u][:, :, DH]).then_inc(n_("rec"), 1)
                        dve.wait_ge(n_("rec"), k + 1)
                        dve.tensor_tensor(att[u].rearrange("p (h e) -> p h e", e=DH), nd[u][:, :, 0:DH],
                                          over(rec[u], DH, 2), ALU.mult).then_inc(n_("att"), 1)
                    for k in range(NT - 2, NT):
                        residual(k)
                        stats_of(k)

                @block.gpsimd
                def _(pool):
                    pool.wait_ge(n_("ones"), 1)
                    for k in range(NT):
                        pool.wait_ge(n_("phi"), k + 1)
                        pool.wait_ge(n_("values"), k + 1)
                        wait(pool, "cum", k - 2 - k % 2)
                        pool.tensor_tensor(
                            outer[k % 4].rearrange("p (h e m) -> p h e m", e=EH, m=DH),
                            over(heads(qk[:, k, D:2 * D], 0, H), EH, 2),
                            over(va[:, k], DH, 3), ALU.mult).then_inc(n_("outer"), 1)

                @block.scalar
                def _(act):
                    norm_stats_act(act, "a1", 1e-6)

                    def transposed(g):
                        act.wait_ge(n_("hnT"), g + 1)
                        wait(act, "qkv", (g - 1) * GT)
                        act.activation(hT[g % 2], PS[:, g % 2, :], ACT.Identity, bias=col("b1_1"),
                                       scale=col("g1_1")).then_inc(n_("hT"), 1)

                    transposed(0)
                    transposed(1)
                    for g in range(NG):
                        for k in range(g * GT, (g + 1) * GT):
                            act.wait_ge(n_("qkv"), k + 1)
                            act.wait_ge(n_("phi"), k + 1)
                            act.activation(va[:, k, :, 0:DH], qkv(k)[:, 2 * D:3 * D]
                                           .rearrange("p (h e) -> p h e", h=H), ACT.Copy).then_inc(n_("values"), 1)
                        if g + 2 < NG:
                            transposed(g + 2)
                    for k in range(NT):
                        act.wait_ge(n_("attT"), k + 1)
                        act.activation(aT[k % 2], PS[:, 6, 0:P], ACT.Copy).then_inc(n_("aT"), 1)

                @block.tensor
                def _(pe):
                    def transposes(g):
                        pe.wait_ge(n_("hn"), g + 1)
                        for t in range(GT):
                            last = pe.transpose(PS[:, g % 2, t * P:(t + 1) * P], hn[g % 2][:, t * D:(t + 1) * D],
                                                ident[:, :])
                        last.then_inc(n_("hnT"), 1)

                    pe.wait_ge(sem("w3_loaded"), 16)
                    transposes(0)
                    transposes(1)
                    for g in range(NG):
                        pe.wait_ge(n_("hT"), g + 1)
                        for t in range(GT):
                            k = g * GT + t
                            wait(pe, "values", k - 5)
                            pe.matmul(qkv(k), hT[g % 2][:, t * P:(t + 1) * P], w("qkv1"), start=True, stop=True)\
                                .then_inc(n_("qkv"), 1)
                        if g + 2 < NG:
                            transposes(g + 2)

                    def transposed_result(k):
                        pe.wait_ge(n_("att"), k + 1)
                        wait(pe, "aT", k)
                        pe.transpose(PS[:, 6, 0:P], att[k % 2], ident[:, :]).then_inc(n_("attT"), 1)

                    def projection(k):
                        pe.wait_ge(n_("aT"), k + 1)
                        wait(pe, "xx", k)
                        pe.matmul(PS[:, 7, 0:D], aT[k % 2], w("wo1"), start=True, stop=True).then_inc(n_("proj"), 1)

                    pe.wait_ge(n_("values"), NT)
                    for k in range(NT):
                        pe.wait_ge(n_("outer"), k + 1)
                        wait(pe, "prod", k - 1)
                        for c, (h0, n) in enumerate(HB):
                            a, b = h0 * EH * DH, (h0 + n) * EH * DH
                            if k % 2:
                                pe.matmul(sums(k, c)[:, 0:b - a], ONES[:, :], outer[(k - 1) % 4][:, a:b], start=True,
                                          stop=False)
                            last = pe.matmul(sums(k, c)[:, 0:b - a], TRI[:, :], outer[k % 4][:, a:b],
                                             start=(k % 2 == 0), stop=True)
                        last.then_inc(n_("cum"), 1)
                        if k >= 2:
                            projection(k - 2)
                        if k >= 1:
                            transposed_result(k - 1)
                    projection(NT - 2)
                    transposed_result(NT - 1)
                    projection(NT - 1)

        def experts(stats):
            at[0] = 0
            HT = cut(T)
            cwT = [cut(T, BF16) for _ in range(2)]
            SEL = cut(EP // 2 * P, BF16)
            hn = [cut(G) for _ in range(2)]
            hT = [cut(G) for _ in range(2)]
            aff = [cut(GT * E) for _ in range(2)]
            rep = [cut(GT * E) for _ in range(2)]
            sg = [cut(GT * E) for _ in range(2)]
            cw = [cut(GT * E) for _ in range(2)]
            rm = [cut(GT * E) for _ in range(2)]
            top = [cut(GT * 8) for _ in range(2)]
            wsum = [cut(GT) for _ in range(2)]
            rsum = [cut(GT) for _ in range(2)]
            EH = E // 2
            cp = [cut(GT * 2 * 3 * EH, BF16).rearrange("p (t f c) -> p t f c", t=GT, f=2) for _ in range(2)]
            part = lambda u, a: cp[u][:, :, :, a * EH:(a + 1) * EH]
            halves = lambda m: m.rearrange("p (t f j) -> p t f j", t=GT, f=2)
            v = lambda i, u: 2 * i + u + 1
            n_ = lambda s: sem("e_" + s)
            bankb = lambda u, k: bank(u, k).bitcast(BF16)

            with nc.Block() as block:
                @block.vector
                def _(dve):
                    norm_stats_dve(dve, "e", stats, 1e-5)
                    for i in range(0, NG // 2):
                        for u in range(2):
                            normalise(dve, i, u, X, hn[u], RS, n_("hn"))
                        for u in range(2):
                            dve.wait_ge(n_("sg"), v(i, u))
                            dve.tensor_tensor(tiles(aff[u]), tiles(bank(u, 1)[:, 0:GT * E]), over(row("eb"), GT),
                                              ALU.add).then_inc(n_("biased"), 1)
                        for u in range(2):
                            dve.wait_ge(n_("biased"), v(i, u))
                            for t in range(GT):
                                last = dve.max(top[u][:, 8 * t:8 * t + 8], aff[u][:, t * E:(t + 1) * E])
                            last.then_inc(n_("top"), 1)
                        for u in range(2):
                            dve.wait_ge(n_("top"), v(i, u))
                            for t in range(GT):
                                last = dve.match_replace(rep[u][:, t * E:(t + 1) * E], top[u][:, 8 * t:8 * t + 8],
                                                         aff[u][:, t * E:(t + 1) * E], LOW)
                            last.then_inc(n_("rep"), 1)
                        for u in range(2):
                            dve.wait_ge(n_("rep"), v(i, u))
                            for t in range(GT):
                                s_ = slice(t * E, (t + 1) * E)
                                last = dve.scalar_tensor_tensor(out=rm[u][:, s_], in0=rep[u][:, s_], scalar=LOW,
                                                                in1=sg[u][:, s_], op0=ALU.is_equal, op1=ALU.mult,
                                                                accum_out=wsum[u][:, t:t + 1])
                            last.then_inc(n_("wsum"), 1)
                        for u in range(2):
                            dve.wait_ge(n_("wsum"), v(i, u))
                            dve.tensor_scalar(wsum[u], wsum[u], 1e-8, None, ALU.add).then_inc(n_("wse"), 1)
                            dve.wait_ge(n_("wse"), v(i, u))
                            dve.reciprocal(rsum[u], wsum[u]).then_inc(n_("rsum"), 1)
                            dve.wait_ge(n_("rsum"), v(i, u))
                            dve.tensor_tensor(tiles(cw[u]), tiles(rm[u]), over(rsum[u], E, 2), ALU.mult)\
                                .then_inc(n_("cw"), 1)
                        for u in range(2):
                            dve.wait_ge(n_("cw"), v(i, u))
                            dve.tensor_copy(part(u, 0), halves(cw[u])).then_inc(n_("c1"), 1)
                        for u in range(2):
                            dve.wait_ge(n_("c1"), v(i, u))
                            dve.tensor_tensor(halves(rm[u]), halves(cw[u]), part(u, 0), ALU.subtract)\
                                .then_inc(n_("r1"), 1)
                        for u in range(2):
                            dve.wait_ge(n_("r1"), v(i, u))
                            dve.tensor_copy(part(u, 1), halves(rm[u])).then_inc(n_("c2"), 1)
                        for u in range(2):
                            dve.wait_ge(n_("c2"), v(i, u))
                            dve.tensor_tensor(part(u, 2), halves(rm[u]), part(u, 1), ALU.subtract)\
                                .then_inc(n_("c3"), 1)

                @block.gpsimd
                def _(pool):
                    pool.memset(SEL, 0.0).then_inc(n_("sel"), 1)
                    for a in range(3):
                        pool.wait_ge(n_("sel"), a + 1)
                        s_ = SEL.rearrange("p (k f m) -> p k f m", f=2, m=F)
                        pool.affine_select(out=s_, in_=s_, compare_op=ALU.not_equal, fill=1.0, base=-EH * a,
                                           pattern=[[-2, EP // 2], [-1, 2], [0, F]], channel_multiplier=1)\
                            .then_inc(n_("sel"), 1)
                    for i in range(0, NG // 2):
                        for u in range(2):
                            pool.wait_ge(n_("hT"), v(i, u))
                            pool.tensor_copy(HT[:, bass.ds((2 * i + u) * G, G)], hT[u]).then_inc(n_("HT"), 1)

                @block.scalar
                def _(act):
                    norm_stats_act(act, "e")
                    for i in range(0, NG // 2):
                        for u in range(2):
                            act.wait_ge(n_("hnT"), v(i, u))
                            act.wait_ge(n_("HT_free"), v(i, u))
                            act.activation(hT[u], bank(u, 0), ACT.Copy).then_inc(n_("hT"), 1)
                        for u in range(2):
                            act.wait_ge(n_("affp"), v(i, u))
                            act.activation(sg[u], bank(u, 1)[:, 0:GT * E], ACT.Sigmoid).then_inc(n_("sg"), 1)
                        for u in range(2):
                            act.wait_ge(n_("cwTp"), v(i, u))
                            for a in range(2):
                                last = act.activation(cwT[a][0:3 * EH, bass.ds((2 * i + u) * G, G)],
                                                      bankb(u, 2 + a)[0:3 * EH, 0:G], ACT.Copy)
                            last.then_inc(n_("cwT"), 1)

                @block.sync
                def _(sp):
                    sp.sem_inc(n_("HT_free"), 2)
                    for i in range(0, NG // 2):
                        for u in range(2):
                            sp.wait_ge(n_("HT"), v(i, u))
                            sp.sem_inc(n_("HT_free"), 1)

                @block.tensor
                def _(pe):
                    for i in range(0, NG // 2):
                        for u in range(2):
                            pe.wait_ge(n_("hn"), v(i, u))
                            for t in range(GT):
                                last = pe.transpose(bank(u, 0)[:, t * P:(t + 1) * P], hn[u][:, t * D:(t + 1) * D],
                                                    ident[:, :])
                            last.then_inc(n_("hnT"), 1)
                        for u in range(2):
                            pe.wait_ge(n_("hT"), v(i, u))
                            for t in range(GT):
                                last = pe.matmul(bank(u, 1)[:, t * E:(t + 1) * E], hT[u][:, t * P:(t + 1) * P],
                                                 w("cent"), start=True, stop=True)
                            last.then_inc(n_("affp"), 1)
                        for u in range(2):
                            pe.wait_ge(n_("c3"), v(i, u))
                            for a in range(2):
                                for t in range(GT):
                                    last = pe.transpose(bankb(u, 2 + a)[0:3 * EH, t * P:(t + 1) * P],
                                                        cp[u][:, t, a, :], identb[:, :])
                            last.then_inc(n_("cwTp"), 1)

            at[0] = T + T + EP // 2 * P // 2
            WU = [cut(P) for _ in range(2)]
            WD = [cut(P) for _ in range(2)]
            si = [cut(G) for _ in range(2)]
            hw = [cut(G) for _ in range(2)]
            res = cut(T)
            m_ = lambda s: sem("g_" + s)
            acc = lambda c: PS[:, c, :]

            def chunk(ap, c):
                return ap[:, c * G:(c + 1) * G]

            def count(k, c, add=1):
                return GT * k + c + 4 + add

            with nc.Block() as block:
                @block.sync
                def _(sp):
                    def load(k, par):
                        s = bass.ds(k * P, P)
                        sp.dma_start(WU[par], wup[:, s]).then_inc(m_(f"w{par}"), 16)
                        sp.dma_start(WD[par], wdown[:, s]).then_inc(m_(f"w{par}"), 16)

                    load(0, 0)
                    load(1, 1)
                    with sp.Fori(0, EP // 2 - 1) as i:
                        for par in range(2):
                            sp.wait_ge(m_("down"), count(2 * i + par, 3))
                            load(2 * i + 2 + par, par)
                    for c in range(NG):
                        sp.wait_ge(m_("res"), c + 1)
                        sp.dma_start(out[:, c * G:(c + 1) * G], chunk(res, c)).then_inc(sem("out_stored"), 16)
                    sp.wait_ge(sem("out_stored"), 16 * NG)

                @block.scalar
                def _(act):
                    def silu(cnt, c, rows_=P):
                        act.wait_ge(m_("up"), cnt)
                        act.activation(si[c % 2][0:rows_], PS[0:rows_, 4 + c % 2, :], ACT.Silu)\
                            .then_inc(m_("si"), 1)

                    for c in range(NG):
                        if c >= 2:
                            act.wait_ge(m_("hw"), c - 1)
                        silu(c + 1, c, F)
                    with act.Fori(0, EP) as k:
                        for c in range(NG):
                            act.wait_ge(m_("hw"), count(k, c, -1))
                            silu(count(k, c), c)
                    for c in range(NG):
                        act.wait_ge(m_("down"), count(EP - 1, c))
                        act.activation(chunk(res, c), acc(c), ACT.Copy).then_inc(m_("res"), 1)

                @block.vector
                def _(dve):
                    for c in range(NG):
                        dve.wait_ge(m_("si"), c + 1)
                        if c >= 2:
                            dve.wait_ge(m_("down"), c - 1)
                        dve.tensor_copy(hw[c % 2][0:F], si[c % 2][0:F]).then_inc(m_("hw"), 1)
                    with dve.Fori(0, EP) as k:
                        for c in range(NG):
                            dve.wait_ge(m_("si"), count(k, c))
                            dve.wait_ge(m_("cwb"), GT * k + c + 1)
                            dve.wait_ge(m_("down"), count(k, c, -1))
                            dve.tensor_tensor(hw[c % 2], PS[:, 6 + c % 2, :], si[c % 2], ALU.mult)\
                                .then_inc(m_("hw"), 1)

                @block.tensor
                def _(pe):
                    for t in range(NT):
                        pe.matmul(acc(t // GT)[:, (t % GT) * P:(t % GT + 1) * P], X[:, t * D:(t + 1) * D],
                                  ident[:, :], start=(t % GT == 0), stop=True, skip_group_check=True)

                    def down(cnt, c, lhs, rows_=P):
                        pe.wait_ge(m_("hw"), cnt)
                        pe.matmul(acc(c), lhs, hw[c % 2][0:rows_], start=False, stop=True, skip_group_check=True)\
                            .then_inc(m_("down"), 1)

                    for c in range(NG):
                        if c >= 2:
                            pe.wait_ge(m_("si"), c - 1)
                        pe.matmul(PS[0:F, 4 + c % 2, :], w("sup"), chunk(HT, c), start=True, stop=True)\
                            .then_inc(m_("up"), 1)
                        if c:
                            down(c, c - 1, w("sdown")[0:F], F)

                    def pair(k, half, par, before):
                        pe.wait_ge(m_(f"w{par}"), 32 * ((k - par) // 2 + 1) if isinstance(k, int)
                                   else 16 * (k + (2 - par)))
                        for c in range(NG):
                            pe.wait_ge(m_("si"), count(k, c, -1))
                            pe.matmul(PS[:, 4 + c % 2, :], WU[par], chunk(HT, c), start=True, stop=True)\
                                .then_inc(m_("up"), 1)
                            pe.wait_ge(m_("hw"), count(k, c, -1))
                            pe.matmul(PS[:, 6 + c % 2, :], SEL[0:3 * EH, bass.ds((k - half * (EP // 2)) * P, P)],
                                      chunk(cwT[half], c)[0:3 * EH], start=True, stop=True).then_inc(m_("cwb"), 1)
                            if c:
                                down(count(k, c - 1), c - 1, WD[par])
                            else:
                                down(count(k, 0, 0), NG - 1, *before)

                    pair(0, 0, 0, (w("sdown")[0:F], F))
                    pair(1, 0, 1, (WD[0],))
                    for half in range(2):
                        with pe.Fori(1 - half, EP // 4) as i:
                            for par in range(2):
                                pair(half * (EP // 2) + 2 * i + par, half, par, (WD[1 - par],))
                    down(count(EP, 0, 0), NG - 1, WD[1])

        set_up()
        phase(linear_attention)
        phase(feed_forward, 0, ACT.Gelu, 1e-5, "a0_stats")
        phase(cross_prepare, 0, "f0_stats")
        phase(cross_attend, 0)
        phase(memory_read, "y0_stats")
        phase(causal_attention, "m_stats")
        phase(feed_forward, 1, ACT.Gelu_apprx_tanh, 1e-6, "a1_stats")
        phase(cross_prepare, 1, "f1_stats")
        phase(cross_attend, 1)
        experts("y1_stats")


def layout(inputs):
    a = {k: np.asarray(v) for k, v in inputs.items()}
    f = np.float32
    hd = np.arange(D).reshape(4, 4, DH).transpose(1, 0, 2).reshape(-1)
    dh = hd.reshape(H, DH).T.reshape(-1)

    def pad(m):
        return m if m.shape[0] == P else np.concatenate([m, np.zeros((P - m.shape[0], m.shape[1]), f)], 0)

    def chunks(m):
        return m.reshape(-1, P, m.shape[1]).transpose(1, 0, 2).reshape(P, -1)

    mats = {
        "qkv0": a["L0_attn_qkv_w"].T, "proj0": a["L0_attn_proj_w"].T, "fc1_0": a["L0_attn_fc1_w"].T,
        "fc2_0": chunks(a["L0_attn_fc2_w"].T),
        "xq0": a["L0_xattn_Wq"].T[:, dh], "xk0": a["L0_xattn_Wk"].T[:, dh], "xv0": a["L0_xattn_Wv"].T[:, hd],
        "xo0": a["L0_xattn_Wo"].T[hd],
        "qproj": a["L0_ffn_q_proj_w"].T, "router": a["L0_ffn_router_w"].T, "keys": a["L0_ffn_aux_keys"].T,
        "values": chunks(a["L0_ffn_aux_values"]), "unc1": a["L0_ffn_unc_w1"].T, "unc2": pad(a["L0_ffn_unc_w2"].T),
        "qkv1": np.concatenate([a[f"L1_attn_w{c}"].reshape(D, D) for c in "qkv"], 1),
        "wo1": a["L1_attn_wo"].reshape(D, D), "fc1_1": a["L1_attn_w1"], "fc2_1": chunks(a["L1_attn_w2"]),
        "xq1": a["L1_xattn_wq"].T[:, dh], "xk1": a["L1_xattn_wk"].T[:, dh], "xv1": a["L1_xattn_wv"].T[:, hd],
        "xo1": a["L1_xattn_wo"].T[hd],
        "cent": a["L1_ffn_centroids"].T, "sup": a["L1_ffn_Ws_up"], "sdown": pad(a["L1_ffn_Ws_down"]),
    }
    vecs = {
        "g1_0": a["L0_attn_norm1_g"], "b1_0": a["L0_attn_norm1_b"], "g2_0": a["L0_attn_norm2_g"],
        "b2_0": a["L0_attn_norm2_b"], "fcb_0": a["L0_attn_fc1_b"], "bq0": a["L0_xattn_bq"][dh],
        "bk0": a["L0_xattn_bk"][dh], "bq1": a["L1_xattn_bq"][dh], "bk1": a["L1_xattn_bk"][dh],
        "uncb1": np.concatenate([a["L0_ffn_unc_b1"], np.zeros(P - UNC, f)]),
        "g1_1": a["L1_attn_ln1_scale"], "b1_1": a["L1_attn_ln1_bias"], "g2_1": a["L1_attn_ln2_scale"],
        "b2_1": a["L1_attn_ln2_bias"], "fcb_1": a["L1_attn_b1"],
    }
    flat = {
        "projb": a["L0_attn_proj_b"], "fc2b_0": a["L0_attn_fc2_b"], "bv0": a["L0_xattn_bv"][hd],
        "bo0": a["L0_xattn_bo"], "fc2b_1": a["L1_attn_b2"], "bv1": a["L1_xattn_bv"][hd], "bo1": a["L1_xattn_bo"],
        "mask": a["L0_ffn_reliability_mask"], "eb": a["L1_ffn_expert_biases"], "uncb2": a["L0_ffn_unc_b2"],
        "gw1": a["L0_ffn_gate_w1"], "gbias": a["L0_ffn_gate_bias"], "decay": a["L1_xattn_time_decay"],
    }
    c = np.ascontiguousarray
    return {
        "x": c(a["x"].reshape(T, D)),
        "ctxT": c(a["ctx_1024"].reshape(T, D).T),
        "wts": c(np.concatenate([mats[n] for n, _ in _W], 1)),
        "cols": c(np.concatenate([vecs[n].reshape(-1, P).T for n, _ in _C], 1)),
        "rows": c(np.broadcast_to(np.concatenate([flat[n].reshape(-1) for n, _ in _R])[None], (P, NR))),
        "positions": position_rows(),
        "wup": c(a["L1_ffn_W_up"].transpose(1, 0, 2).reshape(D, E * F)),
        "wdown": c(a["L1_ffn_W_down"].reshape(EP, P, D).transpose(1, 0, 2).reshape(P, EP * D)),
    }


def position_rows():
    q = np.arange(S)
    late, early = (q >= P).astype(np.float32), (q < P).astype(np.float32)
    zero = np.zeros(S, np.float32)
    rows = []
    for queries, keys, sign in ((late, early, 1), (early, late, -1)):
        rows += [(sign * q * queries, zero, zero, keys, part) for part in range(3)]
        rows += [(zero, queries, -sign * q * keys, zero, part) for part in range(3)]
    return np.stack([np.concatenate([*r[:4], np.eye(3)[r[4]]]) for r in rows]).astype(np.float32)


def program(nc, arrays):
    args = [nc.dram_tensor(f"in_{n}", a.shape, mybir.dt.from_np(a.dtype), kind="ExternalInput").ap()
            for n, a in arrays.items()]
    scratch = [nc.dram_tensor(f"parts{n}", (B, 2, 3, P, S), BF16, kind="Internal").ap() for n in range(2)]
    out = nc.dram_tensor("out_x", (D, T), F32, kind="ExternalOutput").ap()
    nc.disable_value_cache = True
    build(nc, *args, scratch, out)


def kernel(**inputs):
    import concourse.bacc as bacc
    from concourse.bass_utils import run_bass_kernel_spmd as run
    arrays = layout(inputs)
    nc = bacc.Bacc("TRN2", target_bir_lowering=False, num_devices=1)
    program(nc, arrays)
    r = run(nc, [{f"in_{n}": a for n, a in arrays.items()}], core_ids=[0])
    return np.ascontiguousarray(r.results[0]["out_x"].T).reshape(B, S, D)
```

```python
from contextlib import ExitStack

import numpy as np
import concourse.bass as bass
from concourse import mybir

ALU = mybir.AluOpType
ACT = mybir.ActivationFunctionType
AX_X = mybir.AxisListType.X
F32 = mybir.dt.float32
BF16 = mybir.dt.bfloat16
I32 = mybir.dt.int32

P = 128
D = 128
B, S = 8, 256
T = B * S
NT = T // P
H, DH = 16, 8
GT = 4
G = GT * P
NG = NT // GT
HID = 512
HC = HID // P
NMEM, RD = 512, 48
UNC = D // 4
E, F = 64, 64
EP = E // 2
BIG = 1.0e30
LOW = -3.0e38
MINUS_ONES = float(np.array([0xBF80BF80], np.uint32).view(np.float32)[0])
SCRATCH = 31900

_W = [
    ("qkv0", 3 * D), ("proj0", D), ("fc1_0", HID), ("fc2_0", HID),
    ("xq0", D), ("xk0", D), ("xv0", D), ("xo0", D),
    ("qproj", D), ("router", RD), ("keys", NMEM), ("values", HC * D), ("unc1", UNC), ("unc2", 1),
    ("qkv1", 3 * D), ("wo1", D), ("fc1_1", HID), ("fc2_1", HID),
    ("xq1", D), ("xk1", D), ("xv1", D), ("xo1", D),
    ("cent", E), ("sup", F), ("sdown", D),
]
_C = [
    ("g1_0", 1), ("b1_0", 1), ("g2_0", 1), ("b2_0", 1), ("fcb_0", HC),
    ("bq0", 1), ("bk0", 1), ("bq1", 1), ("bk1", 1), ("uncb1", 1),
    ("g1_1", 1), ("b1_1", 1), ("g2_1", 1), ("b2_1", 1), ("fcb_1", HC),
]
_R = [
    ("projb", D), ("fc2b_0", D), ("bv0", D), ("bo0", D), ("fc2b_1", D), ("bv1", D), ("bo1", D),
    ("mask", NMEM), ("eb", E), ("uncb2", 1), ("gw1", 1), ("gbias", 1), ("decay", 1),
]


def _spans(items):
    at, out = 0, {}
    for name, n in items:
        out[name] = (at, at + n)
        at += n
    return out, at


W_AT, NW = _spans(_W)
C_AT, NC_ = _spans(_C)
R_AT, NR = _spans(_R)
W_LOADS = [("qkv0", "xq0"), ("xq0", "qproj"), ("qproj", "qkv1"), ("qkv1", "xq1"), ("xq1", None)]
SCALE = float(np.float32(DH) ** np.float32(-0.5))


def build(nc, x, ctxT, wts, cols, rows, positions, wup, wdown, scratch, out):
    with ExitStack() as ctx:
        def sb(name, shape, dt=F32):
            return ctx.enter_context(nc.sbuf_tensor(name, shape, dt))

        sems, given = {}, []

        def sem(name):
            if name not in sems:
                given.append(name)
                sems[name] = nc.alloc_semaphore(name if given.count(name) == 1 else f"{name}_{given.count(name)}")
            return sems[name]

        def phase(run, *args):
            result = run(*args)
            own = [n for n in sems if not n.endswith(("_loaded", "_stored", "_stats"))]
            nc.clear_and_free_semaphores([sems.pop(n) for n in own])
            nc.all_engine_barrier()
            return result

        X = sb("X", [P, NT * D])
        W = sb("W", [P, NW])
        CO = sb("CO", [P, NC_])
        RO = sb("RO", [P, NR])
        VA = sb("VA", [P, NT * 512])
        XX = VA[:, 0:NT * D]
        ident = sb("ident", [P, P])
        identb = sb("identb", [P, P], BF16)
        ST = sb("ST", [P, NT * 6])
        MV = sb("MV", [P, NT, 2])
        SD = sb("SD", [P, NT])
        RS = sb("RS", [P, NT])
        SD2 = sb("SD2", [P, NT])
        RS2 = sb("RS2", [P, NT])
        AR = sb("AR", [P, SCRATCH])
        PS = ctx.enter_context(nc.psum_tensor("PS", [P, 8, 512], F32))

        at = [0]

        def cut(n, dt=F32):
            words = n if dt == F32 else (n + 1) // 2
            v = AR[:, at[0]:at[0] + words]
            at[0] += words
            assert at[0] <= SCRATCH
            return v if dt == F32 else v.bitcast(dt)

        def w(name, a=0, n=None):
            s, e = W_AT[name]
            return W[:, s + a:(e if n is None else s + a + n)]

        def col(name, k=0):
            return CO[:, C_AT[name][0] + k:C_AT[name][0] + k + 1]

        def row(name, k=0):
            s, e = R_AT[name]
            return RO[:, s:e]

        def tiles(ap, n=GT):
            return ap.rearrange("p (t d) -> p t d", t=n)

        def over(ap, n, axis=1):
            v = ap.unsqueeze(axis)
            shape = list(v.shape)
            shape[axis] = n
            return v.broadcast_to(shape)

        TRI = sb("TRI", [P, P])
        ONES = sb("ONES", [P, P])
        HM = sb("HM", [P, H])
        BM = sb("BM", [P, P])

        CONST = 5

        def set_up():
            with nc.Block() as block:
                @block.sync
                def _(sp):
                    for g in range(NG):
                        sp.dma_start(X[:, g * G:(g + 1) * G].rearrange("p (t d) -> p t d", t=GT),
                                     x[g * G:(g + 1) * G, :].rearrange("(t p) d -> p t d", p=P))\
                            .then_inc(sem(f"x{g}_loaded"), 16)
                    sp.dma_start(CO[:, :], cols).then_inc(sem("cols_loaded"), 16)
                    sp.dma_start(RO[:, :], rows).then_inc(sem("rows_loaded"), 16)
                    for k, (a, b) in enumerate(W_LOADS):
                        lo, hi = W_AT[a][0], (W_AT[b][0] if b else NW)
                        sp.dma_start(W[:, lo:hi], wts[:, lo:hi]).then_inc(sem(f"w{k}_loaded"), 16)

                @block.gpsimd
                def _(pool):
                    c = sem("const_filled")
                    d = sem("const_ready")
                    pool.memset(ident[:, :], 0.0).then_inc(c, 1)
                    pool.memset(identb[:, :], 0.0).then_inc(c, 1)
                    pool.memset(TRI[:, :], 1.0).then_inc(c, 1)
                    pool.memset(ONES[:, :], 1.0).then_inc(d, 1)
                    pool.memset(HM[:, :], 1.0).then_inc(c, 1)
                    pool.wait_ge(c, 4)
                    for m in (ident, identb):
                        pool.affine_select(out=m[:, :], in_=m[:, :], compare_op=ALU.not_equal, fill=1.0, base=0,
                                           pattern=[[-1, P]], channel_multiplier=1).then_inc(d, 1)
                    pool.affine_select(out=TRI[:, :], in_=TRI[:, :], compare_op=ALU.is_ge, fill=0.0, base=0,
                                       pattern=[[1, P]], channel_multiplier=-1).then_inc(d, 1)
                    pool.affine_select(out=HM[:, :], in_=HM[:, :], compare_op=ALU.is_ge, fill=0.0, base=0,
                                       pattern=[[-DH, H]], channel_multiplier=1).then_inc(c, 1)
                    pool.wait_ge(c, 5)
                    pool.affine_select(out=HM[:, :], in_=HM[:, :], compare_op=ALU.is_ge, fill=0.0, base=DH - 1,
                                       pattern=[[DH, H]], channel_multiplier=-1).then_inc(c, 1)
                    pool.wait_ge(c, 6)
                    pool.tensor_copy(BM[:, :].rearrange("p (h e) -> p h e", h=H),
                                     over(HM[:, :], DH, 2)).then_inc(d, 1)

                @block.vector
                def _(dve):
                    for g in range(NG):
                        dve.wait_ge(sem(f"x{g}_loaded"), 16)
                        for t in range(g * GT, (g + 1) * GT):
                            dve.bn_stats(ST[:, 6 * t:6 * t + 6], X[:, t * D:(t + 1) * D]).then_inc(sem("stats0"), 1)


        def norm_stats_dve(dve, tag, stats, eps, eps2=None):
            n_ = lambda s: sem(f"{tag}_{s}")
            dve.wait_ge(sem(stats), NT)
            for t in range(NT):
                i = dve.bn_aggr(MV[:, t, :], ST[:, 6 * t:6 * t + 6])
            i.then_inc(n_("mv"), 1)
            dve.wait_ge(n_("mv"), 1)
            dve.tensor_scalar(SD[:, :], MV[:, :, 1], eps, None, ALU.add).then_inc(n_("ve"), 1)
            dve.wait_ge(n_("sd"), 1)
            dve.reciprocal(RS[:, :], SD[:, :]).then_inc(n_("rs"), 1)
            dve.wait_ge(n_("rs"), 1)
            if eps2 is None:
                return
            dve.tensor_tensor(SD2[:, :], MV[:, :, 1], RS[:, :], ALU.mult).then_inc(n_("v2"), 1)
            dve.wait_ge(n_("v2"), 1)
            dve.tensor_tensor(SD2[:, :], SD2[:, :], RS[:, :], ALU.mult).then_inc(n_("v2"), 1)
            dve.wait_ge(n_("v2"), 2)
            dve.tensor_scalar(SD2[:, :], SD2[:, :], eps2, None, ALU.add).then_inc(n_("v2"), 1)
            dve.wait_ge(n_("sd"), 2)
            dve.reciprocal(SD2[:, :], SD2[:, :]).then_inc(n_("v2"), 1)
            dve.wait_ge(n_("v2"), 4)
            dve.tensor_tensor(RS2[:, :], SD2[:, :], RS[:, :], ALU.mult).then_inc(n_("v2"), 1)
            dve.wait_ge(n_("v2"), 5)

        def norm_stats_act(act, tag, eps2=None):
            n_ = lambda s: sem(f"{tag}_{s}")
            act.wait_ge(n_("ve"), 1)
            act.activation(SD[:, :], SD[:, :], ACT.Sqrt).then_inc(n_("sd"), 1)
            if eps2 is not None:
                act.wait_ge(n_("v2"), 3)
                act.activation(SD2[:, :], SD2[:, :], ACT.Sqrt).then_inc(n_("sd"), 1)

        def normed(dve, g, src, dst, rs, done):
            for t in range(GT):
                k = g * GT + t
                last = dve.tensor_scalar(dst[:, t * D:(t + 1) * D], src[:, k * D:(k + 1) * D],
                                         MV[:, k, 0:1], rs[:, k:k + 1], ALU.subtract, ALU.mult)
            last.then_inc(done, 1)

        def bank(u, k):
            return PS[:, 4 * u + k, :]

        def linear_attention():
            at[0] = 0
            h0 = [cut(G) for _ in range(2)]
            hn = [cut(G) for _ in range(2)]
            hb = [cut(G) for _ in range(2)]
            hT = [cut(G) for _ in range(2)]
            eq = [cut(G) for _ in range(2)]
            rq = [cut(G) for _ in range(2)]
            ek = [cut(G) for _ in range(2)]
            rk = [cut(G) for _ in range(2)]
            fq = [cut(G) for _ in range(2)]
            fk = [cut(G) for _ in range(2)]
            va = [cut(GT * (D + 1)).rearrange("p (t c) -> p t c", t=GT) for _ in range(2)]
            kvm = [cut(2 * (D + H)).rearrange("p (b c) -> p b c", b=2) for _ in range(2)]
            ks = [cut(2) for _ in range(2)]
            den = [cut(GT * H) for _ in range(2)]
            rec = [cut(GT * H) for _ in range(2)]
            att = [cut(G) for _ in range(2)]
            aT = [cut(G) for _ in range(2)]
            kvp = lambda u: PS[:, 4 * u + 2:4 * u + 4, :].rearrange("p b (t c) -> p (b t) c", t=2)
            nd = lambda u, k: PS[:, 4 * u + 1 + k, 0:2 * (D + H)].rearrange("p (t c) -> p t c", t=2)
            kvb = lambda u: bank(u, 0)[:, 0:2 * (D + 1)].rearrange("p (b c) -> p b c", b=2)
            n_ = lambda s: sem("a0_" + s)

            with nc.Block() as block:
                @block.vector
                def _(dve):
                    def features(g):
                        u = g % 2
                        dve.wait_ge(n_("k"), g + 1)
                        dve.scalar_tensor_tensor(out=fk[u], in0=ek[u], scalar=1.0, in1=rk[u],
                                                 op0=ALU.min, op1=ALU.add).then_inc(n_("fk"), 1)
                        dve.wait_ge(n_("q"), g + 1)
                        dve.scalar_tensor_tensor(out=fq[u], in0=eq[u], scalar=1.0, in1=rq[u],
                                                 op0=ALU.min, op1=ALU.add).then_inc(n_("fq"), 1)

                    def sums_of_heads(g):
                        u = g % 2
                        dve.wait_ge(n_("kv"), g + 1)
                        dve.tensor_copy(ks[u][:, :], kvb(u)[:, :, D]).then_inc(n_("ks"), 1)
                        dve.tensor_tensor(kvm[u][:, :, 0:D], kvb(u)[:, :, 0:D], over(BM[:, :], 2), ALU.mult)
                        dve.wait_ge(n_("ks"), g + 1)
                        for b in range(2):
                            last = dve.tensor_scalar(kvm[u][:, b, D:D + H], HM[:, :], ks[u][:, b:b + 1], None,
                                                     ALU.mult)
                        last.then_inc(n_("kvm"), 1)

                    def quotients(g):
                        u = g % 2
                        dve.wait_ge(n_("nd"), g + 1)
                        for k in range(2):
                            last = dve.tensor_scalar(tiles(den[u][:, 2 * k * H:2 * (k + 1) * H], 2),
                                                     nd(u, k)[:, :, D:D + H], 1e-6, None, ALU.add)
                        last.then_inc(n_("den"), 1)
                        dve.wait_ge(n_("den"), g + 1)
                        dve.reciprocal(rec[u][:, :], den[u][:, :]).then_inc(n_("rec"), 1)
                        dve.wait_ge(n_("rec"), g + 1)
                        for k in range(2):
                            last = dve.tensor_tensor(
                                att[u][:, 2 * k * D:2 * (k + 1) * D].rearrange("p (t h e) -> p t h e", t=2, h=H),
                                nd(u, k)[:, :, 0:D].rearrange("p t (h e) -> p t h e", h=H),
                                over(rec[u][:, 2 * k * H:2 * (k + 1) * H].rearrange("p (t h) -> p t h", t=2), DH, 3),
                                ALU.mult)
                        last.then_inc(n_("att"), 1)

                    def residual(g):
                        dve.wait_ge(n_("proj"), g + 1)
                        dve.wait_ge(n_("hb"), g + 1)
                        dve.tensor_tensor(XX[:, g * G:(g + 1) * G], bank(g % 2, 3), hb[g % 2],
                                          ALU.add).then_inc(n_("xx"), 1)
                        dve.wait_ge(n_("xx"), g + 1)
                        for k in range(g * GT, (g + 1) * GT):
                            dve.bn_stats(ST[:, 6 * k:6 * k + 6], XX[:, k * D:(k + 1) * D]).then_inc(n_("stats"), 1)

                    norm_stats_dve(dve, "a0", "stats0", 1e-5, 1e-5)
                    normed(dve, 0, X, hn[0], RS2, n_("hn"))
                    for u in range(2):
                        dve.memset(va[u][:, :, D:D + 1], 1.0).then_inc(n_("ones"), 1)
                    dve.wait_ge(sem("const_ready"), CONST)
                    for g in range(NG + 1):
                        if g:
                            sums_of_heads(g - 1)
                        if g + 1 < NG:
                            normed(dve, g + 1, X, hn[(g + 1) % 2], RS2, n_("hn"))
                        if g:
                            quotients(g - 1)
                        if g < NG:
                            features(g)
                        if g:
                            residual(g - 1)

                @block.gpsimd
                def _(pool):
                    pool.wait_ge(sem("rows_loaded"), 16)
                    pool.wait_ge(n_("rs"), 1)
                    for g in range(NG):
                        if g >= 2:
                            pool.wait_ge(n_("xx"), g - 1)
                        normed(pool, g, X, h0[g % 2], RS, n_("h0"))
                        pool.wait_ge(n_("h0"), g + 1)
                        pool.tensor_tensor(tiles(hb[g % 2]), tiles(h0[g % 2]), over(row("projb"), GT), ALU.add)\
                            .then_inc(n_("hb"), 1)

                @block.scalar
                def _(act):
                    norm_stats_act(act, "a0", 1e-5)
                    act.wait_ge(sem("cols_loaded"), 16)
                    for g in range(NG + 1):
                        u = g % 2
                        if g < NG:
                            act.wait_ge(n_("hnT"), g + 1)
                            act.activation(hT[u], bank(u, 0), ACT.Identity, bias=col("b1_0"), scale=col("g1_0"))\
                                .then_inc(n_("hT"), 1)
                            act.wait_ge(n_("kvp"), g + 1)
                            act.activation(tiles(ek[u]), kvp(u)[:, :, 0:D], ACT.Exp)
                            act.activation(tiles(rk[u]), kvp(u)[:, :, 0:D], ACT.Relu).then_inc(n_("k"), 1)
                            act.activation(va[u][:, :, 0:D], kvp(u)[:, :, D:2 * D], ACT.Copy).then_inc(n_("va"), 1)
                            act.wait_ge(n_("qp"), g + 1)
                            act.activation(eq[u], bank(u, 1), ACT.Exp)
                            act.activation(rq[u], bank(u, 1), ACT.Relu).then_inc(n_("q"), 1)
                        if g:
                            act.wait_ge(n_("attT"), g)
                            act.activation(aT[1 - u], bank(1 - u, 0), ACT.Copy).then_inc(n_("aT"), 1)

                @block.tensor
                def _(pe):
                    def transposes(g):
                        u = g % 2
                        pe.wait_ge(n_("hn"), g + 1)
                        for t in range(GT):
                            last = pe.transpose(bank(u, 0)[:, t * P:(t + 1) * P], hn[u][:, t * D:(t + 1) * D],
                                                ident[:, :])
                        last.then_inc(n_("hnT"), 1)

                    def projections(g):
                        u = g % 2
                        if g >= 2:
                            pe.wait_ge(n_("xx"), g - 1)
                        pe.wait_ge(n_("hT"), g + 1)
                        for t in range(GT):
                            last = pe.matmul(kvp(u)[:, t, :], hT[u][:, t * P:(t + 1) * P],
                                             w("qkv0", D, 2 * D), start=True, stop=True)
                        last.then_inc(n_("kvp"), 1)
                        pe.matmul(bank(u, 1), w("qkv0", 0, D), hT[u], start=True, stop=True).then_inc(n_("qp"), 1)

                    def numerators(g):
                        u = g % 2
                        pe.wait_ge(n_("kvm"), g + 1)
                        pe.wait_ge(n_("fq"), g + 1)
                        for t in range(GT):
                            last = pe.matmul(nd(u, t // 2)[:, t % 2, :], fq[u][:, t * P:(t + 1) * P],
                                             kvm[u][:, t // 2, :], start=True, stop=True)
                        last.then_inc(n_("nd"), 1)

                    def key_values(g):
                        u = g % 2
                        pe.wait_ge(n_("fk"), g + 1)
                        pe.wait_ge(n_("va"), g + 1)
                        for b in range(2):
                            for t in range(2):
                                last = pe.matmul(kvb(u)[:, b, :], fk[u][:, (2 * b + t) * D:(2 * b + t + 1) * D],
                                                 va[u][:, 2 * b + t, :], start=(t == 0), stop=(t == 1))
                        last.then_inc(n_("kv"), 1)

                    def transposed_result(g):
                        u = g % 2
                        pe.wait_ge(n_("att"), g + 1)
                        for t in range(GT):
                            last = pe.transpose(bank(u, 0)[:, t * P:(t + 1) * P], att[u][:, t * D:(t + 1) * D],
                                                ident[:, :])
                        last.then_inc(n_("attT"), 1)

                    def output(g):
                        u = g % 2
                        pe.wait_ge(n_("aT"), g + 1)
                        for t in range(GT):
                            last = pe.matmul(bank(u, 3)[:, t * D:(t + 1) * D], aT[u][:, t * P:(t + 1) * P],
                                             w("proj0"), start=True, stop=True)
                        last.then_inc(n_("proj"), 1)

                    pe.wait_ge(sem("const_ready"), CONST)
                    pe.wait_ge(sem("w0_loaded"), 16)
                    for g in range(NG + 1):
                        if g < NG:
                            transposes(g)
                        if g:
                            numerators(g - 1)
                        if g < NG:
                            projections(g)
                        if g:
                            transposed_result(g - 1)
                        if g < NG:
                            key_values(g)
                        if g:
                            output(g - 1)

        def feed_forward(L, func, eps, stats):
            at[0] = 0
            hn = [cut(G) for _ in range(NG)]
            hT = [cut(G) for _ in range(2)]
            res = [cut(G) for _ in range(NG)]
            hid = [cut(HC * G) for _ in range(2)]
            n_ = lambda s: sem(f"f{L}_" + s)
            order = [1, 2, 3, 0]
            OUT = 3

            with nc.Block() as block:
                @block.vector
                def _(dve):
                    norm_stats_dve(dve, f"f{L}", stats, eps)
                    for g in range(NG):
                        normed(dve, g, XX, hn[g], RS, n_("hn"))
                    for g in range(NG):
                        dve.wait_ge(n_("fc2"), g + 1)
                        dve.wait_ge(n_("res"), g + 1)
                        dve.tensor_tensor(X[:, g * G:(g + 1) * G], bank(g % 2, OUT), res[g], ALU.add)\
                            .then_inc(n_("x"), 1)
                        dve.wait_ge(n_("x"), g + 1)
                        for k in range(g * GT, (g + 1) * GT):
                            dve.bn_stats(ST[:, 6 * k:6 * k + 6], X[:, k * D:(k + 1) * D]).then_inc(n_("stats"), 1)

                @block.gpsimd
                def _(pool):
                    for g in range(NG):
                        s_ = slice(g * G, (g + 1) * G)
                        pool.tensor_tensor(res[g], X[:, s_], XX[:, s_], ALU.add).then_inc(n_("sum"), 1)
                        pool.wait_ge(n_("sum"), g + 1)
                        pool.tensor_tensor(tiles(res[g]), tiles(res[g]), over(row(f"fc2b_{L}"), GT), ALU.add)\
                            .then_inc(n_("res"), 1)

                @block.scalar
                def _(act):
                    norm_stats_act(act, f"f{L}")

                    def transposed(g):
                        act.wait_ge(n_("hnT"), g + 1)
                        act.activation(hT[g % 2], bank(g % 2, 0), ACT.Identity, bias=col(f"b2_{L}"),
                                       scale=col(f"g2_{L}")).then_inc(n_("hT"), 1)

                    transposed(0)
                    transposed(1)
                    for g in range(NG):
                        u = g % 2
                        if g >= 2:
                            act.wait_ge(n_("fc2"), g - 1)
                        for c in range(HC):
                            act.wait_ge(n_("fc1"), g * HC + c + 1)
                            act.activation(hid[u][:, c * G:(c + 1) * G], bank(u, order[c]), func,
                                           bias=col(f"fcb_{L}", c)).then_inc(n_("hid"), 1)
                        if 1 <= g < NG - 1:
                            transposed(g + 1)

                @block.tensor
                def _(pe):
                    def transposes(g):
                        u = g % 2
                        pe.wait_ge(n_("hn"), g + 1)
                        if g >= 2:
                            pe.wait_ge(n_("hid"), (g - 1) * HC)
                        for t in range(GT):
                            last = pe.transpose(bank(u, 0)[:, t * P:(t + 1) * P], hn[g][:, t * D:(t + 1) * D],
                                                ident[:, :])
                        last.then_inc(n_("hnT"), 1)

                    def up(g):
                        u = g % 2
                        pe.wait_ge(n_("hT"), g + 1)
                        for c in range(HC):
                            if g >= 2 and order[c] == OUT:
                                pe.wait_ge(n_("x"), g - 1)
                            pe.matmul(bank(u, order[c]), w(f"fc1_{L}", c * P, P), hT[u], start=True,
                                      stop=True).then_inc(n_("fc1"), 1)

                    def down(g):
                        u = g % 2
                        pe.wait_ge(n_("hid"), (g + 1) * HC)
                        for t in range(GT):
                            for c in range(HC):
                                last = pe.matmul(bank(u, OUT)[:, t * D:(t + 1) * D],
                                                 hid[u][:, c * G + t * P:c * G + (t + 1) * P],
                                                 w(f"fc2_{L}", c * D, D), start=(c == 0), stop=(c == HC - 1))
                        last.then_inc(n_("fc2"), 1)

                    if L:
                        pe.wait_ge(sem("w3_loaded"), 16)
                    transposes(0)
                    transposes(1)
                    up(0)
                    for g in range(1, NG):
                        up(g)
                        if g + 1 < NG:
                            transposes(g + 1)
                        down(g - 1)
                    down(NG - 1)

        MROW = 96
        DROW = 72
        DR = 12
        KTILE = S // P
        VB = [VA[:, NT * D + k * 1024:NT * D + (k + 1) * 1024].rearrange("p (t h c) -> p t h c", t=KTILE, h=H)
              for k in range(2)]

        def cross_memory():
            at[0] = 0
            QS = cut(4 * H * S, BF16)
            KS = cut(4 * H * S, BF16)
            bias = cut(KTILE * S).rearrange("p (t c) -> p t c", t=KTILE)
            dist = cut(P, BF16)
            decI = cut(3 * P, BF16).rearrange("p (a c) -> p a c", a=3)
            return QS, KS, bias, dist, decI

        def spread_values(pool, b, done):
            for jj in range(2):
                dst = VB[b % 2].rearrange("p t (x j c) e -> p (t x) j c e", j=2, c=4)
                src = VA[:, b * S:(b + 1) * S].rearrange("p (x j c e) -> p x j c e", j=2, c=4, e=DH)
                last = pool.tensor_copy(dst[:, :, jj, :, 16 * jj:16 * jj + DH], src[:, :, jj])
            last.then_inc(done, 1)

        LOAD = 16 * 4

        def loaded(L, b):
            return sem(f"parts{L}{b % 2}_loaded")

        def stored(L, g):
            return sem(f"parts{L}{g}_stored")

        def store_parts(sp, L, g, parts):
            for b in range(2):
                sp.dma_start(scratch[L][2 * g + b].rearrange("k a r t -> r (k a) t"),
                             parts[:, :, :, b * S:(b + 1) * S].rearrange("p k a t -> p (k a) t"))\
                    .then_inc(stored(L, g), 16)

        def load_stacks(sp, L, b, QS, KS):
            at_ = bass.ds(slot(b), H * S)
            sp.wait_ge(stored(L, b // 2), 32)
            for a in range(3):
                sp.dma_start(QS[24 * a:24 * a + 24, at_],
                             over(scratch[L][b, 0, a].rearrange("(e h) t -> e (h t)", h=H), 3, 0))\
                    .then_inc(loaded(L, b), 16)
            sp.dma_start(KS[0:72, at_], over(scratch[L][b, 1].rearrange("a (e h) t -> (a e) (h t)", h=H), 3, 0))\
                .then_inc(loaded(L, b), 16)

        def slot(b):
            return b % 4 * (H * S)

        def cross_prepare(L, stats):
            z = f"x{L}_"
            QS, KS, bias, dist, decI = cross_memory()
            V = VA[:, 0:NT * D]
            gap = cut(P)
            gapi = cut(P).bitcast(I32)
            dec = cut(6)
            decb = cut(2, BF16)
            decrow = cut(2)
            PR = cut(4 * S + 3)
            QD, KD = cut(S, BF16), cut(S, BF16)
            hn = [cut(G) for _ in range(NG)]
            hT = [cut(G) for _ in range(2)]
            qk = [cut(2 * G).rearrange("p (k t) -> p k t", k=2) for _ in range(3)]
            cg = [VA[:, NT * D + 2048 + u * G:NT * D + 2048 + (u + 1) * G] for u in range(2)]
            bq = cut(1)
            minus = cut(S, BF16)
            parts = [cut(6 * G, BF16).rearrange("p (k a t) -> p k a t", k=2, a=3) for _ in range(NG)]

            def decay_tables(dve):
                s, c = sem(z + "d"), dec
                dve.tensor_scalar(c[:, 0:1], row("decay"), -1.0, None, ALU.mult).then_inc(s, 1)
                dve.wait_ge(sem(z + "iota"), 1)
                dve.tensor_copy(gap, gapi).then_inc(s, 1)
                dve.wait_ge(s, 2)
                dve.tensor_copy(decb[:, 0:1], c[:, 0:1]).then_inc(s, 1)
                dve.scalar_tensor_tensor(out=gap, in0=gap, scalar=-1.0, in1=gap, op0=ALU.mult,
                                         op1=ALU.max).then_inc(s, 1)
                dve.wait_ge(s, 4)
                dve.tensor_copy(c[:, 1:2], decb[:, 0:1]).then_inc(s, 1)
                dve.tensor_copy(dist, gap).then_inc(s, 1)
                dve.wait_ge(sem(z + "bias"), 1)
                for t in range(KTILE):
                    dve.tensor_scalar(bias[:, t, t * P:(t + 1) * P], gap, c[:, 0:1], None, ALU.mult)\
                        .then_inc(s, 1)
                dve.wait_ge(s, 8)
                dve.tensor_tensor(c[:, 4:5], c[:, 0:1], c[:, 1:2], ALU.subtract).then_inc(s, 1)
                dve.wait_ge(s, 9)
                dve.tensor_copy(decb[:, 1:2], c[:, 4:5]).then_inc(s, 1)
                dve.wait_ge(s, 10)
                dve.tensor_copy(c[:, 2:3], decb[:, 1:2]).then_inc(s, 1)
                dve.wait_ge(s, 11)
                dve.tensor_tensor(c[:, 3:4], c[:, 4:5], c[:, 2:3], ALU.subtract).then_inc(s, 1)
                dve.wait_ge(s, 12)
                for a in range(3):
                    dve.tensor_scalar(decI[:, a, :], ident[:, :], c[:, 1 + a:2 + a], None, ALU.mult)\
                        .then_inc(s, 1)
                pick = PR[0:DR, 4 * S:4 * S + 3]
                dve.wait_ge(sem(z + "positions"), 16)
                dve.tensor_scalar(decrow[0:DR, 0:1], pick[:, 0:1], c[0:DR, 1:2], None, ALU.mult).then_inc(s, 1)
                for a in (1, 2):
                    dve.wait_ge(s, 15 + a)
                    dve.scalar_tensor_tensor(out=decrow[0:DR, 0:1], in0=pick[:, a:a + 1],
                                             scalar=c[0:DR, 1 + a:2 + a], in1=decrow[0:DR, 0:1], op0=ALU.mult,
                                             op1=ALU.add).then_inc(s, 1)
                dve.wait_ge(s, 18)
                for k, rows_ in enumerate((QD, KD)):
                    dve.scalar_tensor_tensor(out=rows_[0:DR], in0=PR[0:DR, (2 * k + 1) * S:(2 * k + 2) * S],
                                             scalar=decrow[0:DR, 0:1], in1=PR[0:DR, 2 * k * S:(2 * k + 1) * S],
                                             op0=ALU.mult, op1=ALU.add).then_inc(sem(z + "decay_rows"), 1)

            with nc.Block() as block:
                @block.gpsimd
                def _(pool):
                    clear = sem(z + "cleared")
                    if L == 0:
                        pool.memset(bias, 0.0).then_inc(clear, 1)
                        pool.memset(dist, 0.0).then_inc(clear, 1)
                    else:
                        pool.iota(gapi, pattern=[[-1, P]], base=0, channel_multiplier=1).then_inc(sem(z + "iota"), 1)
                        pool.memset(bias, 0.0).then_inc(sem(z + "bias"), 1)
                    pool.memset(QS.bitcast(F32), 0.0).then_inc(clear, 1)
                    pool.memset(KS.bitcast(F32), 0.0).then_inc(clear, 1)
                    pool.memset(minus.bitcast(F32), MINUS_ONES).then_inc(clear, 1)
                    if L == 0:
                        for m in VB:
                            pool.memset(m, 0.0).then_inc(clear, 1)
                    if L == 0:
                        pool.wait_ge(clear, 7)
                        for m in VB:
                            for jj in range(2):
                                pool.memset(m.rearrange("p t (x j c) e -> p (t x) j c e", j=2, c=4)
                                            [:, :, jj, :, 16 * jj + DH:16 * jj + 16], 1.0).then_inc(clear, 1)
                        pool.affine_select(out=bias, in_=bias, compare_op=ALU.is_ge, fill=-BIG, base=0,
                                           pattern=[[P, 2], [-1, S]], channel_multiplier=1).then_inc(clear, 1)
                        pool.affine_select(out=dist, in_=dist, compare_op=ALU.is_ge,
                                           fill=-BIG, base=0, pattern=[[1, P]], channel_multiplier=-1)\
                            .then_inc(clear, 1)
                    pool.wait_ge(clear, 13 if L == 0 else 3)
                    for g in range(NG):
                        pool.wait_ge(sem(z + "hn"), g + 1)
                        s_ = slice(g * G, (g + 1) * G)
                        pool.tensor_tensor(tiles(X[:, s_]), tiles(X[:, s_]), over(row(f"bo{L}"), GT), ALU.add)\
                            .then_inc(sem(z + "xb"), 1)
                    for b in range(2):
                        pool.wait_ge(sem(z + "v"), 1)
                        spread_values(pool, b, sem(z + "VB"))

                @block.vector
                def _(dve):
                    norm_stats_dve(dve, f"x{L}", stats, 1e-5)
                    dve.tensor_scalar(bq, col(f"bq{L}"), SCALE, None, ALU.mult).then_inc(sem(z + "bq"), 1)
                    def third_parts(g):
                        dve.wait_ge(sem(z + "p2"), g + 1)
                        dve.tensor_tensor(parts[g][:, :, 2, :], qk[g % 3], parts[g][:, :, 1, :], ALU.subtract)\
                            .then_inc(sem(z + "p3"), 1)

                    for g in range(NG):
                        normed(dve, g, X, hn[g], RS, sem(z + "hn"))
                    if L == 1:
                        decay_tables(dve)
                    for g in range(NG):
                        u = g % 2
                        dve.wait_ge(sem(z + "vp"), g + 1)
                        dve.tensor_tensor(tiles(V[:, g * G:(g + 1) * G]), tiles(bank(u, 3)),
                                          over(row(f"bv{L}"), GT), ALU.add).then_inc(sem(z + "v"), 1)
                        dve.wait_ge(sem(z + "p1"), g + 1)
                        dve.tensor_tensor(qk[g % 3], qk[g % 3], parts[g][:, :, 0, :], ALU.subtract)\
                            .then_inc(sem(z + "r1"), 1)
                        if g:
                            third_parts(g - 1)
                    third_parts(NG - 1)

                @block.scalar
                def _(act):
                    norm_stats_act(act, f"x{L}")
                    act.wait_ge(sem(z + "bq"), 1)

                    def transposed(g):
                        act.wait_ge(sem(z + "hnT"), g + 1)
                        act.activation(hT[g % 2], bank(g % 2, 0), ACT.Copy).then_inc(sem(z + "hT"), 1)

                    def first_parts(g):
                        u = g % 2
                        act.wait_ge(sem(z + "qkp"), g + 1)
                        if g >= 3:
                            act.wait_ge(sem(z + "p3"), g - 2)
                        for k, (bias_, scale) in enumerate(((bq, SCALE), (col(f"bk{L}"), 1.0))):
                            act.activation(qk[g % 3][:, k, :], bank(u, 1 + k), ACT.Identity, bias=bias_, scale=scale)
                            last = act.activation(parts[g][:, k, 0, :], bank(u, 1 + k), ACT.Identity, bias=bias_,
                                                  scale=scale)
                        last.then_inc(sem(z + "p1"), 1)

                    def second_parts(g):
                        act.wait_ge(sem(z + "r1"), g + 1)
                        act.activation(parts[g][:, :, 1, :], qk[g % 3], ACT.Copy).then_inc(sem(z + "p2"), 1)

                    transposed(0)
                    for g in range(NG):
                        if g + 1 < NG:
                            transposed(g + 1)
                        first_parts(g)
                        if g:
                            second_parts(g - 1)
                    second_parts(NG - 1)

                @block.tensor
                def _(pe):
                    pe.wait_ge(sem(f"w{1 if L == 0 else 4}_loaded"), 16)
                    for g in range(NG):
                        u = g % 2
                        pe.wait_ge(sem(z + "hn"), g + 1)
                        for t in range(GT):
                            last = pe.transpose(bank(u, 0)[:, t * P:(t + 1) * P], hn[g][:, t * D:(t + 1) * D],
                                                ident[:, :])
                        last.then_inc(sem(z + "hnT"), 1)
                        pe.wait_ge(sem(z + f"ctx{u}"), 16 * (g // 2 + 1))
                        if g >= 2:
                            pe.wait_ge(sem(z + "p1"), g - 1)
                            pe.wait_ge(sem(z + "v"), g - 1)
                        pe.matmul(bank(u, 2), w(f"xk{L}"), cg[u], start=True, stop=True)
                        for t in range(GT):
                            last = pe.matmul(bank(u, 3)[:, t * D:(t + 1) * D], cg[u][:, t * P:(t + 1) * P],
                                             w(f"xv{L}"), start=True, stop=True)
                        last.then_inc(sem(z + "vp"), 1)
                        pe.wait_ge(sem(z + "hT"), g + 1)
                        pe.matmul(bank(u, 1), w(f"xq{L}"), hT[u], start=True, stop=True)\
                            .then_inc(sem(z + "qkp"), 1)

                @block.sync
                def _(sp):
                    def context(g):
                        sp.dma_start(cg[g % 2], ctxT[:, g * G:(g + 1) * G]).then_inc(sem(z + f"ctx{g % 2}"), 16)

                    context(0)
                    context(1)
                    if L == 1:
                        sp.dma_start(PR[0:DR], positions).then_inc(sem(z + "positions"), 16)
                    for g in range(2, NG):
                        sp.wait_ge(sem(z + "vp"), g - 1)
                        context(g)
                    sp.wait_ge(sem(z + "cleared"), 5 if L == 0 else 3)
                    sp.dma_start(KS[MROW:MROW + 3, :].rearrange("r (n t) -> r n t", t=S),
                                 over(minus[0:3], 4 * H)).then_inc(sem(z + "filled"), 16)
                    for g in range(2):
                        sp.wait_ge(sem(z + "p3"), g + 1)
                        store_parts(sp, L, g, parts[g])
                        if g == 0 and L == 1:
                            sp.wait_ge(sem(z + "decay_rows"), 2)
                            for stack, rows_ in ((QS, QD), (KS, KD)):
                                sp.dma_start(stack[DROW:DROW + DR, :].rearrange("r (n t) -> r n t", t=S),
                                             over(rows_[0:DR], 4 * H)).then_inc(sem(z + "filled"), 16)
                        if g == 0:
                            load_stacks(sp, L, 0, QS, KS)
                    sp.wait_ge(sem(z + "filled"), 16 if L == 0 else 48)

            return parts[NG - 2:]

        def cross_attend(L, last_parts):
            z = f"y{L}_"
            QS, KS, bias, dist, decI = cross_memory()
            PT = cut(4 * 2 * 512).rearrange("p (n s c) -> p n s c", n=4, s=2)
            junk = cut(8 * S, BF16).rearrange("p (n c) -> p n c", n=8)
            M = cut(2 * H).rearrange("p (t h) -> p t h", t=2)
            MR = cut(2 * 8).rearrange("p (t h) -> p t h", t=2)
            MP = cut(2 * 2 * 24, BF16).rearrange("p (f t c) -> p f t c", f=2, t=2)
            mT = cut(2 * S, BF16).rearrange("p (f c) -> p f c", f=2)
            OT = VA[:, NT * D + 2048:NT * D + 2560]
            aT = VA[:, NT * D + 2560:NT * D + 2816]
            att = VA[:, NT * D + 2816:NT * D + 3072].rearrange("p (t c) -> p t c", t=2)
            rec = VA[:, NT * D + 3072:NT * D + 3104].rearrange("p (x h) -> p x h", x=4)
            misc = PS[:, 7, :]
            miscb = PS[:, 7, :].bitcast(BF16)
            O = PS[:, 6, :]
            KEYS = [P, 2 * P] if L == 0 else [S, S]
            NCOL = 3 * P if L == 0 else 2 * S

            def wait(e, s, value):
                if not isinstance(value, int) or value > 0:
                    e.wait_ge(sem(z + s), value)

            def pe_max_scores(pe, b, pos):
                wait(pe, "max", 16 * b + pos - 1)
                for t in range(2):
                    last = pe.matmul(PS[:, pos % 2, t * S:t * S + KEYS[t]],
                                     QS[0:MROW, bass.ds(slot(b) + pos * S + t * P, P)],
                                     KS[0:MROW, bass.ds(slot(b) + pos * S, KEYS[t])], start=True, stop=True)
                last.then_inc(sem(z + "A"), 1)

            def pe_scores(pe, b, n, s):
                if s == 0:
                    wait(pe, "exp", 8 * b + n - 1)
                    if n % 4 == 0:
                        wait(pe, f"mrow{n // 4}", 48 * b + 48)
                pos = 2 * n + s
                bk = PS[:, 2 + 2 * (n % 2) + s, :]
                for t in range(2):
                    q0 = P * t if L == 0 else 0
                    pe.matmul(bk[:, t * S:t * S + S - q0], KS[:, bass.ds(slot(b) + pos * S + t * P, P)],
                              QS[:, bass.ds(slot(b) + pos * S + q0, S - q0)], start=True, stop=True)
                    own = t * S + t * P - q0
                    for lhs in ([identb[:, :]] if L == 0 else [decI[:, a, :] for a in range(3)]):
                        last = pe.matmul(bk[:, own:own + P], lhs, dist, start=False, stop=True,
                                         skip_group_check=True)
                if s == 1:
                    last.then_inc(sem(z + "S"), 1)

            def pe_values(pe, b, j):
                wait(pe, "exp", 8 * b + 2 * j + 2)
                if j == 0:
                    wait(pe, "OT", b)
                    wait(pe, "VB", b - 1)
                for t in range(2):
                    q0 = P * t if L == 0 else 0
                    for c in range(4):
                        first = t == 0 and j == 0
                        last = pe.matmul(
                            O[32 * c:32 * c + 32, (j // 2) * S + q0:(j // 2 + 1) * S],
                            VB[b % 2][:, t, 4 * j + c, :], PT[:, (2 * j + c // 2) % 4, c % 2, t * S:t * S + S - q0],
                            start=first, stop=(t == 1), skip_group_check=True)
                last.then_inc(sem(z + "pv"), 1)

            def pe_mT(pe, b, f):
                wait(pe, "mp", 2 * b + f + 1)
                for t in range(2):
                    last = pe.transpose(miscb[0:24, t * P:(t + 1) * P], MP[:, f, t, :], identb[:, :])
                last.then_inc(sem(z + "mTp"), 1)

            def pe_tail1(pe, b):
                wait(pe, "OT", b + 1)
                for x4 in range(2):
                    for t in range(2):
                        last = pe.transpose(misc[:, (2 * x4 + t) * P:(2 * x4 + t + 1) * P],
                                            OT[:, x4 * S + t * P:x4 * S + (t + 1) * P], ident[:, :])
                last.then_inc(sem(z + "t1"), 1)

            def pe_tail2(pe, b):
                wait(pe, "att", b + 1)
                for t in range(2):
                    last = pe.transpose(misc[:, t * P:(t + 1) * P], att[:, t, :], ident[:, :])
                last.then_inc(sem(z + "t2"), 1)

            def pe_tail3(pe, b):
                wait(pe, "aT", b + 1)
                for t in range(2):
                    last = pe.matmul(misc[:, t * D:(t + 1) * D], aT[:, t * P:(t + 1) * P], w(f"xo{L}"),
                                     start=True, stop=True)
                last.then_inc(sem(z + "o"), 1)

            def pe_iteration(pe, b):
                first, last = b == 0, b == B - 1
                for n in range(8):
                    if n == 1:
                        wait(pe, "x", b - 1)
                        pe_mT(pe, b, 1)
                    if n == 5 and not last:
                        wait(pe, "att", b)
                        wait(pe, "mT", 2 * b + 2)
                        pe_mT(pe, b + 1, 0)
                    if n == 0 and not last:
                        pe.wait_ge(loaded(L, b + 1), LOAD * ((b + 1) // 2 + 1))
                    for s in range(2):
                        pe_scores(pe, b, n, s)
                        if not last:
                            pe_max_scores(pe, b + 1, 2 * n + s)
                    if n == 1 and not first:
                        wait(pe, "mT", 2 * b + 2)
                        pe_tail1(pe, b - 1)
                    if n == 5 and not first:
                        if not last:
                            wait(pe, "mT", 2 * b + 3)
                        pe_tail2(pe, b - 1)
                    if n == 6 and not first:
                        pe_tail3(pe, b - 1)
                    if n in (3, 5, 7):
                        pe_values(pe, b, (n - 3) // 2)
                pe_values(pe, b, 3)

            def dve_max(dve, b, n):
                for pos in (2 * n, 2 * n + 1):
                    wait(dve, "A", 16 * b + pos + 1)
                    wait(dve, "max", 16 * b + pos - 3)
                    for t in range(2):
                        last = dve.tensor_tensor_reduce(junk[:, 2 * (pos % 4) + t, 0:KEYS[t]],
                                                        PS[:, pos % 2, t * S:t * S + KEYS[t]],
                                                        bias[:, t, 0:KEYS[t]], 1.0, LOW, ALU.add, ALU.max,
                                                        M[:, t, pos:pos + 1])
                    last.then_inc(sem(z + "max"), 1)

            def pool_parts(pool, b, f):
                m, mp = M[:, :, 8 * f:8 * f + 8], MP[:, f].rearrange("p t (a h) -> p t a h", a=3)
                wait(pool, "max", 16 * b + 8 * f + 8)
                s, k = sem(z + "split"), 6 * b + 3 * f
                pool.tensor_copy(mp[:, :, 0, :], m).then_inc(s, 1)
                pool.wait_ge(s, k + 1)
                pool.tensor_tensor(MR, m, mp[:, :, 0, :], ALU.subtract).then_inc(s, 1)
                pool.wait_ge(s, k + 2)
                pool.tensor_copy(mp[:, :, 1, :], MR).then_inc(s, 1)
                pool.wait_ge(s, k + 3)
                pool.tensor_tensor(mp[:, :, 2, :], MR, mp[:, :, 1, :], ALU.subtract).then_inc(sem(z + "mp"), 1)

            def dve_normalise(dve, b):
                T1 = misc.rearrange("p (x c e) -> p x c e", x=4, e=16)
                wait(dve, "t1", b + 1)
                dve.reciprocal(rec, T1[:, :, :, DH]).then_inc(sem(z + "rec"), 1)
                wait(dve, "rec", b + 1)
                for x4 in range(2):
                    for t in range(2):
                        o = att[:, t, x4 * 64:(x4 + 1) * 64].rearrange("p (j c e) -> p c j e", j=2, e=DH)
                        i_ = T1[:, 2 * x4 + t, :, 0:DH].rearrange("p (c j) e -> p c j e", j=2)
                        r = over(rec[:, 2 * x4 + t, :].rearrange("p (c j) -> p c j", j=2), DH, 3)
                        last = dve.tensor_tensor(o, i_, r, ALU.mult)
                last.then_inc(sem(z + "att"), 1)

            def dve_residual(dve, b):
                wait(dve, "o", b + 1)
                xs = X[:, b * S:(b + 1) * S]
                dve.tensor_tensor(xs, misc[:, 0:S], xs, ALU.add).then_inc(sem(z + "x"), 1)

            def dve_stats(dve, b):
                wait(dve, "x", b + 1)
                for t in range(2):
                    k = 2 * b + t
                    dve.bn_stats(ST[:, 6 * k:6 * k + 6], X[:, k * D:(k + 1) * D]).then_inc(sem(z + "stats"), 1)

            def dve_iteration(dve, b):
                first, last = b == 0, b == B - 1
                for n in range(8):
                    if not last:
                        dve_max(dve, b + 1, n)
                    if n == 7 and not first:
                        dve_residual(dve, b - 1)
                    if n == 1 and b >= 2:
                        dve_stats(dve, b - 2)
                    if n == 3 and not first:
                        dve_normalise(dve, b - 1)

            def act_exp(act, b, n):
                wait(act, "S", 8 * b + n + 1)
                wait(act, "pv", 4 * b + n // 2 - 1)
                act.activation(PT[:, n % 4, :, 0:NCOL], PS[:, 2 + 2 * (n % 2):4 + 2 * (n % 2), 0:NCOL], ACT.Exp)\
                    .then_inc(sem(z + "exp"), 1)

            def act_mT(act, b, f):
                wait(act, "mTp", 2 * b + f + 1)
                wait(act, f"mrow{f}", 48 * b)
                act.activation(mT[0:24, f, :], miscb[0:24, 0:S], ACT.Copy).then_inc(sem(z + "mT"), 1)

            def act_iteration(act, b):
                first, last = b == 0, b == B - 1
                for n in range(8):
                    act_exp(act, b, n)
                    if n == 0 and not first:
                        wait(act, "pv", 4 * b)
                        act.activation(OT, O, ACT.Copy).then_inc(sem(z + "OT"), 1)
                    if n == 0:
                        act_mT(act, b, 1)
                    if n == 4 and not last:
                        act_mT(act, b + 1, 0)
                    if n == 5 and not first:
                        wait(act, "t2", b)
                        act.activation(aT, misc[:, 0:S], ACT.Copy).then_inc(sem(z + "aT"), 1)

            def sp_mrow(sp, b, f):
                wait(sp, "mT", 2 * b + f + 1)
                for a in range(3):
                    sp.dma_start(QS[MROW + a:MROW + a + 1, bass.ds(slot(b) + f * 8 * S, 8 * S)]
                                 .rearrange("o (h t) -> o h t", h=8),
                                 mT[8 * a:8 * a + 8, f, :]).then_inc(sem(z + f"mrow{f}"), 16)

            def sp_iteration(sp, b):
                sp_mrow(sp, b, 1)
                if b + 3 < B:
                    wait(sp, "pv", 4 * b)
                    sp.wait_ge(loaded(L, b + 3), LOAD * ((b + 1) // 2 + 1))
                    load_stacks(sp, L, b + 3, QS, KS)
                if b + 1 < B:
                    sp_mrow(sp, b + 1, 0)

            with nc.Block() as block:
                @block.gpsimd
                def _(pool):
                    pool_parts(pool, 0, 0)
                    pool_parts(pool, 0, 1)
                    for b in range(B):
                        if 1 <= b < B - 1:
                            wait(pool, "pv", 4 * b)
                            spread_values(pool, b + 1, sem(z + "VB"))
                        if b + 1 < B:
                            pool_parts(pool, b + 1, 0)
                        if b + 1 < B:
                            pool_parts(pool, b + 1, 1)

                @block.sync
                def _(sp):
                    load_stacks(sp, L, 1, QS, KS)
                    store_parts(sp, L, NG - 2, last_parts[0])
                    sp.wait_ge(loaded(L, 2), LOAD)
                    load_stacks(sp, L, 2, QS, KS)
                    sp_mrow(sp, 0, 0)
                    store_parts(sp, L, NG - 1, last_parts[1])
                    for b in range(B):
                        sp_iteration(sp, b)

                @block.tensor
                def _(pe):
                    pe.wait_ge(loaded(L, 0), LOAD)
                    for pos in range(H):
                        pe_max_scores(pe, 0, pos)
                        if pos == 9:
                            pe_mT(pe, 0, 0)
                    wait(pe, "mT", 1)
                    for b in range(B):
                        pe_iteration(pe, b)
                    wait(pe, "x", B - 1)
                    pe_tail1(pe, B - 1)
                    pe_tail2(pe, B - 1)
                    pe_tail3(pe, B - 1)

                @block.vector
                def _(dve):
                    for n in range(8):
                        dve_max(dve, 0, n)
                    for b in range(B):
                        dve_iteration(dve, b)
                    dve_stats(dve, B - 2)
                    dve_normalise(dve, B - 1)
                    dve_residual(dve, B - 1)
                    dve_stats(dve, B - 1)

                @block.scalar
                def _(act):
                    act_mT(act, 0, 0)
                    for b in range(B):
                        act_iteration(act, b)
                    wait(act, "pv", 4 * B)
                    act.activation(OT, O, ACT.Copy).then_inc(sem(z + "OT"), 1)
                    wait(act, "t2", B)
                    act.activation(aT, misc[:, 0:S], ACT.Copy).then_inc(sem(z + "aT"), 1)


        def memory_read(stats):
            at[0] = 0
            hs = cut(NT * D)
            rq = cut(NT * P)
            rk = cut(NMEM)
            hT = [cut(G) for _ in range(2)]
            front_w = cut(P)
            h1 = [cut(G) for _ in range(2)]
            sc = [cut(NMEM) for _ in range(3)]
            ex = [cut(NMEM) for _ in range(2)]
            rep = [cut(NMEM) for _ in range(2)]
            wt = [cut(NMEM) for _ in range(2)]
            wT = [cut(NMEM) for _ in range(2)]
            top = [cut(8) for _ in range(2)]
            ntop = [cut(1) for _ in range(2)]
            den = [cut(1) for _ in range(2)]
            rden = [cut(1) for _ in range(2)]
            coef = [cut(1) for _ in range(2)]
            lrn, var, lv, sig, unc, gate = (cut(NT) for _ in range(6))
            lsum, lall, linv = (cut(1) for _ in range(3))
            n_ = lambda s: sem("m_" + s)
            UP = 64
            MASK = 64
            front = lambda g, k: PS[:, 3 * (g % 2) + k, :]
            score = lambda k: PS[:, 3 + k % 2, :]
            turned = lambda k: PS[:, 5 + k % 2, :]
            read = lambda k: PS[:, 7, (k % 4) * D:(k % 4 + 1) * D]

            def wait(e, s, value):
                if value > 0:
                    e.wait_ge(n_(s), value)

            with nc.Block() as block:
                @block.vector
                def _(dve):
                    norm_stats_dve(dve, "m", stats, 1e-5)
                    dve.tensor_tensor(var, MV[:, :, 1], RS[:, :], ALU.mult).then_inc(n_("chain"), 1)
                    for g in range(NG):
                        normed(dve, g, X, hs[:, g * G:(g + 1) * G], RS, n_("hs"))
                        if g == 0:
                            dve.wait_ge(n_("chain"), 1)
                            dve.tensor_tensor(var, var, RS[:, :], ALU.mult).then_inc(n_("var"), 1)
                    dve.wait_ge(n_("lv"), 1)
                    dve.tensor_reduce(lsum, lv, AX_X, ALU.add).then_inc(n_("lsum"), 1)
                    for g in range(NG):
                        dve.wait_ge(n_("learned"), g + 1)
                        dve.tensor_scalar(lrn[:, g * GT:(g + 1) * GT], front(g, 2)[:, 0:GT],
                                          row("uncb2"), None, ALU.add).then_inc(n_("lrn"), 1)
                    dve.wait_ge(n_("lall"), 1)
                    dve.tensor_scalar(lall, PS[:, 6, 0:1], 1.0 / T, 1e-6, ALU.mult, ALU.add)\
                        .then_inc(n_("chain"), 1)
                    dve.wait_ge(n_("chain"), 2)
                    dve.reciprocal(linv, lall).then_inc(n_("chain"), 1)
                    dve.wait_ge(n_("chain"), 3)
                    dve.tensor_scalar(unc, lv, linv, 0.5, ALU.mult, ALU.mult).then_inc(n_("chain"), 1)
                    dve.wait_ge(n_("chain"), 4)
                    dve.wait_ge(n_("sig"), 1)
                    dve.scalar_tensor_tensor(out=unc, in0=sig, scalar=2.5, in1=unc, op0=ALU.mult, op1=ALU.add)\
                        .then_inc(n_("chain"), 1)
                    dve.wait_ge(n_("chain"), 5)
                    dve.tensor_scalar(unc, unc, 0.0, 5.0, ALU.max, ALU.min).then_inc(n_("unc"), 1)
                    dve.wait_ge(n_("gate"), 1)
                    dve.wait_ge(n_("xh"), NG)

                    def gated(k):
                        xs = X[:, k * D:(k + 1) * D]
                        dve.wait_ge(n_("agg"), k + 1)
                        dve.wait_ge(n_("coef"), k + 1)
                        dve.scalar_tensor_tensor(out=xs, in0=read(k), scalar=coef[k % 2], in1=xs,
                                                 op0=ALU.mult, op1=ALU.add).then_inc(n_("x"), 1)

                    def inverse(k):
                        dve.wait_ge(n_("wt"), k + 1)
                        dve.reciprocal(rden[k % 2], den[k % 2]).then_inc(n_("rden"), 1)

                    def stats_of(k):
                        dve.wait_ge(n_("x"), k + 1)
                        dve.bn_stats(ST[:, 6 * k:6 * k + 6], X[:, k * D:(k + 1) * D]).then_inc(n_("stats"), 1)

                    def best(k):
                        dve.wait_ge(n_("sc"), k + 1)
                        wait(dve, "ntop", k - 1)
                        dve.max(top[k % 2], sc[k % 3]).then_inc(n_("top"), 1)

                    best(0)
                    for k in range(NT):
                        u = k % 2
                        if k + 1 < NT:
                            best(k + 1)
                        if k:
                            inverse(k - 1)
                        if k >= 3:
                            stats_of(k - 3)
                        dve.wait_ge(n_("top"), k + 1)
                        dve.match_replace(rep[u], top[u], sc[k % 3], LOW).then_inc(n_("rep"), 1)
                        dve.wait_ge(n_("rep"), k + 1)
                        dve.wait_ge(n_("ex"), k + 1)
                        dve.scalar_tensor_tensor(out=wt[u], in0=rep[u], scalar=LOW, in1=ex[u], op0=ALU.is_equal,
                                                 op1=ALU.mult, accum_out=den[u]).then_inc(n_("wt"), 1)
                        if k >= 2:
                            gated(k - 2)
                    inverse(NT - 1)
                    for k in range(NT - 2, NT):
                        gated(k)
                    for k in range(NT - 3, NT):
                        stats_of(k)

                @block.gpsimd
                def _(pool):
                    pool.memset(front_w, 0.0).then_inc(n_("front_clear"), 1)
                    pool.memset(rk[0:MASK + 1], 0.0).then_inc(n_("cleared"), 1)
                    pool.memset(rq[0:MASK + 1], 0.0).then_inc(n_("cleared"), 1)
                    pool.wait_ge(n_("cleared"), 2)
                    pool.memset(rq[MASK:MASK + 1], 1.0).then_inc(n_("cleared"), 1)
                    pool.wait_ge(n_("cleared"), 3)
                    for g in range(NG):
                        pool.wait_ge(n_("hs"), g + 1)
                        s_ = slice(g * G, (g + 1) * G)
                        pool.tensor_tensor(X[:, s_], X[:, s_], hs[:, s_], ALU.add).then_inc(n_("xh"), 1)
                    pool.wait_ge(n_("gate"), 1)

                    def coefficient(k):
                        pool.wait_ge(n_("rden"), k + 1)
                        pool.tensor_tensor(coef[k % 2], gate[:, k:k + 1], rden[k % 2], ALU.mult)\
                            .then_inc(n_("coef"), 1)

                    for k in range(NT):
                        u = k % 2
                        pool.wait_ge(n_("top"), k + 1)
                        pool.tensor_scalar(ntop[u], top[u][:, 0:1], -1.0, None, ALU.mult).then_inc(n_("ntop"), 1)
                        if k:
                            coefficient(k - 1)
                    coefficient(NT - 1)

                @block.scalar
                def _(act):
                    norm_stats_act(act, "m")
                    act.wait_ge(n_("var"), 1)
                    act.activation(lv, var, ACT.Ln, bias=1.0).then_inc(n_("lv"), 1)
                    act.wait_ge(n_("cleared"), 3)
                    act.activation(rk[MASK:MASK + 1], row("mask")[MASK:MASK + 1], ACT.Copy)
                    act.wait_ge(n_("rkp"), 1)
                    act.activation(rk[0:RD], PS[0:RD, 7, :], ACT.Copy).then_inc(n_("rk"), 1)

                    act.wait_ge(n_("front_clear"), 1)
                    act.activation(front_w[:, UP:UP + UNC], w("unc1"), ACT.Copy)
                    act.activation(front_w[:, 0:RD], PS[:, 6, 0:RD], ACT.Copy).then_inc(n_("front_w"), 1)

                    def transposed(g):
                        act.wait_ge(n_("hsT"), g + 1)
                        act.activation(hT[g % 2], front(g, 0), ACT.Copy).then_inc(n_("hT"), 1)

                    transposed(0)
                    for g in range(NG):
                        if g + 1 < NG:
                            transposed(g + 1)
                        act.wait_ge(n_("fronts"), g + 1)
                        act.activation(rq[0:RD, g * G:(g + 1) * G], front(g, 1)[0:RD], ACT.Copy,
                                       scale=float(1.0 / np.sqrt(RD))).then_inc(n_("rq"), 1)
                        act.activation(h1[g % 2][UP:UP + UNC], front(g, 1)[UP:UP + UNC], ACT.Gelu,
                                       bias=col("uncb1")[UP:UP + UNC]).then_inc(n_("h1"), 1)
                    act.wait_ge(n_("lrn"), NG)
                    act.activation(sig, lrn, ACT.Sigmoid).then_inc(n_("sig"), 1)
                    act.wait_ge(n_("unc"), 1)
                    act.activation(gate, unc, ACT.Sigmoid, bias=row("gbias"), scale=row("gw1"))\
                        .then_inc(n_("gate"), 1)

                    def scores_out(k):
                        act.wait_ge(n_("scores"), k + 1)
                        wait(act, "rep", k - 2)
                        act.activation(sc[k % 3], score(k), ACT.Copy).then_inc(n_("sc"), 1)

                    def weights_out(k):
                        act.wait_ge(n_("wTp"), k + 1)
                        act.activation(wT[k % 2], turned(k), ACT.Copy).then_inc(n_("wT"), 1)

                    scores_out(0)
                    scores_out(1)
                    for k in range(NT):
                        act.wait_ge(n_("ntop"), k + 1)
                        wait(act, "wt", k - 1)
                        act.activation(ex[k % 2], sc[k % 3], ACT.Exp, bias=ntop[k % 2]).then_inc(n_("ex"), 1)
                        if k:
                            weights_out(k - 1)
                        if k + 2 < NT:
                            scores_out(k + 2)
                    weights_out(NT - 1)

                @block.tensor
                def _(pe):
                    pe.wait_ge(sem("w2_loaded"), 16)
                    pe.matmul(PS[:, 6, 0:RD], w("qproj"), w("router"), start=True, stop=True)
                    pe.matmul(PS[0:RD, 7, :], w("router"), w("keys"), start=True, stop=True)\
                        .then_inc(n_("rkp"), 1)

                    def transposes(g):
                        pe.wait_ge(n_("hs"), g + 1)
                        for t in range(GT):
                            k = g * GT + t
                            last = pe.transpose(front(g, 0)[:, t * P:(t + 1) * P], hs[:, k * D:(k + 1) * D],
                                                ident[:, :])
                        last.then_inc(n_("hsT"), 1)

                    def learned(g):
                        if g >= 2:
                            pe.wait_ge(n_("lrn"), g - 1)
                        pe.wait_ge(n_("h1"), g + 1)
                        for t in range(GT):
                            last = pe.matmul(front(g, 2)[:, t:t + 1], h1[g % 2][UP:UP + UNC, t * P:(t + 1) * P],
                                             w("unc2")[UP:UP + UNC], start=True, stop=True)
                        last.then_inc(n_("learned"), 1)

                    transposes(0)
                    transposes(1)
                    pe.wait_ge(n_("front_w"), 1)
                    for g in range(NG):
                        pe.wait_ge(n_("hT"), g + 1)
                        if g >= 2:
                            pe.wait_ge(n_("h1"), g - 1)
                        pe.matmul(front(g, 1)[0:UP + UNC], front_w[:, 0:UP + UNC], hT[g % 2], start=True, stop=True)\
                            .then_inc(n_("fronts"), 1)
                        if g + 2 < NG:
                            transposes(g + 2)
                        if g:
                            learned(g - 1)
                    learned(NG - 1)
                    pe.wait_ge(n_("lsum"), 1)
                    pe.matmul(PS[:, 6, 0:1], ONES[:, :], lsum, start=True, stop=True).then_inc(n_("lall"), 1)

                    def scores(k):
                        pe.wait_ge(n_("rq"), NG)
                        wait(pe, "sc", k - 1)
                        pe.matmul(score(k), rq[0:MASK + 1, k * P:(k + 1) * P], rk[0:MASK + 1],
                                  start=True, stop=True).then_inc(n_("scores"), 1)

                    def read_memory(k):
                        pe.wait_ge(n_("wT"), k + 1)
                        wait(pe, "x", k)
                        for c in range(HC):
                            last = pe.matmul(read(k), wT[k % 2][:, c * P:(c + 1) * P], w("values", c * D, D),
                                             start=(c == 0), stop=(c == HC - 1))
                        last.then_inc(n_("agg"), 1)

                    pe.wait_ge(n_("lrn"), NG)
                    pe.wait_ge(n_("rk"), 1)
                    scores(0)
                    scores(1)
                    pe.wait_ge(n_("chain"), 2)
                    scores(2)
                    for k in range(NT):
                        if k + 3 < NT:
                            scores(k + 3)
                        pe.wait_ge(n_("wt"), k + 1)
                        for c in range(HC):
                            last = pe.transpose(turned(k)[:, c * P:(c + 1) * P], wt[k % 2][:, c * P:(c + 1) * P],
                                                ident[:, :])
                        last.then_inc(n_("wTp"), 1)
                        if k:
                            read_memory(k - 1)
                    read_memory(NT - 1)

        def causal_attention(stats):
            at[0] = 0
            EH = DH + 1
            FW = H * EH * DH
            HB = [(0, 6), (6, 5), (11, 5)]
            hn = [cut(G) for _ in range(2)]
            hT = [cut(G) for _ in range(2)]
            hb = cut(NT * D)
            qk = cut(NT * 2 * D).rearrange("p (t c) -> p t c", t=NT)
            va = cut(NT * H * EH).rearrange("p (t h e) -> p t h e", t=NT, h=H)
            outer = [cut(FW) for _ in range(4)]
            prod = [cut(FW) for _ in range(2)]
            nd = [cut(H * EH).rearrange("p (h e) -> p h e", h=H) for _ in range(2)]
            rec = [cut(H) for _ in range(2)]
            att = [cut(D) for _ in range(3)]
            aT = [cut(D) for _ in range(2)]
            n_ = lambda s: sem("a1_" + s)
            qkv = lambda k: PS[:, 2 + k % 6, 0:3 * D]
            sums = lambda k, c: PS[:, 3 * (k % 2) + c, :]

            def heads(ap, h0, n):
                return ap[:, h0 * DH:(h0 + n) * DH].rearrange("p (h m) -> p h m", m=DH)

            def wait(e, s, value):
                if value > 0:
                    e.wait_ge(n_(s), value)

            with nc.Block() as block:
                @block.vector
                def _(dve):
                    norm_stats_dve(dve, "a1", stats, 1e-5, 1e-6)
                    normed(dve, 0, X, hn[0], RS2, n_("hn"))
                    normed(dve, 1, X, hn[1], RS2, n_("hn"))
                    dve.memset(va[:, :, :, DH:EH], 1.0).then_inc(n_("ones"), 1)
                    for g in range(NG):
                        for k in range(g * GT, (g + 1) * GT):
                            dve.wait_ge(n_("qkv"), k + 1)
                            dve.tensor_scalar(qk[:, k, :], qkv(k)[:, 0:2 * D], 0.0, 1e-3, ALU.max, ALU.add)\
                                .then_inc(n_("phi"), 1)
                        if g + 2 < NG:
                            normed(dve, g + 2, X, hn[g % 2], RS2, n_("hn"))
                    def residual(k):
                        dve.wait_ge(n_("proj"), k + 1)
                        dve.wait_ge(n_("hb"), k // GT + 1)
                        dve.tensor_tensor(XX[:, k * D:(k + 1) * D], PS[:, 7, 0:D], hb[:, k * D:(k + 1) * D],
                                          ALU.add).then_inc(n_("xx"), 1)

                    def stats_of(k):
                        dve.wait_ge(n_("xx"), k + 1)
                        dve.bn_stats(ST[:, 6 * k:6 * k + 6], XX[:, k * D:(k + 1) * D]).then_inc(n_("stats"), 1)

                    for k in range(NT):
                        u = k % 2
                        dve.wait_ge(n_("cum"), k + 1)
                        for c, (h0, n) in enumerate(HB):
                            last = dve.tensor_tensor(
                                prod[u][:, h0 * EH * DH:(h0 + n) * EH * DH]
                                .rearrange("p (h e m) -> p h e m", e=EH, m=DH),
                                sums(k, c)[:, 0:n * EH * DH].rearrange("p (h e m) -> p h e m", e=EH, m=DH),
                                over(heads(qk[:, k, 0:D], h0, n), EH, 2), ALU.mult)
                        last.then_inc(n_("prod"), 1)
                        if k >= 3:
                            residual(k - 3)
                        dve.wait_ge(n_("prod"), k + 1)
                        dve.tensor_reduce(nd[u].rearrange("p h e -> p (h e)"),
                                          prod[u].rearrange("p (c m) -> p c m", m=DH), AX_X, ALU.add)\
                            .then_inc(n_("nd"), 1)
                        if k >= 3:
                            stats_of(k - 3)
                        dve.wait_ge(n_("nd"), k + 1)
                        dve.reciprocal(rec[u], nd[u][:, :, DH]).then_inc(n_("rec"), 1)
                        dve.wait_ge(n_("rec"), k + 1)
                        dve.tensor_tensor(att[k % 3].rearrange("p (h e) -> p h e", e=DH), nd[u][:, :, 0:DH],
                                          over(rec[u], DH, 2), ALU.mult).then_inc(n_("att"), 1)
                    for k in range(NT - 3, NT):
                        residual(k)
                        stats_of(k)

                @block.gpsimd
                def _(pool):
                    pool.wait_ge(n_("rs"), 1)
                    for g in range(NG):
                        normed(pool, g, X, hb[:, g * G:(g + 1) * G], RS, n_("hb"))
                    pool.wait_ge(n_("ones"), 1)
                    for k in range(NT):
                        pool.wait_ge(n_("phi"), k + 1)
                        pool.wait_ge(n_("values"), k + 1)
                        wait(pool, "cum", k - 2 - k % 2)
                        pool.tensor_tensor(
                            outer[k % 4].rearrange("p (h e m) -> p h e m", e=EH, m=DH),
                            over(heads(qk[:, k, D:2 * D], 0, H), EH, 2),
                            over(va[:, k], DH, 3), ALU.mult).then_inc(n_("outer"), 1)

                @block.scalar
                def _(act):
                    norm_stats_act(act, "a1", 1e-6)

                    def transposed(g):
                        act.wait_ge(n_("hnT"), g + 1)
                        wait(act, "qkv", (g - 1) * GT)
                        act.activation(hT[g % 2], PS[:, g % 2, :], ACT.Identity, bias=col("b1_1"),
                                       scale=col("g1_1")).then_inc(n_("hT"), 1)

                    transposed(0)
                    transposed(1)
                    for g in range(NG):
                        for k in range(g * GT, (g + 1) * GT):
                            act.wait_ge(n_("qkv"), k + 1)
                            act.wait_ge(n_("phi"), k + 1)
                            act.activation(va[:, k, :, 0:DH], qkv(k)[:, 2 * D:3 * D]
                                           .rearrange("p (h e) -> p h e", h=H), ACT.Copy).then_inc(n_("values"), 1)
                        if g + 2 < NG:
                            transposed(g + 2)
                    for k in range(NT):
                        act.wait_ge(n_("attT"), k + 1)
                        act.activation(aT[k % 2], PS[:, 6, 0:P], ACT.Copy).then_inc(n_("aT"), 1)

                @block.tensor
                def _(pe):
                    def transposes(g):
                        pe.wait_ge(n_("hn"), g + 1)
                        for t in range(GT):
                            last = pe.transpose(PS[:, g % 2, t * P:(t + 1) * P], hn[g % 2][:, t * D:(t + 1) * D],
                                                ident[:, :])
                        last.then_inc(n_("hnT"), 1)

                    pe.wait_ge(sem("w3_loaded"), 16)
                    transposes(0)
                    transposes(1)
                    for g in range(NG):
                        pe.wait_ge(n_("hT"), g + 1)
                        for t in range(GT):
                            k = g * GT + t
                            wait(pe, "values", k - 5)
                            pe.matmul(qkv(k), hT[g % 2][:, t * P:(t + 1) * P], w("qkv1"), start=True, stop=True)\
                                .then_inc(n_("qkv"), 1)
                        if g + 2 < NG:
                            transposes(g + 2)

                    def transposed_result(k):
                        pe.wait_ge(n_("att"), k + 1)
                        wait(pe, "aT", k)
                        pe.transpose(PS[:, 6, 0:P], att[k % 3], ident[:, :]).then_inc(n_("attT"), 1)

                    def projection(k):
                        pe.wait_ge(n_("aT"), k + 1)
                        wait(pe, "xx", k)
                        pe.matmul(PS[:, 7, 0:D], aT[k % 2], w("wo1"), start=True, stop=True).then_inc(n_("proj"), 1)

                    pe.wait_ge(n_("values"), NT)
                    for k in range(NT):
                        pe.wait_ge(n_("outer"), k + 1)
                        wait(pe, "prod", k - 1)
                        for c, (h0, n) in enumerate(HB):
                            a, b = h0 * EH * DH, (h0 + n) * EH * DH
                            if k % 2:
                                pe.matmul(sums(k, c)[:, 0:b - a], ONES[:, :], outer[(k - 1) % 4][:, a:b], start=True,
                                          stop=False)
                            last = pe.matmul(sums(k, c)[:, 0:b - a], TRI[:, :], outer[k % 4][:, a:b],
                                             start=(k % 2 == 0), stop=True)
                        last.then_inc(n_("cum"), 1)
                        if k >= 3:
                            projection(k - 3)
                        if k >= 2:
                            transposed_result(k - 2)
                    for k in range(NT - 3, NT):
                        projection(k)
                        if k + 1 < NT:
                            transposed_result(k + 1)

        def experts(stats):
            at[0] = 0
            HT = cut(T)
            cwT = [cut(T, BF16) for _ in range(2)]
            SEL = cut(EP // 2 * P, BF16)
            hn = [cut(G) for _ in range(NG)]
            aff = [cut(GT * E) for _ in range(2)]
            rep = [cut(GT * E) for _ in range(2)]
            sg = [cut(GT * E) for _ in range(NG)]
            cw = [cut(GT * E) for _ in range(2)]
            rm = [cut(GT * E) for _ in range(2)]
            chosen = [cut(GT * E) for _ in range(2)]
            top = [cut(GT * 8) for _ in range(2)]
            wsum = [cut(GT) for _ in range(2)]
            rsum = [cut(GT) for _ in range(2)]
            EH = E // 2
            cp = [cut(GT * 2 * 3 * EH, BF16).rearrange("p (t f c) -> p t f c", t=GT, f=2) for _ in range(2)]
            part = lambda u, a: cp[u][:, :, :, a * EH:(a + 1) * EH]
            halves = lambda m: m.rearrange("p (t f j) -> p t f j", t=GT, f=2)
            n_ = lambda s: sem("e_" + s)
            bankb = lambda u, k: bank(u, k).bitcast(BF16)

            aff_ = lambda g: bank(g % 2, 1 if g < 2 else 0)[:, 0:GT * E]

            with nc.Block() as block:
                @block.vector
                def _(dve):
                    norm_stats_dve(dve, "e", stats, 1e-5)
                    for g in range(NG):
                        normed(dve, g, X, hn[g], RS, n_("hn"))
                    for g in range(NG):
                        u = g % 2
                        dve.wait_ge(n_("sg"), g + 1)
                        dve.tensor_tensor(tiles(aff[u]), tiles(aff_(g)), over(row("eb"), GT),
                                          ALU.add).then_inc(n_("biased"), 1)
                        dve.wait_ge(n_("biased"), g + 1)
                        for t in range(GT):
                            last = dve.max(top[u][:, 8 * t:8 * t + 8], aff[u][:, t * E:(t + 1) * E])
                        last.then_inc(n_("top"), 1)
                        dve.wait_ge(n_("top"), g + 1)
                        for t in range(GT):
                            last = dve.match_replace(rep[u][:, t * E:(t + 1) * E], top[u][:, 8 * t:8 * t + 8],
                                                     aff[u][:, t * E:(t + 1) * E], LOW)
                        last.then_inc(n_("rep"), 1)
                        dve.wait_ge(n_("rep"), g + 1)
                        for t in range(GT):
                            s_ = slice(t * E, (t + 1) * E)
                            last = dve.scalar_tensor_tensor(out=chosen[u][:, s_], in0=rep[u][:, s_], scalar=LOW,
                                                            in1=sg[g][:, s_], op0=ALU.is_equal, op1=ALU.mult,
                                                            accum_out=wsum[u][:, t:t + 1])
                        last.then_inc(n_("wsum"), 1)
                        dve.wait_ge(n_("wsum"), g + 1)
                        dve.tensor_scalar(wsum[u], wsum[u], 1e-8, None, ALU.add).then_inc(n_("wse"), 1)
                        dve.wait_ge(n_("wse"), g + 1)
                        dve.reciprocal(rsum[u], wsum[u]).then_inc(n_("rsum"), 1)
                        dve.wait_ge(n_("rsum"), g + 1)
                        if g >= 2:
                            dve.wait_ge(n_("c3"), g - 1)
                        dve.tensor_tensor(tiles(cw[u]), tiles(chosen[u]), over(rsum[u], E, 2), ALU.mult)\
                            .then_inc(n_("cw"), 1)
                        dve.wait_ge(n_("cw"), g + 1)
                        if g >= 2:
                            dve.wait_ge(n_("cwTp"), g - 1)
                        dve.tensor_copy(part(u, 0), halves(cw[u])).then_inc(n_("c1"), 1)
                        dve.wait_ge(n_("c1"), g + 1)
                        dve.tensor_tensor(halves(rm[u]), halves(cw[u]), part(u, 0), ALU.subtract)\
                            .then_inc(n_("r1"), 1)

                @block.gpsimd
                def _(pool):
                    pool.memset(SEL, 0.0).then_inc(n_("sel"), 1)
                    for a in range(3):
                        pool.wait_ge(n_("sel"), a + 1)
                        s_ = SEL.rearrange("p (k f m) -> p k f m", f=2, m=F)
                        pool.affine_select(out=s_, in_=s_, compare_op=ALU.not_equal, fill=1.0, base=-EH * a,
                                           pattern=[[-2, EP // 2], [-1, 2], [0, F]], channel_multiplier=1)\
                            .then_inc(n_("sel"), 1)
                    for g in range(NG):
                        u = g % 2
                        pool.wait_ge(n_("r1"), g + 1)
                        pool.tensor_copy(part(u, 1), halves(rm[u])).then_inc(n_("c2"), 1)
                        pool.wait_ge(n_("c2"), g + 1)
                        pool.tensor_tensor(part(u, 2), halves(rm[u]), part(u, 1), ALU.subtract)\
                            .then_inc(n_("c3"), 1)

                @block.scalar
                def _(act):
                    norm_stats_act(act, "e")
                    for g in range(NG):
                        act.wait_ge(n_("hnT"), g + 1)
                        act.activation(HT[:, g * G:(g + 1) * G], bank(g % 2, 0), ACT.Copy).then_inc(n_("hT"), 1)
                    for g in range(NG):
                        act.wait_ge(n_("affp"), g + 1)
                        act.activation(sg[g], aff_(g), ACT.Sigmoid).then_inc(n_("sg"), 1)
                    for g in range(NG):
                        act.wait_ge(n_("cwTp"), g + 1)
                        for a in range(2):
                            last = act.activation(cwT[a][0:3 * EH, g * G:(g + 1) * G],
                                                  bankb(g % 2, 2 + a)[0:3 * EH, 0:G], ACT.Copy)
                        last.then_inc(n_("cwT"), 1)

                @block.tensor
                def _(pe):
                    def affinities(g):
                        pe.wait_ge(n_("hT"), g + 1)
                        for t in range(GT):
                            k = g * GT + t
                            last = pe.matmul(aff_(g)[:, t * E:(t + 1) * E], HT[:, k * P:(k + 1) * P],
                                             w("cent"), start=True, stop=True)
                        last.then_inc(n_("affp"), 1)

                    for g in range(NG):
                        pe.wait_ge(n_("hn"), g + 1)
                        if g >= 2:
                            pe.wait_ge(n_("hT"), g - 1)
                        for t in range(GT):
                            last = pe.transpose(bank(g % 2, 0)[:, t * P:(t + 1) * P], hn[g][:, t * D:(t + 1) * D],
                                                ident[:, :])
                        last.then_inc(n_("hnT"), 1)
                    for g in range(NG):
                        affinities(g)
                    for g in range(NG):
                        u = g % 2
                        pe.wait_ge(n_("c3"), g + 1)
                        if g >= 2:
                            pe.wait_ge(n_("cwT"), g - 1)
                        for a in range(2):
                            for t in range(GT):
                                last = pe.transpose(bankb(u, 2 + a)[0:3 * EH, t * P:(t + 1) * P],
                                                    cp[u][:, t, a, :], identb[:, :])
                        last.then_inc(n_("cwTp"), 1)

            at[0] = T + T + EP // 2 * P // 2
            WU = [cut(P) for _ in range(2)]
            WD = [cut(P) for _ in range(2)]
            si = [cut(G) for _ in range(2)]
            hw = [cut(G) for _ in range(2)]
            res = cut(T)
            m_ = lambda s: sem("g_" + s)
            acc = lambda c: PS[:, c, :]

            def chunk(ap, c):
                return ap[:, c * G:(c + 1) * G]

            def count(k, c, add=1):
                return GT * k + c + 4 + add

            with nc.Block() as block:
                @block.sync
                def _(sp):
                    def load(k, par):
                        s = bass.ds(k * P, P)
                        sp.dma_start(WU[par], wup[:, s]).then_inc(m_(f"w{par}"), 16)
                        sp.dma_start(WD[par], wdown[:, s]).then_inc(m_(f"w{par}"), 16)

                    load(0, 0)
                    load(1, 1)
                    with sp.Fori(0, EP // 2 - 1) as i:
                        for par in range(2):
                            sp.wait_ge(m_("down"), count(2 * i + par, 3))
                            load(2 * i + 2 + par, par)
                    for c in range(NG):
                        sp.wait_ge(m_("res"), c + 1)
                        sp.dma_start(out[:, c * G:(c + 1) * G], chunk(res, c)).then_inc(sem("out_stored"), 16)
                    sp.wait_ge(sem("out_stored"), 16 * NG)

                @block.scalar
                def _(act):
                    def silu(cnt, c, rows_=P):
                        act.wait_ge(m_("up"), cnt)
                        act.activation(si[c % 2][0:rows_], PS[0:rows_, 4 + c % 2, :], ACT.Silu)\
                            .then_inc(m_("si"), 1)

                    for c in range(NG):
                        if c >= 2:
                            act.wait_ge(m_("hw"), c - 1)
                        silu(c + 1, c, F)
                    with act.Fori(0, EP) as k:
                        for c in range(NG):
                            act.wait_ge(m_("hw"), count(k, c, -1))
                            silu(count(k, c), c)
                    for c in range(NG):
                        act.wait_ge(m_("down"), count(EP - 1, c))
                        act.activation(chunk(res, c), acc(c), ACT.Copy).then_inc(m_("res"), 1)

                @block.vector
                def _(dve):
                    for c in range(NG):
                        dve.wait_ge(m_("si"), c + 1)
                        if c >= 2:
                            dve.wait_ge(m_("down"), c - 1)
                        dve.tensor_copy(hw[c % 2][0:F], si[c % 2][0:F]).then_inc(m_("hw"), 1)
                    with dve.Fori(0, EP) as k:
                        for c in range(NG):
                            dve.wait_ge(m_("si"), count(k, c))
                            dve.wait_ge(m_("cwb"), GT * k + c + 1)
                            dve.wait_ge(m_("down"), count(k, c, -1))
                            dve.tensor_tensor(hw[c % 2], PS[:, 6 + c % 2, :], si[c % 2], ALU.mult)\
                                .then_inc(m_("hw"), 1)

                @block.tensor
                def _(pe):
                    for t in range(NT):
                        pe.matmul(acc(t // GT)[:, (t % GT) * P:(t % GT + 1) * P], X[:, t * D:(t + 1) * D],
                                  ident[:, :], start=(t % GT == 0), stop=True, skip_group_check=True)

                    def down(cnt, c, lhs, rows_=P):
                        pe.wait_ge(m_("hw"), cnt)
                        pe.matmul(acc(c), lhs, hw[c % 2][0:rows_], start=False, stop=True, skip_group_check=True)\
                            .then_inc(m_("down"), 1)

                    for c in range(NG):
                        if c >= 2:
                            pe.wait_ge(m_("si"), c - 1)
                        pe.matmul(PS[0:F, 4 + c % 2, :], w("sup"), chunk(HT, c), start=True, stop=True)\
                            .then_inc(m_("up"), 1)
                        if c:
                            down(c, c - 1, w("sdown")[0:F], F)

                    def pair(k, half, par, before):
                        pe.wait_ge(m_(f"w{par}"), 32 * ((k - par) // 2 + 1) if isinstance(k, int)
                                   else 16 * (k + (2 - par)))
                        for c in range(NG):
                            pe.wait_ge(m_("si"), count(k, c, -1))
                            pe.matmul(PS[:, 4 + c % 2, :], WU[par], chunk(HT, c), start=True, stop=True)\
                                .then_inc(m_("up"), 1)
                            pe.wait_ge(m_("hw"), count(k, c, -1))
                            pe.matmul(PS[:, 6 + c % 2, :], SEL[0:3 * EH, bass.ds((k - half * (EP // 2)) * P, P)],
                                      chunk(cwT[half], c)[0:3 * EH], start=True, stop=True).then_inc(m_("cwb"), 1)
                            if c:
                                down(count(k, c - 1), c - 1, WD[par])
                            else:
                                down(count(k, 0, 0), NG - 1, *before)

                    pair(0, 0, 0, (w("sdown")[0:F], F))
                    pair(1, 0, 1, (WD[0],))
                    for half in range(2):
                        with pe.Fori(1 - half, EP // 4) as i:
                            for par in range(2):
                                pair(half * (EP // 2) + 2 * i + par, half, par, (WD[1 - par],))
                    down(count(EP, 0, 0), NG - 1, WD[1])

        set_up()
        phase(linear_attention)
        phase(feed_forward, 0, ACT.Gelu, 1e-5, "a0_stats")
        phase(cross_attend, 0, phase(cross_prepare, 0, "f0_stats"))
        phase(memory_read, "y0_stats")
        phase(causal_attention, "m_stats")
        phase(feed_forward, 1, ACT.Gelu_apprx_tanh, 1e-6, "a1_stats")
        phase(cross_attend, 1, phase(cross_prepare, 1, "f1_stats"))
        experts("y1_stats")


def layout(inputs):
    a = {k: np.asarray(v) for k, v in inputs.items()}
    f = np.float32
    hd = np.arange(D).reshape(4, 4, DH).transpose(1, 0, 2).reshape(-1)
    dh = hd.reshape(H, DH).T.reshape(-1)

    def pad(m):
        return m if m.shape[0] == P else np.concatenate([m, np.zeros((P - m.shape[0], m.shape[1]), f)], 0)

    def lower(m):
        out = np.zeros((P, m.shape[1]), f)
        out[64:64 + m.shape[0]] = m
        return out

    def chunks(m):
        return m.reshape(-1, P, m.shape[1]).transpose(1, 0, 2).reshape(P, -1)

    mats = {
        "qkv0": a["L0_attn_qkv_w"].T, "proj0": a["L0_attn_proj_w"].T, "fc1_0": a["L0_attn_fc1_w"].T,
        "fc2_0": chunks(a["L0_attn_fc2_w"].T),
        "xq0": a["L0_xattn_Wq"].T[:, dh], "xk0": a["L0_xattn_Wk"].T[:, dh], "xv0": a["L0_xattn_Wv"].T[:, hd],
        "xo0": a["L0_xattn_Wo"].T[hd],
        "qproj": a["L0_ffn_q_proj_w"], "router": a["L0_ffn_router_w"].T, "keys": a["L0_ffn_aux_keys"].T,
        "values": chunks(a["L0_ffn_aux_values"]), "unc1": a["L0_ffn_unc_w1"].T, "unc2": lower(a["L0_ffn_unc_w2"].T),
        "qkv1": np.concatenate([a[f"L1_attn_w{c}"].reshape(D, D) for c in "qkv"], 1),
        "wo1": a["L1_attn_wo"].reshape(D, D), "fc1_1": a["L1_attn_w1"], "fc2_1": chunks(a["L1_attn_w2"]),
        "xq1": a["L1_xattn_wq"].T[:, dh], "xk1": a["L1_xattn_wk"].T[:, dh], "xv1": a["L1_xattn_wv"].T[:, hd],
        "xo1": a["L1_xattn_wo"].T[hd],
        "cent": a["L1_ffn_centroids"].T, "sup": a["L1_ffn_Ws_up"], "sdown": pad(a["L1_ffn_Ws_down"]),
    }
    vecs = {
        "g1_0": a["L0_attn_norm1_g"], "b1_0": a["L0_attn_norm1_b"], "g2_0": a["L0_attn_norm2_g"],
        "b2_0": a["L0_attn_norm2_b"], "fcb_0": a["L0_attn_fc1_b"], "bq0": a["L0_xattn_bq"][dh],
        "bk0": a["L0_xattn_bk"][dh], "bq1": a["L1_xattn_bq"][dh], "bk1": a["L1_xattn_bk"][dh],
        "uncb1": lower(a["L0_ffn_unc_b1"][:, None]),
        "g1_1": a["L1_attn_ln1_scale"], "b1_1": a["L1_attn_ln1_bias"], "g2_1": a["L1_attn_ln2_scale"],
        "b2_1": a["L1_attn_ln2_bias"], "fcb_1": a["L1_attn_b1"],
    }
    flat = {
        "projb": a["L0_attn_proj_b"], "fc2b_0": a["L0_attn_fc2_b"], "bv0": a["L0_xattn_bv"][hd],
        "bo0": a["L0_xattn_bo"], "fc2b_1": a["L1_attn_b2"], "bv1": a["L1_xattn_bv"][hd], "bo1": a["L1_xattn_bo"],
        "mask": a["L0_ffn_reliability_mask"], "eb": a["L1_ffn_expert_biases"], "uncb2": a["L0_ffn_unc_b2"],
        "gw1": a["L0_ffn_gate_w1"], "gbias": a["L0_ffn_gate_bias"], "decay": a["L1_xattn_time_decay"],
    }
    c = np.ascontiguousarray
    return {
        "x": c(a["x"].reshape(T, D)),
        "ctxT": c(a["ctx_1024"].reshape(T, D).T),
        "wts": c(np.concatenate([mats[n] for n, _ in _W], 1)),
        "cols": c(np.concatenate([vecs[n].reshape(-1, P).T for n, _ in _C], 1)),
        "rows": c(np.broadcast_to(np.concatenate([flat[n].reshape(-1) for n, _ in _R])[None], (P, NR))),
        "positions": position_rows(),
        "wup": c(a["L1_ffn_W_up"].transpose(1, 0, 2).reshape(D, E * F)),
        "wdown": c(a["L1_ffn_W_down"].reshape(EP, P, D).transpose(1, 0, 2).reshape(P, EP * D)),
    }


def position_rows():
    q = np.arange(S)
    late, early = (q >= P).astype(np.float32), (q < P).astype(np.float32)
    zero = np.zeros(S, np.float32)
    rows = []
    for queries, keys, sign in ((late, early, 1), (early, late, -1)):
        rows += [(sign * q * queries, zero, zero, keys, part) for part in range(3)]
        rows += [(zero, queries, -sign * q * keys, zero, part) for part in range(3)]
    return np.stack([np.concatenate([*r[:4], np.eye(3)[r[4]]]) for r in rows]).astype(np.float32)


def program(nc, arrays):
    args = [nc.dram_tensor(f"in_{n}", a.shape, mybir.dt.from_np(a.dtype), kind="ExternalInput").ap()
            for n, a in arrays.items()]
    scratch = [nc.dram_tensor(f"parts{n}", (B, 2, 3, P, S), BF16, kind="Internal").ap() for n in range(2)]
    out = nc.dram_tensor("out_x", (D, T), F32, kind="ExternalOutput").ap()
    nc.disable_value_cache = True
    build(nc, *args, scratch, out)


def kernel(**inputs):
    import concourse.bacc as bacc
    from concourse.bass_utils import run_bass_kernel_spmd as run
    arrays = layout(inputs)
    nc = bacc.Bacc("TRN2", target_bir_lowering=False, num_devices=1)
    program(nc, arrays)
    r = run(nc, [{f"in_{n}": a for n, a in arrays.items()}], core_ids=[0])
    return np.ascontiguousarray(r.results[0]["out_x"].T).reshape(B, S, D)
```
